# Optimizing a Trainium2 kernel written in Bass

```python
import numpy as np
import jax
import jax.numpy as jnp

def _softmax(x, axis=-1):
    return jax.nn.softmax(x, axis=axis)

def _gelu(x):
    return jax.nn.gelu(x, approximate=True)

def _silu(x):
    return jax.nn.silu(x)

def _sigmoid(x):
    return jax.nn.sigmoid(x)

def _layernorm(x, axis=-1, eps=1e-05):
    m = jnp.mean(x, axis=axis, keepdims=True)
    v = jnp.var(x, axis=axis, keepdims=True)
    return (x - m) / jnp.sqrt(v + eps)

def _scatter_add(tgt, idx, src, axis=0):
    return tgt.at[idx].add(src)

def _segment_sum(src, seg, n):
    return jax.ops.segment_sum(src, seg, n)
kernel_name = 'mk_cond_seq_d1_seqx_r2_440f1b'

def setup_inputs(seed: int=0):
    np.random.seed(seed)
    _w = jnp.asarray

    def _rec_inputs():
        import jax
        import jax.numpy as jnp
        _rk = jax.random.key(seed)
        x = 1.648e-05 + 1 * jax.random.normal(jax.random.fold_in(_rk, 1), (8, 512, 576), jnp.float32)
        _lenS = 512 - jax.random.randint(jax.random.fold_in(_rk, 7), (8,), 0, max(1, 512 // 4) + 1, jnp.int32)
        _lenS2 = 512 - jax.random.randint(jax.random.fold_in(_rk, 8), (8,), 0, max(1, 512 // 4) + 1, jnp.int32)
        cond_1152 = 0.00914911 + 1.00357 * jax.random.normal(jax.random.fold_in(_rk, 11), (8, 576), jnp.float32)
        return (x, cond_1152)
    x, cond_1152 = _rec_inputs()

    def _L0_cond_setup():
        import math
        import jax, jax.numpy as jnp
        import numpy as np
        B, T, D = (8, 512, 576)
        H = 16
        E = 4
        EPS = 1e-06

        def _layer_norm(x):
            mu = jnp.mean(x, axis=-1, keepdims=True)
            var = jnp.mean(jnp.square(x - mu), axis=-1, keepdims=True)
            return (x - mu) * jax.lax.rsqrt(var + EPS)

        def _modulate(x, shift, scale):
            return x * (1.0 + scale) + shift

        def _attention(y, qkv_w, qkv_b, out_w, out_b):
            b, t, d = y.shape
            hd = d // H
            qkv = y @ qkv_w + qkv_b
            q, k, v = jnp.split(qkv, 3, axis=-1)
            q = q.reshape(b, t, H, hd).transpose(0, 2, 1, 3)
            k = k.reshape(b, t, H, hd).transpose(0, 2, 1, 3)
            v = v.reshape(b, t, H, hd).transpose(0, 2, 1, 3)
            scores = jnp.einsum('bhqd,bhkd->bhqk', q, k) / math.sqrt(hd)
            attn = jax.nn.softmax(scores, axis=-1)
            out = jnp.einsum('bhqk,bhkd->bhqd', attn, v)
            out = out.transpose(0, 2, 1, 3).reshape(b, t, d)
            return out @ out_w + out_b
        key = jax.random.key(seed)
        ks = jax.random.split(key, 12)
        std = 0.02
        return {'x': jax.random.normal(ks[0], (B, T, D), dtype=jnp.float32), 'c': jax.random.normal(ks[1], (B, D), dtype=jnp.float32), 'qkv_w': jax.random.normal(ks[2], (D, 3 * D), dtype=jnp.float32) * std, 'qkv_b': jnp.zeros((3 * D,), dtype=jnp.float32), 'out_w': jax.random.normal(ks[3], (D, D), dtype=jnp.float32) * std, 'out_b': jnp.zeros((D,), dtype=jnp.float32), 'w1': jax.random.normal(ks[4], (D, E * D), dtype=jnp.float32) * std, 'b1': jnp.zeros((E * D,), dtype=jnp.float32), 'w2': jax.random.normal(ks[5], (E * D, D), dtype=jnp.float32) * std, 'b2': jnp.zeros((D,), dtype=jnp.float32), 'ada_w': jax.random.normal(ks[6], (D, 6 * D), dtype=jnp.float32) * std, 'ada_b': jnp.zeros((6 * D,), dtype=jnp.float32)}
    _L0_cond_all = _L0_cond_setup()
    _L0_cond_in = {k: v for k, v in _L0_cond_all.items() if k in ('qkv_w', 'qkv_b', 'out_w', 'out_b', 'w1', 'b1', 'w2', 'b2', 'ada_w', 'ada_b')}
    del _L0_cond_all
    return {'x': x, 'cond_1152': cond_1152, 'L0_cond_qkv_w': _L0_cond_in['qkv_w'], 'L0_cond_qkv_b': _L0_cond_in['qkv_b'], 'L0_cond_out_w': _L0_cond_in['out_w'], 'L0_cond_out_b': _L0_cond_in['out_b'], 'L0_cond_w1': _L0_cond_in['w1'], 'L0_cond_b1': _L0_cond_in['b1'], 'L0_cond_w2': _L0_cond_in['w2'], 'L0_cond_b2': _L0_cond_in['b2'], 'L0_cond_ada_w': _L0_cond_in['ada_w'], 'L0_cond_ada_b': _L0_cond_in['ada_b']}

def reference(x, cond_1152, L0_cond_qkv_w, L0_cond_qkv_b, L0_cond_out_w, L0_cond_out_b, L0_cond_w1, L0_cond_b1, L0_cond_w2, L0_cond_b2, L0_cond_ada_w, L0_cond_ada_b):
    import jax
    import jax.numpy as jnp

    def _L0_cond_ref(x, c, qkv_w, qkv_b, out_w, out_b, w1, b1, w2, b2, ada_w, ada_b):
        import math
        import jax, jax.numpy as jnp
        import numpy as np
        B, T, D = (8, 512, 576)
        H = 16
        E = 4
        EPS = 1e-06

        def _layer_norm(x):
            mu = jnp.mean(x, axis=-1, keepdims=True)
            var = jnp.mean(jnp.square(x - mu), axis=-1, keepdims=True)
            return (x - mu) * jax.lax.rsqrt(var + EPS)

        def _modulate(x, shift, scale):
            return x * (1.0 + scale) + shift

        def _attention(y, qkv_w, qkv_b, out_w, out_b):
            b, t, d = y.shape
            hd = d // H
            qkv = y @ qkv_w + qkv_b
            q, k, v = jnp.split(qkv, 3, axis=-1)
            q = q.reshape(b, t, H, hd).transpose(0, 2, 1, 3)
            k = k.reshape(b, t, H, hd).transpose(0, 2, 1, 3)
            v = v.reshape(b, t, H, hd).transpose(0, 2, 1, 3)
            scores = jnp.einsum('bhqd,bhkd->bhqk', q, k) / math.sqrt(hd)
            attn = jax.nn.softmax(scores, axis=-1)
            out = jnp.einsum('bhqk,bhkd->bhqd', attn, v)
            out = out.transpose(0, 2, 1, 3).reshape(b, t, d)
            return out @ out_w + out_b
        mods = (jax.nn.silu(c) @ ada_w + ada_b)[:, None, :]
        m0, m1, m2, m3, m4, m5 = jnp.split(mods, 6, axis=-1)
        y = _modulate(_layer_norm(x), m0, m1)
        x = x + m2 * _attention(y, qkv_w, qkv_b, out_w, out_b)
        y = _modulate(_layer_norm(x), m3, m4)
        y = jax.nn.gelu(y @ w1 + b1, approximate=True)
        x = x + m5 * (y @ w2 + b2)
        return x
    x = _L0_cond_ref(x, cond_1152, L0_cond_qkv_w, L0_cond_qkv_b, L0_cond_out_w, L0_cond_out_b, L0_cond_w1, L0_cond_b1, L0_cond_w2, L0_cond_b2, L0_cond_ada_w, L0_cond_ada_b)
    return x

_drawn_inputs = setup_inputs


def setup_inputs(seed=0):
    import zlib

    import numpy as np

    out = dict(_drawn_inputs(seed))
    spreads = {'L0_cond_qkv_b': (0.0, 0.574),
     'L0_cond_out_b': (0.0, 0.1),
     'L0_cond_b1': (0.0, 0.452),
     'L0_cond_b2': (0.0, 0.286),
     'L0_cond_ada_b': (0.0, 0.1)}
    factors = {}
    for name, (base, spread) in spreads.items():
        noise = np.random.default_rng([zlib.crc32(name.encode()), seed]).standard_normal(out[name].shape)
        drawn = base * np.exp(spread * noise) if base else spread * noise
        out[name] = jnp.asarray(drawn.astype(out[name].dtype))
    for name, factor in factors.items():
        out[name] = (out[name] * factor).astype(out[name].dtype)
    return out
```

```python
import concourse.bass as bass
from concourse import mybir

F32 = mybir.dt.float32
F32R = mybir.dt.float32r
ACT = mybir.ActivationFunctionType
ALU = mybir.AluOpType
AX_X = mybir.AxisListType.X

B, T, D = 8, 512, 576
H, HD = 16, 36
E = 4 * D
P = 128
EPS = 1e-6
NT = T // P
NK = 5
TAIL = D - 4 * P
DP = NK * P
NQ = 4
HQ = H // NQ
NC = 2 * D // P
QW = HQ * HD
UN = 2 * H
VW = 2 * HD + 1
HALF = D // 2
NJ = E // P
YA = 256
YB = D - YA
SCALE = float(HD) ** -0.5
RAW = E
CHUNKS = {0: (0, 1, 2), 1: (3, 4), 2: (5, 6), 3: (7, 8)}


def v_count(uses, half, t):
    if uses.jobs is PROLOGUE:
        return t
    return uses.b * 2 * NT + NT + (1 - half) * NT + t


class Layout:

    def __init__(self, nc, base):
        self.nc, self.at = nc, base

    def tile(self, name, shape, dtype=F32):
        n = 4
        for s in shape[1:]:
            n *= s
        t = self.nc.alloc_sbuf_tensor_at(name, shape, dtype, offset=self.at)
        self.at += (n + 31) // 32 * 32
        return t


def f32(ap):
    return ap.bitcast(F32)


def unit_jobs(has_next):
    jobs = {}
    for unit in range(UN):
        q, u = divmod(unit, 8)
        slot = {0: 0, 3: 1, 6: 2, 7: 3}.get(u)
        here = []
        if slot is not None:
            if q in (0, 1):
                work = [[("P", 5 + 2 * q)], [("P", 6 + 2 * q)]]
                if q == 0:
                    work += [[("V", 1, 0), ("V", 1, 1)], [("V", 1, 2), ("V", 1, 3)]]
                else:
                    work += [[("T", 0), ("T", 1), ("T", 2)], [("T", 3), ("T", 4)]] if has_next else [[], []]
            elif not has_next:
                work = [[], [], [], []]
            elif q == 2:
                work = [[("P", 0)], [("P", 1)], [("P", 2)], []]
            else:
                work = [[("P", 3)], [("P", 4)], [("V", 0, 0), ("V", 0, 1)], [("V", 0, 2), ("V", 0, 3)]]
            here += work[slot]
        if u == 6 and (q < 3 or has_next):
            here.append(("M", (q + 1) % NQ))
        if unit % 2 and unit >= 3:
            here.append(("O", (unit - 3) // 2))
        jobs[unit] = here
    flush = [("O", H - 1)]
    for t in range(NT + 1):
        if t < NT:
            flush += [("XA", t), ("XB", t)]
        if t > 0:
            flush += [("Y", t - 1, 0), ("Y", t - 1, 1)]
    jobs["flush"] = flush
    return jobs


def in_order(jobs):
    return [j for k in list(range(UN)) + ["flush"] for j in jobs[k]]


PROLOGUE = ([("T", k) for k in range(NK)] + [("P", c) for c in range(5)]
            + [("V", 0, t) for t in range(NT)] + [("M", 0)])
JOBS = {True: unit_jobs(True), False: unit_jobs(False)}
N_BODY = len(in_order(JOBS[True]))
assert N_BODY % 2 == 0


class Uses:

    def __init__(self, first, jobs, b=0):
        self.first, self.jobs, self.b = first, jobs, b
        self.parity = 0 if jobs is PROLOGUE else len(PROLOGUE) % 2

    def bank(self, job):
        return (self.parity + self.jobs.index(job)) % 2

    def full(self, job):
        return self.first + self.jobs.index(job) + 1

    def before(self, job):
        n = self.jobs.index(job)
        return self.jobs[n - 2] if n >= 2 else None


def body_uses(b, has_next):
    return Uses(b * N_BODY + len(PROLOGUE), in_order(JOBS[has_next]), b)


def conditioned_block(nc, x, cond_t, wqk, bqk, wv, bv, wo, bo, w1, b1, w2, b2, ada_w, ada_b, out):
    base = (nc.sbuf_base + 63) // 64 * 64
    lay = Layout(nc, base)
    sem = nc.alloc_semaphore

    mods = nc.dram_tensor("mods", [6, B, D], F32, kind="Internal").ap()
    qk_scr = nc.dram_tensor("qk_scr", [B, 2, 2 * D, T], F32, kind="Internal").ap()
    x1 = nc.dram_tensor("x1", [B, T, D], F32, kind="Internal").ap()

    ident = lay.tile("ident", [P, P])
    stats = lay.tile("stats", [P, NT, 2, 6])
    moments = lay.tile("moments", [P, NT, 2])
    rstd = lay.tile("rstd", [P, NT])
    eps_half = lay.tile("eps_half", [P, 2, NT])
    modt = lay.tile("modt", [P, 2, NK])
    phase_base = lay.at
    nident = lay.tile("nident", [P, P])
    merge = lay.tile("merge", [VW, HD + 1])
    bqk_sb = lay.tile("bqk_sb", [P, NC])
    rowmax = lay.tile("rowmax", [P, NT, H])
    rden = lay.tile("rden", [P, 4, NT, 1])
    negmax = lay.tile("negmax", [HQ, 2, T], F32R)
    wqk_hi = lay.tile("wqk_hi", [P, NK, 2 * D], F32R)
    wqk_lo = lay.tile("wqk_lo", [P, NK - 1, 2 * D], F32R)
    wv_hi = lay.tile("wv_hi", [P, NK, D], F32R)
    wv_lo = lay.tile("wv_lo", [P, NK - 1, D], F32R)
    wo_hi = lay.tile("wo_hi", [P, NK, D], F32R)
    wo_lo = lay.tile("wo_lo", [P, NK - 1, D], F32R)
    y_hi = lay.tile("y_hi", [P, NK, T], F32R)
    y_lo = lay.tile("y_lo", [P, NK, T], F32R)
    y_tmp = lay.tile("y_tmp", [P, T])
    dense = lay.tile("dense", [P, 3, 2, T], F32R)
    v_tmp = lay.tile("v_tmp", [P, HALF])
    xt = lay.tile("xt", [P, NT, DP])
    attn = lay.tile("attn", [P, NT, DP])
    resid_tmp = lay.tile("resid_tmp", [P, D])
    bv_sb = lay.tile("bv_sb", [P, D])
    bo_sb = lay.tile("bo_sb", [P, D])
    m2_sb = lay.tile("m2_sb", [P, D])
    pv_sb = lay.tile("pv_sb", [VW, 2, T])
    shared = lay.at
    qs = [lay.tile(f"qs{i}", [3 * HD + 2, HQ, T], F32R) for i in range(2)]
    ks = [lay.tile(f"ks{i}", [3 * HD + 2, HQ, T], F32R) for i in range(2)]
    v_sb = lay.tile("v_sb", [P, NT, H, VW], F32R)
    e_at = lay.at
    e_lo = lay.tile("e_lo", [P, 2, 2 * T], F32R)
    e_hi = lay.tile("e_hi", [P, 2, 2 * T], F32R)
    a_end = lay.at
    lay.at = e_at
    e_f = lay.tile("e_f", [P, 2, 2 * T])
    lay.at = e_at
    at_hi = lay.tile("at_hi", [P, 2, NK, P], F32R)
    at_lo = lay.tile("at_lo", [P, 2, NK, P], F32R)
    lay.at = shared
    raw = [lay.tile(f"raw{i}", [P, NK, D]) for i in range(4)]
    cond_sb = lay.tile("cond_sb", [P, NK, B])
    cond_e = lay.tile("cond_e", [P, NK, B])
    cond_s = lay.tile("cond_s", [P, NK, B])
    mod_row = lay.tile("mod_row", [B, 2, D])
    adab_sb = lay.tile("adab_sb", [B, 6, D])
    assert lay.at <= a_end <= nc.sbuf_usable_end, (lay.at, a_end)
    lay.at = phase_base
    w1_hi = lay.tile("w1_hi", [P, NK, E], F32R)
    w1_lo = lay.tile("w1_lo", [P, NK - 1, E], F32R)
    w2_hi = lay.tile("w2_hi", [P, NJ, D], F32R)
    w2_lo = lay.tile("w2_lo", [P, NJ, D], F32R)
    b1_sb = lay.tile("b1_sb", [P, NJ])
    m5_sb = lay.tile("m5_sb", [P, D])
    b2_sb = lay.tile("b2_sb", [P, D])
    z_tmp = lay.tile("z_tmp", [P, T])
    raw_at = lay.at
    z_hi = lay.tile("z_hi", [P, NK, T], F32R)
    z_lo = lay.tile("z_lo", [P, NK, T], F32R)
    g_f = lay.tile("g_f", [P, 2, T])
    h_hi = lay.tile("h_hi", [P, 2, T], F32R)
    h_lo = lay.tile("h_lo", [P, 2, T], F32R)
    xn = lay.tile("xn", [P, NT, DP])
    xr = lay.tile("xr", [P, 2, D])
    y_out = lay.tile("y_out", [P, D])
    b_end = lay.at
    lay.at = raw_at
    raw2 = [lay.tile(f"raw2_{i}", [P, RAW]) for i in range(3)]
    assert lay.at <= b_end <= nc.sbuf_usable_end, b_end

    mm = [nc.alloc_psum_tensor(f"mm{i}", [P, 512], F32) for i in range(2)]
    pv = [nc.alloc_psum_tensor(f"pv{i}", [P, 512], F32) for i in range(2)]
    sct = nc.alloc_psum_tensor("sct", [P, 2, 512], F32)
    scs = nc.alloc_psum_tensor("scs", [P, 2, 512], F32)
    y_pair = pv
    y_own = [sct[:, 0, :], sct[:, 1, :], scs[:, 0, :], scs[:, 1, :]]

    s_const = sem("s_const")
    s_small = sem("s_small")
    s_ada = [sem(f"s_ada{i}") for i in range(2)]
    s_raw = sem("s_raw")
    s_rawk = [sem(f"s_rawk{i}") for i in range(4)]
    s_cond = sem("s_cond")
    s_mod_full = sem("s_mod_full")
    s_mod_row = sem("s_mod_row")
    s_mod_out = [sem(f"s_mod_out{i}") for i in range(2)]
    s_w_hi = sem("s_w_hi")
    s_w_lo = sem("s_w_lo")
    mm_full = sem("mm_full")
    xn_in = sem("xn_in")
    xr_in = sem("xr_in")
    modt_in = sem("modt_in")
    m2_in = sem("m2_in")
    chain = sem("chain")
    scaled = sem("scaled")
    var_done = sem("var_done")
    rstd_done = sem("rstd_done")
    xhat_done = sem("xhat_done")
    ytmp_done = sem("ytmp_done")
    yhi_done = sem("yhi_done")
    y_done = sem("y_done")
    p_hi = sem("p_hi")
    p_done = sem("p_done")
    dense_out = [sem(f"dense_out{i}") for i in range(3)]
    vtmp_done = sem("vtmp_done")
    vhi_done = sem("vhi_done")
    v_done = sem("v_done")
    stack_in = [sem(f"stack_in{i}") for i in range(2)]
    scs_full = sem("scs_full")
    scs_free = sem("scs_free")
    neg_hi = sem("neg_hi")
    neg_done = sem("neg_done")
    rows_in = [sem(f"rows_in{i}") for i in range(2)]
    sct_full = sem("sct_full")
    sct_free = sem("sct_free")
    ehi_done = sem("ehi_done")
    elo_done = sem("elo_done")
    pv_done = sem("pv_done")
    pv_out = sem("pv_out")
    rden_done = sem("rden_done")
    o_done = sem("o_done")
    at_hi_done = sem("at_hi_done")
    at_done = sem("at_done")
    yb_done = sem("yb_done")
    r_mul = sem("r_mul")
    r_add = sem("r_add")
    x1_out = sem("x1_out")
    sp_steps = sem("sp_steps")
    a_over = sem("a_over")

    sems_b = {n: sem("b_" + n) for n in (
        "small w_hi w_lo mm_full xn_in xr_in0 xr_in1 modt_in m5_in chain var_done rstd_done"
        " scaled xhat_done ztmp_done zhi_done z_done g_done hhi_done h_done m2_done yo_done o_mul"
        " o_add out0 out1").split()}

    def gather_mod(eng, section, b, done):
        src = mods[section:section + 2, b, :]
        for n in range(2):
            eng.dma_start(modt[:, n, 0:4], src[n, 0:4 * P].rearrange("(k p) -> p k", p=P)).then_inc(done, 16)
        tail = src[:, 4 * P:D].rearrange("s (p o) -> p s o", o=1)
        eng.dma_start(modt[0:TAIL, :, 4:5], tail).then_inc(done, 16)
        eng.dma_start(modt[TAIL:P, :, 4:5], tail).then_inc(done, 16)

    def load_rows(eng, dst, src, done):
        eng.dma_start(dst[:, 0:4, :], src[0:4 * P, :].rearrange("(k p) n -> p k n", p=P)).then_inc(done, 16)
        eng.dma_start(dst[0:TAIL, 4, :], src[4 * P:D, :]).then_inc(done, 16)
        eng.dma_start(dst[TAIL:P, 4, :], src[4 * P:D, :]).then_inc(done, 16)

    slow = nc.allow_non_contiguous_dma(reason="a feature to a partition, 5 KB a batch")
    slow.__enter__()
    block = nc.Block()
    block.__enter__()

    @block.sync
    def _(sp):
        def write_chunk(b, c):
            sp.wait_ge(p_done, b * NC + c + 1)
            sp.dma_start(qk_scr[b, :, c * P:(c + 1) * P, :].rearrange("h p t -> p h t"),
                         f32(dense[:, c % 3, :, :])).then_inc(dense_out[c % 3], 16)

        def load_stack(b, q, units=None):
            for c in CHUNKS[q] if q == 0 else (CHUNKS[q][0] - 1,) + CHUNKS[q]:
                sp.wait_ge(dense_out[c % 3], b * 48 + 16 * (c // 3 + 2))
                sp.sem_inc(sp_steps, 1)
            if units is not None:
                sp.wait_ge(sct_full, units)
            par = q % 2
            for dst, first, parts in ((qs[par], 0, (0, 1, 0)), (ks[par], QW, (0, 0, 1))):
                at = 2 * QW * q + first
                for n, part in enumerate(parts):
                    sp.dma_start(f32(dst[n * HD:(n + 1) * HD, :, :]),
                                 qk_scr[b, part, at:at + QW, :].rearrange("(i r) t -> r i t", r=HD)
                                 ).then_inc(stack_in[par], 16)

        def load_neg(count, q):
            sp.wait_ge(neg_done, count)
            for n in range(2):
                sp.dma_start(f32(qs[q % 2][3 * HD + n:3 * HD + n + 1, :, :]), f32(negmax[:, n, :])
                             ).then_inc(rows_in[q % 2], 16)

        def load_x(b, dst_cols, done):
            for t in range(NT):
                sp.dma_start(xt[:, t, 0:D], x[b, t * P:(t + 1) * P, :]).then_inc(done, 16)

        for s in dense_out:
            sp.sem_inc(s, 16)
        sp.sem_inc(x1_out, 16)
        load_rows(sp, cond_sb, cond_t, s_small)
        for s in range(6):
            sp.dma_start(adab_sb[:, s, :], ada_b[s * D:(s + 1) * D].partition_broadcast(B)).then_inc(s_small, 16)
        sp.dma_start(bqk_sb[:, :], bqk).then_inc(s_small, 16)
        sp.dma_start(bv_sb[:, :], bv.partition_broadcast(P)).then_inc(s_small, 16)
        sp.dma_start(bo_sb[:, :], bo.partition_broadcast(P)).then_inc(s_small, 16)
        load_rows(sp, raw[0], ada_w[:, 0:D], s_ada[0])
        load_rows(sp, raw[1], ada_w[:, D:2 * D], s_ada[1])
        load_x(0, None, xn_in)
        for i in range(2):
            load_rows(sp, raw[2 + i], wqk[:, i * D:(i + 1) * D], s_rawk[i])
        for s in range(6):
            sp.wait_ge(s_mod_row, 2 * s + 2)
            sp.dma_start(mods[s], mod_row[:, s % 2, :]).then_inc(s_mod_out[s % 2], 16)
            if s + 2 < 6:
                load_rows(sp, raw[s % 2], ada_w[:, (s + 2) * D:(s + 3) * D], s_ada[s % 2])
            if s == 1:
                for i in range(2):
                    sp.wait_ge(s_mod_out[i], 16)
                gather_mod(sp, 0, 0, modt_in)
        for i, w in enumerate((wv, wo)):
            sp.wait_ge(s_w_hi, i + 1)
            sp.wait_ge(s_w_lo, 2 * i + 2)
            load_rows(sp, raw[2 + i], w, s_rawk[2 + i])
        for i in range(2):
            sp.wait_ge(s_mod_out[i], 48)
        sp.dma_start(m2_sb[:, :], mods[2, 0].partition_broadcast(P)).then_inc(m2_in, 16)
        for c in range(5):
            write_chunk(0, c)
        sp.wait_ge(s_w_hi, 4)
        sp.wait_ge(s_w_lo, 8)
        sp.wait_ge(s_const, 11)
        load_stack(0, 0)
        load_neg(1, 0)

        def body(b, has_next):
            for q in range(NQ):
                nb, nq = (b, q + 1) if q < 3 else (b + 1, 0)
                if q < 3 or has_next:
                    load_stack(nb, nq, b * UN + 8 * q + 1)
                if q == 0 and has_next:
                    sp.wait_ge(x1_out, b * 64 + 16)
                    load_x(b + 1, None, xn_in)
                    sp.wait_ge(y_done, b * NK + NK)
                    gather_mod(sp, 0, b + 1, modt_in)
                if q == 2:
                    if has_next:
                        sp.wait_ge(mm_full, body_uses(b, has_next).full(("T", NK - 1)))
                    else:
                        sp.wait_ge(x1_out, b * 64 + 16)
                    load_x(b, None, xr_in)
                    if has_next is not None:
                        sp.wait_ge(x1_out, b * 64 + 16)
                        sp.dma_start(m2_sb[:, :], mods[2, b].partition_broadcast(P)).then_inc(m2_in, 16)
                if q < 2:
                    write_chunk(b, 5 + 2 * q)
                    write_chunk(b, 6 + 2 * q)
                elif has_next:
                    for c in CHUNKS[0] if q == 2 else CHUNKS[1]:
                        write_chunk(b + 1, c)
                if q < 3 or has_next:
                    load_neg(b * NQ + q + 2, nq)
            for t in range(NT):
                sp.wait_ge(r_add, b * NT + t + 2)
                sp.dma_start(x1[b, t * P:(t + 1) * P, :], xt[:, t, 0:D]).then_inc(x1_out, 16)

        with sp.Fori(0, B - 1) as b:
            body(b, True)
        body(B - 1, False)
        sp.wait_ge(x1_out, 64 * B + 16)

        s = sems_b
        sp.wait_ge(a_over, 4)
        sp.dma_start(b1_sb[:, :], b1).then_inc(s["small"], 16)
        sp.dma_start(b2_sb[:, :], b2.partition_broadcast(P)).then_inc(s["small"], 16)
        for n in range(10):
            if n >= 3:
                sp.wait_ge(s["w_hi"], n - 2)
                sp.wait_ge(s["w_lo"], n - 2)
            slot, done = raw2[n % 3], s_rawk[n % 3]
            if n < 4:
                sp.dma_start(slot[:, :], w1[n * P:(n + 1) * P, :]).then_inc(done, 16)
            elif n == 4:
                sp.dma_start(slot[0:TAIL, :], w1[4 * P:D, :]).then_inc(done, 16)
                sp.dma_start(slot[TAIL:P, :], w1[4 * P:D, :]).then_inc(done, 16)
            else:
                j = 4 * (n - 5)
                m = min(4, NJ - j)
                sp.dma_start(slot[:, 0:m * D].rearrange("p (j n) -> p j n", n=D),
                             w2[j * P:(j + m) * P, :].rearrange("(j p) n -> p j n", p=P)).then_inc(done, 16)
        sp.wait_ge(s["w_hi"], 10)
        sp.wait_ge(s["w_lo"], 10)

        def load_x1(b):
            for t in range(NT):
                sp.dma_start(xn[:, t, 0:D], x1[b, t * P:(t + 1) * P, :]).then_inc(s["xn_in"], 16)
            gather_mod(sp, 3, b, s["modt_in"])

        load_x1(0)

        def body_b(b, has_next):
            if has_next:
                sp.wait_ge(s["z_done"], b * NK + NK)
                load_x1(b + 1)
            for t in range(NT):
                if t == 0:
                    sp.wait_ge(s["out0"], b * 32 + 16)
                    sp.wait_ge(s["out1"], b * 32 + 16)
                    sp.dma_start(m5_sb[:, :], mods[5, b].partition_broadcast(P)).then_inc(s["m5_in"], 16)
                if t >= 2:
                    sp.wait_ge(s[f"out{t % 2}"], b * 32 + 16 * (t // 2) + 16)
                sp.dma_start(xr[:, t % 2, :], x1[b, t * P:(t + 1) * P, :]).then_inc(s[f"xr_in{t % 2}"], 16)
                if t >= 1:
                    store(b, t - 1)
            store(b, NT - 1)

        def store(b, t):
            sp.wait_ge(s["o_add"], b * NT + t + 2)
            sp.dma_start(out[b, t * P:(t + 1) * P, :], xr[:, t % 2, :]).then_inc(s[f"out{t % 2}"], 16)

        sp.sem_inc(s["out0"], 16)
        sp.sem_inc(s["out1"], 16)
        with sp.Fori(0, B - 1) as b:
            body_b(b, True)
        body_b(B - 1, False)
        sp.wait_ge(s["out0"], 32 * B + 16)
        sp.wait_ge(s["out1"], 32 * B + 16)

    @block.gpsimd
    def _(pool):
        def inverse_deviation(count, var_sem, done):
            pool.wait_ge(var_sem, NT * count)
            pool.tensor_tensor(rstd[:, :], moments[:, :, 1], eps_half[:, 0, :], ALU.add).then_inc(done, 1)
            pool.wait_ge(done, 2 * count - 1)
            pool.tensor_tensor(rstd[:, :], rstd[:, :], eps_half[:, 1, :], ALU.pow).then_inc(done, 1)

        for n, (m, v) in enumerate(((ident[:, :], 0.0), (nident[:, :], 0.0), (merge[:, :], 0.0),
                                    (eps_half[:, 0, :], EPS), (eps_half[:, 1, :], -0.5))):
            if n:
                pool.wait_ge(s_const, n)
            pool.memset(m, v).then_inc(s_const, 1)
        for n, (m, fill) in enumerate(((ident, 1.0), (nident, -1.0))):
            pool.wait_ge(s_const, 5 + n)
            pool.affine_select(out=m[:, :], in_=m[:, :], compare_op=ALU.not_equal, fill=fill,
                               base=0, pattern=[[-1, P]], channel_multiplier=1).then_inc(s_const, 1)
        pool.wait_ge(s_const, 7)
        pool.affine_select(out=merge[:, 0:HD], in_=merge[:, 0:HD], compare_op=ALU.not_equal, fill=1.0,
                           base=0, pattern=[[-1, HD]], channel_multiplier=1).then_inc(s_const, 1)
        pool.wait_ge(s_const, 8)
        pool.affine_select(out=merge[:, :], in_=merge[:, :], compare_op=ALU.not_equal, fill=1.0,
                           base=-HD, pattern=[[-1, HD + 1]], channel_multiplier=1).then_inc(s_const, 1)
        inverse_deviation(1, var_done, rstd_done)
        pool.wait_ge(s_w_hi, 4)
        pool.wait_ge(s_w_lo, 8)
        pool.wait_ge(s_mod_row, 12)
        for i in range(2):
            pool.wait_ge(s_mod_out[i], 48)
        for i in range(2):
            pool.wait_ge(s_const, 9 + i)
            pool.memset(f32(ks[i][96:3 * HD + 2, :, :]), 1.0).then_inc(s_const, 1)
        pool.wait_ge(s_const, 11)
        pool.memset(f32(v_sb[:, :, :, VW - 1:VW]), 1.0).then_inc(s_const, 1)

        pool.sem_inc(r_add, 1)

        def body(b, has_next):
            if has_next:
                inverse_deviation(b + 2, var_done, rstd_done)
            for t in range(NT):
                if t == 0:
                    pool.wait_ge(m2_in, b * 16 + 32)
                    pool.wait_ge(xr_in, b * 64 + 64)
                pool.wait_ge(yb_done, b * 2 * NT + 2 * t + 3)
                pool.tensor_tensor(resid_tmp[:, :], resid_tmp[:, :], m2_sb[:, :], ALU.mult).then_inc(r_mul, 1)
                pool.wait_ge(r_mul, b * NT + t + 1)
                pool.tensor_tensor(xt[:, t, 0:D], xt[:, t, 0:D], resid_tmp[:, :], ALU.add).then_inc(r_add, 1)

        with pool.Fori(0, B - 1) as b:
            body(b, True)
        body(B - 1, False)
        pool.wait_ge(r_add, NT * B + 1)
        pool.sem_inc(a_over, 1)

        s = sems_b
        pool.sem_inc(s["o_add"], 1)
        inverse_deviation(1, s["var_done"], s["rstd_done"])

        def body_b(b, has_next):
            if has_next:
                inverse_deviation(b + 2, s["var_done"], s["rstd_done"])
            for t in range(NT):
                if t == 0:
                    pool.wait_ge(s["m5_in"], b * 16 + 16)
                pool.wait_ge(s["yo_done"], b * 2 * NT + 2 * t + 3)
                pool.tensor_tensor(y_out[:, :], y_out[:, :], m5_sb[:, :], ALU.mult).then_inc(s["o_mul"], 1)
                pool.wait_ge(s["o_mul"], b * NT + t + 1)
                pool.wait_ge(s[f"xr_in{t % 2}"], b * 32 + 16 * (t // 2) + 16)
                pool.tensor_tensor(xr[:, t % 2, :], xr[:, t % 2, :], y_out[:, :], ALU.add).then_inc(s["o_add"], 1)

        with pool.Fori(0, B - 1) as b:
            body_b(b, True)
        body_b(B - 1, False)

    @block.scalar
    def _(act):
        def chunk_hi(b, c, uses):
            act.wait_ge(mm_full, uses.full(("P", c)))
            act.wait_ge(dense_out[c % 3], b * 48 + 16 * (c // 3) + 16)
            act.activation(dense[:, c % 3, 0, :], mm[uses.bank(("P", c))][:, :], ACT.Identity,
                           bias=bqk_sb[:, c:c + 1]).then_inc(p_hi, 1)

        def v_high(n, half, t):
            act.wait_ge(vtmp_done, n)
            hd = H // 2
            act.activation(v_sb[:, t, half * hd:(half + 1) * hd, 0:HD],
                           v_tmp[:, :].rearrange("p (h d) -> p h d", d=HD), ACT.Copy).then_inc(vhi_done, 1)

        def modulate(b, k, uses):
            act.wait_ge(mm_full, uses.full(("T", k)))
            if k == 0:
                act.wait_ge(modt_in, b * 64 + 64)
            else:
                act.wait_ge(y_done, b * NK + k)
            act.activation(y_tmp[:, :], mm[uses.bank(("T", k))][:, :], ACT.Identity,
                           bias=modt[:, 0, k:k + 1], scale=modt[:, 1, k:k + 1]).then_inc(ytmp_done, 1)
            act.wait_ge(ytmp_done, b * NK + k + 1)
            act.activation(y_hi[:, k, :], y_tmp[:, :], ACT.Copy).then_inc(yhi_done, 1)

        act.wait_ge(s_small, 48 + 96 + 48)
        act.activation(cond_e[:, :, :], cond_sb[:, :, :], ACT.Exp, scale=-1.0).then_inc(s_cond, 1)
        for n, (dst, col) in enumerate(((wqk_hi, 0), (wqk_hi, D), (wv_hi, 0), (wo_hi, 0))):
            act.wait_ge(s_rawk[n], 48)
            act.activation(dst[:, :, col:col + D], raw[2 + n % 2][:, :, :], ACT.Copy).then_inc(s_w_hi, 1)
        pro = Uses(0, PROLOGUE)
        for k in range(NK):
            modulate(0, k, pro)
        for c in range(5):
            chunk_hi(0, c, pro)
        for t in range(NT):
            v_high(t + 1, 0, t)
        act.wait_ge(mm_full, pro.full(("M", 0)))
        act.activation(negmax[:, 0, :], mm[pro.bank(("M", 0))][0:HQ, :], ACT.Copy).then_inc(neg_hi, 1)
        act.sem_inc(sct_free, 1)
        act.sem_inc(pv_out, 2)

        def head_out(b, h, uses):
            act.wait_ge(pv_done, b * UN + 2 * h + 4)
            if h >= 2:
                act.wait_ge(mm_full, uses.full(("O", h - 2)))
            act.activation(pv_sb[:, h % 2, :], pv[h % 2][0:VW, :], ACT.Copy).then_inc(pv_out, 1)

        def body(b, has_next):
            uses = body_uses(b, has_next)
            for unit in range(UN):
                n = b * UN + unit
                act.wait_ge(sct_full, n + 2)
                act.wait_ge(pv_done, n + 1)
                act.activation(e_f[:, unit % 2, :].rearrange("p (k t) -> p k t", k=2), sct[:, :, :],
                               ACT.Exp, scale=SCALE).then_inc(sct_free, 1)
                act.wait_ge(sct_free, n + 2)
                act.activation(e_hi[:, unit % 2, :], e_f[:, unit % 2, :], ACT.Copy).then_inc(ehi_done, 1)
                for job in JOBS[has_next][unit]:
                    if job[0] == "P":
                        chunk_hi(b if job[1] >= 5 else b + 1, job[1], uses)
                    elif job[0] == "V":
                        v_high(v_count(uses, job[1], job[2]) + 1, job[1], job[2])
                    elif job[0] == "T":
                        modulate(b + 1, job[1], uses)
                    elif job[0] == "M":
                        q = job[1]
                        act.wait_ge(mm_full, uses.full(job))
                        before = (q - 1) % NQ
                        act.wait_ge(rows_in[before % 2], b * 64 + 32 * (before // 2) + 32)
                        act.activation(negmax[:, 0, :], mm[uses.bank(job)][0:HQ, :], ACT.Copy).then_inc(neg_hi, 1)
                if unit % 2 == 0 and unit >= 2:
                    head_out(b, unit // 2 - 1, uses)
            head_out(b, H - 1, uses)
            for t in range(NT):
                for part, (lo, hi) in (("XA", (0, 4)), ("XB", (4, 5))):
                    act.wait_ge(mm_full, uses.full((part, t)))
                    if t >= 2:
                        act.wait_ge(mm_full, uses.full(("Y", t - 2, 1)))
                    w = (hi - lo) * P
                    act.activation(at_hi[:, t % 2, lo:hi, :],
                                   mm[uses.bank((part, t))][:, 0:w].rearrange("p (k t) -> p k t", t=P),
                                   ACT.Copy).then_inc(at_hi_done, 1)

        with act.Fori(0, B - 1) as b:
            body(b, True)
        body(B - 1, False)
        act.wait_ge(at_hi_done, 2 * NT * B)
        act.sem_inc(a_over, 1)

        s = sems_b
        for n in range(10):
            act.wait_ge(s_rawk[n % 3], 48 + 16 * (n // 3 + 1) + (16 if n % 3 == 1 and n >= 4 else 0))
            if n < 5:
                dst, src = w1_hi[:, n, :], raw2[n % 3][:, :]
            else:
                j = 4 * (n - 5)
                m = min(4, NJ - j)
                dst, src = w2_hi[:, j:j + m, :], raw2[n % 3][:, 0:m * D].rearrange("p (j n) -> p j n", n=D)
            act.activation(dst, src, ACT.Copy).then_inc(s["w_hi"], 1)

        def body_b(b):
            for k in range(NK):
                act.wait_ge(s["mm_full"], b * (NK + NJ) + k + 1)
                if k == 0:
                    act.wait_ge(s["modt_in"], b * 64 + 64)
                else:
                    act.wait_ge(s["z_done"], b * NK + k)
                act.activation(z_tmp[:, :], mm[k % 2][:, :], ACT.Identity, bias=modt[:, 0, k:k + 1],
                               scale=modt[:, 1, k:k + 1]).then_inc(s["ztmp_done"], 1)
                act.wait_ge(s["ztmp_done"], b * NK + k + 1)
                act.activation(z_hi[:, k, :], z_tmp[:, :], ACT.Copy).then_inc(s["zhi_done"], 1)
            for j in range(NJ):
                act.wait_ge(s["mm_full"], b * (NK + NJ) + NK + j + 1)
                if j >= 2:
                    act.wait_ge(s["m2_done"], b * NJ + j - 1)
                act.activation(g_f[:, j % 2, :], mm[(j + 1) % 2][:, :], ACT.Gelu_apprx_tanh,
                               bias=b1_sb[:, j:j + 1]).then_inc(s["g_done"], 1)
                act.wait_ge(s["g_done"], b * NJ + j + 2)
                act.activation(h_hi[:, j % 2, :], g_f[:, j % 2, :], ACT.Copy).then_inc(s["hhi_done"], 1)

        act.sem_inc(s["g_done"], 1)
        act.wait_ge(s["small"], 32)
        with act.Fori(0, B) as b:
            body_b(b)

    @block.vector
    def _(dve):
        def moments_of(b, tile_in, in_sem, ch, done, t):
            if t == 0:
                dve.wait_ge(in_sem, b * 64 + 64)
            dve.bn_stats(stats[:, t, 0, :], tile_in[:, t, 0:HALF]).then_inc(ch, 1)
            dve.bn_stats(stats[:, t, 1, :], tile_in[:, t, HALF:D]).then_inc(ch, 1)
            dve.wait_ge(ch, b * 3 * NT + 3 * t + 2)
            dve.sem_inc(ch, 1)
            dve.bn_aggr(moments[:, t, :], stats[:, t, :, :]).then_inc(done, 1)

        def normalise(b, tile, rs, sc, done, t):
            if t == 0:
                dve.wait_ge(rs, b * 2 + 2)
            dve.tensor_scalar(tile[:, t, 0:D], tile[:, t, 0:D], moments[:, t, 0:1], rstd[:, t:t + 1],
                              ALU.subtract, ALU.mult).then_inc(sc, 1)
            dve.wait_ge(sc, b * NT + t + 1)
            dve.tensor_copy(tile[:, t, D:DP], tile[:, t, 4 * P:D]).then_inc(done, 1)

        def y_low(b, k, hi_sem, hi_t, lo_t, tmp, done):
            dve.wait_ge(hi_sem, b * NK + k + 1)
            dve.tensor_tensor(lo_t[:, k, :], tmp[:, :], f32(hi_t[:, k, :]), ALU.subtract).then_inc(done, 1)

        def chunk_low(b, c, uses):
            dve.wait_ge(p_hi, b * NC + c + 1)
            bank = uses.bank(("P", c))
            dve.scalar_tensor_tensor(dense[:, c % 3, 1, :], mm[bank][:, :], bqk_sb[:, c:c + 1],
                                     f32(dense[:, c % 3, 0, :]), ALU.add, ALU.subtract).then_inc(p_done, 1)

        def v_low(n, half, t, uses):
            bank = uses.bank(("V", half, t))
            dve.wait_ge(mm_full, uses.full(("V", half, t)))
            if not (isinstance(n, int) and n == 0):
                dve.wait_ge(v_done, n)
            dve.tensor_tensor(v_tmp[:, :], mm[bank][:, 0:HALF], bv_sb[:, half * HALF:(half + 1) * HALF],
                              ALU.add).then_inc(vtmp_done, 1)
            dve.wait_ge(vhi_done, n + 1)
            hd = H // 2
            hs = slice(half * hd, (half + 1) * hd)
            dve.tensor_tensor(v_sb[:, t, hs, HD:2 * HD], v_tmp[:, :].rearrange("p (h d) -> p h d", d=HD),
                              f32(v_sb[:, t, hs, 0:HD]), ALU.subtract).then_inc(v_done, 1)

        def max_of(n, q, i, half):
            dve.wait_ge(scs_full, n + 1)
            dve.tensor_reduce(rowmax[:, 2 * half:2 * half + 2, q * HQ + i:q * HQ + i + 1],
                              scs[:, :, :], AX_X, ALU.max).then_inc(scs_free, 1)

        def neg_low(count, q, uses):
            bank = uses.bank(("M", q))
            dve.wait_ge(neg_hi, count)
            dve.tensor_tensor(negmax[:, 1, :], mm[bank][0:HQ, :], f32(negmax[:, 0, :]), ALU.subtract
                              ).then_inc(neg_done, 1)

        dve.sem_inc(yb_done, 1)
        for t in range(NT):
            moments_of(0, xt, xn_in, chain, var_done, t)
        dve.wait_ge(s_cond, 1)
        dve.tensor_scalar(cond_e[:, :, :], cond_e[:, :, :], 1.0, None, ALU.add).then_inc(s_cond, 1)
        dve.wait_ge(s_cond, 2)
        dve.reciprocal(cond_e[:, :, :], cond_e[:, :, :]).then_inc(s_cond, 1)
        dve.wait_ge(s_cond, 3)
        dve.tensor_tensor(cond_s[:, :, :], cond_sb[:, :, :], cond_e[:, :, :], ALU.mult).then_inc(s_cond, 1)
        for t in range(NT):
            normalise(0, xt, rstd_done, scaled, xhat_done, t)

        def mod_half(s, half):
            n = 2 * s + half
            dve.wait_ge(s_mod_full, n + 1)
            if s >= 2 and half == 0:
                dve.wait_ge(s_mod_out[s % 2], 16 * (s // 2))
            cols = slice(half * HALF, (half + 1) * HALF)
            one = 1.0 if s in (1, 4) else 0.0
            dve.scalar_tensor_tensor(mod_row[:, s % 2, cols], scs[0:B, half, 0:HALF], one,
                                     adab_sb[:, s, cols], ALU.add, ALU.add).then_inc(s_mod_row, 1)

        def weights_low(n):
            dst, hi, col = ((wqk_lo, wqk_hi, 0), (wqk_lo, wqk_hi, D), (wv_lo, wv_hi, 0), (wo_lo, wo_hi, 0))[n]
            r = raw[2 + n % 2]
            dve.wait_ge(s_w_hi, n + 1)
            dve.tensor_tensor(dst[:, :, col:col + D], r[:, 0:4, :], f32(hi[:, 0:4, col:col + D]), ALU.subtract
                              ).then_inc(s_w_lo, 1)
            dve.tensor_tensor(hi[TAIL:P, 4, col:col + D], r[TAIL:P, 4, :], f32(hi[TAIL:P, 4, col:col + D]),
                              ALU.subtract).then_inc(s_w_lo, 1)

        for s in range(2):
            mod_half(s, 0)
            mod_half(s, 1)
        weights_low(0)
        weights_low(1)
        pro = Uses(0, PROLOGUE)
        for s in range(2, 6):
            mod_half(s, 0)
            mod_half(s, 1)
        weights_low(2)
        weights_low(3)
        dve.wait_ge(s_mod_row, 12)
        dve.sem_inc(scs_free, 1)
        for k in range(NK):
            dve.wait_ge(ytmp_done, k + 1)
            y_low(0, k, yhi_done, y_hi, y_lo, y_tmp, y_done)
        for c in range(5):
            chunk_low(0, c, pro)
        for t in range(NT):
            if t == 0:
                dve.wait_ge(s_const, 12)
            v_low(t, 0, t, pro)
        for i in range(HQ):
            for half in range(2):
                max_of(2 * i + half, 0, i, half)
        neg_low(1, 0, pro)

        def norm(b, h, uses):
            bank = uses.bank(("O", h))
            dve.wait_ge(mm_full, uses.full(("O", h)))
            src = mm[bank][:, 0:NT * 64].rearrange("p (t c) -> p t c", c=64)
            dve.reciprocal(rden[:, h % 4, :, :], src[:, :, HD:HD + 1]).then_inc(rden_done, 1)
            dve.wait_ge(rden_done, b * H + h + 1)
            dve.tensor_tensor(attn[:, :, h * HD:(h + 1) * HD], src[:, :, 0:HD],
                              rden[:, h % 4, :, :].to_broadcast([P, NT, HD]), ALU.mult).then_inc(o_done, 1)

        def body(b, has_next):
            uses = body_uses(b, has_next)
            for unit in range(UN):
                q, u = divmod(unit, 8)
                n = b * UN + unit
                has_s = u in (1, 2, 4, 5) and (q < 3 or has_next)
                i = {1: 0, 2: 1, 4: 2, 5: 3}.get(u)
                sn = b * 2 * H + 2 * HQ + (q * HQ + (i or 0)) * 2
                if has_s:
                    max_of(sn, (q + 1) % NQ, i, 0)
                dve.wait_ge(ehi_done, n + 1)
                dve.tensor_tensor(e_lo[:, unit % 2, :], e_f[:, unit % 2, :], f32(e_hi[:, unit % 2, :]),
                                  ALU.subtract).then_inc(elo_done, 1)
                for job in JOBS[has_next][unit]:
                    if job[0] == "P":
                        chunk_low(b if job[1] >= 5 else b + 1, job[1], uses)
                    elif job[0] == "V":
                        v_low(v_count(uses, job[1], job[2]), job[1], job[2], uses)
                    elif job[0] == "T":
                        dve.wait_ge(ytmp_done, b * NK + NK + job[1] + 1)
                        y_low(b + 1, job[1], yhi_done, y_hi, y_lo, y_tmp, y_done)
                    elif job[0] == "M":
                        neg_low(b * NQ + q + 2, job[1], uses)
                    elif job[0] == "O":
                        norm(b, job[1], uses)
                if has_s:
                    max_of(sn + 1, (q + 1) % NQ, i, 1)
                if has_next and q == 0 and u in (2, 3, 6, 7):
                    t = (2, 3, 6, 7).index(u)
                    moments_of(b + 1, xt, xn_in, chain, var_done, t)
                if has_next and q == 1 and u < 4:
                    normalise(b + 1, xt, rstd_done, scaled, xhat_done, u)
            norm(b, H - 1, uses)
            dve.wait_ge(o_done, b * (H + 1) + H)
            dve.tensor_copy(attn[:, :, D:DP], attn[:, :, 4 * P:D]).then_inc(o_done, 1)

            def transposed_low(t):
                for part, (lo, hi), k in (("XA", (0, 4), 0), ("XB", (4, 5), 1)):
                    bank = uses.bank((part, t))
                    w = (hi - lo) * P
                    dve.wait_ge(at_hi_done, b * 2 * NT + 2 * t + k + 1)
                    dve.tensor_tensor(at_lo[:, t % 2, lo:hi, :],
                                      mm[bank][:, 0:w].rearrange("p (k t) -> p k t", t=P),
                                      f32(at_hi[:, t % 2, lo:hi, :]), ALU.subtract).then_inc(at_done, 1)

            def plus_bias(t):
                for half in range(2):
                    bank = uses.bank(("Y", t, half))
                    cols = slice(half * HALF, (half + 1) * HALF)
                    dve.wait_ge(mm_full, uses.full(("Y", t, half)))
                    if half == 0:
                        dve.wait_ge(r_add, b * NT + t + 1)
                    dve.tensor_tensor(resid_tmp[:, cols], mm[bank][:, 0:HALF], bo_sb[:, cols], ALU.add
                                      ).then_inc(yb_done, 1)

            transposed_low(0)
            for t in range(NT):
                if t + 1 < NT:
                    transposed_low(t + 1)
                plus_bias(t)

        with dve.Fori(0, B - 1) as b:
            body(b, True)
        body(B - 1, False)
        dve.wait_ge(yb_done, 2 * NT * B + 1)
        dve.sem_inc(a_over, 1)

        s = sems_b
        dve.sem_inc(s["yo_done"], 1)
        for n in range(10):
            dve.wait_ge(s["w_hi"], n + 1)
            r = raw2[n % 3]
            if n < 4:
                dve.tensor_tensor(w1_lo[:, n, :], r[:, :], f32(w1_hi[:, n, :]), ALU.subtract).then_inc(s["w_lo"], 1)
            elif n == 4:
                dve.tensor_tensor(w1_hi[TAIL:P, 4, :], r[TAIL:P, :], f32(w1_hi[TAIL:P, 4, :]),
                                  ALU.subtract).then_inc(s["w_lo"], 1)
            else:
                j = 4 * (n - 5)
                m = min(4, NJ - j)
                dve.tensor_tensor(w2_lo[:, j:j + m, :], r[:, 0:m * D].rearrange("p (j n) -> p j n", n=D),
                                  f32(w2_hi[:, j:j + m, :]), ALU.subtract).then_inc(s["w_lo"], 1)

        def norm_b(b, first):
            if first:
                for t in range(NT):
                    moments_of(b, xn, s["xn_in"], s["chain"], s["var_done"], t)
            else:
                for t in range(NT):
                    normalise(b, xn, s["rstd_done"], s["scaled"], s["xhat_done"], t)

        norm_b(0, True)
        norm_b(0, False)

        def hidden_low(b, j):
            dve.wait_ge(s["hhi_done"], b * NJ + j + 1)
            dve.tensor_tensor(h_lo[:, j % 2, :], g_f[:, j % 2, :], f32(h_hi[:, j % 2, :]), ALU.subtract
                              ).then_inc(s["h_done"], 1)

        def body_b(b, has_next):
            for k in range(NK):
                dve.wait_ge(s["ztmp_done"], b * NK + k + 1)
                y_low(b, k, s["zhi_done"], z_hi, z_lo, z_tmp, s["z_done"])
            for j in range(NJ):
                hidden_low(b, j)
                if has_next and j == 6:
                    norm_b(b + 1, True)
                if has_next and j == 8:
                    norm_b(b + 1, False)
            dve.wait_ge(s["m2_done"], b * NJ + NJ)
            dve.wait_ge(s["small"], 32)
            for t in range(NT):
                dve.wait_ge(s["o_add"], b * NT + t + 1)
                pair = y_pair[t // 2][:, YA * (t % 2):YA * (t % 2) + YA]
                dve.tensor_tensor(y_out[:, 0:YA], pair, b2_sb[:, 0:YA], ALU.add).then_inc(s["yo_done"], 1)
                dve.tensor_tensor(y_out[:, YA:D], y_own[t][:, 0:YB], b2_sb[:, YA:D], ALU.add
                                  ).then_inc(s["yo_done"], 1)

        with dve.Fori(0, B - 1) as b:
            body_b(b, True)
        body_b(B - 1, False)

    @block.tensor
    def _(pe):
        def bank_free(uses, job):
            b, last = uses.b, uses.before(job)
            if last is None:
                if uses.jobs is not PROLOGUE:
                    pe.wait_ge(yb_done, b * 2 * NT + 1)
                return
            kind, n = last[0], last[1]
            nxt = 0 if uses.jobs is PROLOGUE else 1
            if kind == "T":
                pe.wait_ge(ytmp_done, (b + nxt) * NK + n + 1)
            elif kind == "P":
                pe.wait_ge(p_done, (b + (nxt if n < 5 else 0)) * NC + n + 1)
            elif kind == "V":
                pe.wait_ge(vtmp_done, v_count(uses, n, last[2]) + 1)
            elif kind == "M":
                pe.wait_ge(neg_done, b * NQ + (n - 1) % NQ + 2 if nxt else 1)
            elif kind == "O":
                pe.wait_ge(o_done, b * (H + 1) + n + 1)
            elif kind in ("XA", "XB"):
                pe.wait_ge(at_done, b * 2 * NT + 2 * n + (2 if kind == "XB" else 1))
            else:
                pe.wait_ge(yb_done, b * 2 * NT + 2 * n + last[2] + 2)

        def split_product(acc, w_hi, w_lo, y_h, y_l, done=None):
            n = 0
            for k in range(NK - 1):
                for lhs, rhs in ((w_hi(k), y_h(k)), (w_hi(k), y_l(k)), (w_lo(k), y_h(k))):
                    pe.matmul(acc, lhs, rhs, start=(n == 0), stop=False)
                    n += 1
            pe.matmul(acc, w_hi(4), y_h(4), start=False, stop=False)
            return pe.matmul(acc, w_hi(4), y_l(4), start=False, stop=True)

        def project(b, c, uses):
            job = ("P", c)
            bank = uses.bank(job)
            bank_free(uses, job)
            if c == 0:
                pe.wait_ge(y_done, b * NK + NK)
            cols = slice(c * P, (c + 1) * P)
            split_product(mm[bank][:, :], lambda k: wqk_hi[:, k, cols], lambda k: wqk_lo[:, k, cols],
                          lambda k: y_hi[:, k, :], lambda k: y_lo[:, k, :]).then_inc(mm_full, 1)

        def project_v(half, t, uses):
            job = ("V", half, t)
            bank = uses.bank(job)
            bank_free(uses, job)
            cols = slice(half * HALF, (half + 1) * HALF)
            toks = slice(t * P, (t + 1) * P)
            acc = mm[bank][:, 0:HALF]
            n = 0
            for k in range(NK - 1):
                for lhs, rhs in ((y_hi, wv_hi), (y_hi, wv_lo), (y_lo, wv_hi)):
                    pe.matmul(acc, lhs[:, k, toks], rhs[:, k, cols], start=(n == 0), stop=False)
                    n += 1
            pe.matmul(acc, y_hi[:, 4, toks], wv_hi[:, 4, cols], start=False, stop=False)
            pe.matmul(acc, y_lo[:, 4, toks], wv_hi[:, 4, cols], start=False, stop=True).then_inc(mm_full, 1)

        def transpose_y(k, uses):
            job = ("T", k)
            bank = uses.bank(job)
            bank_free(uses, job)
            for t in range(NT):
                last = pe.transpose(mm[bank][:, t * P:(t + 1) * P], xt[:, t, k * P:(k + 1) * P], ident[:, :])
            last.then_inc(mm_full, 1)

        def scores(n, q, i, half):
            pe.wait_ge(scs_free, n + 1)
            for j in range(2):
                t = 2 * half + j
                last = pe.matmul(scs[:, j, :], qs[q % 2][0:3 * HD, i, t * P:(t + 1) * P],
                                 ks[q % 2][0:3 * HD, i, :], start=True, stop=True)
            last.then_inc(scs_full, 1)

        def maxima(q, uses):
            job = ("M", q)
            bank = uses.bank(job)
            bank_free(uses, job)
            for t in range(NT):
                last = pe.matmul(mm[bank][0:HQ, t * P:(t + 1) * P], rowmax[:, t, q * HQ:(q + 1) * HQ],
                                 nident[:, :], start=True, stop=True)
            last.then_inc(mm_full, 1)

        pe.wait_ge(s_cond, 4)
        for s in range(6):
            pe.wait_ge(s_ada[s % 2], 48 * (s // 2 + 1))
            for half in range(2):
                if s >= 1:
                    pe.wait_ge(s_mod_row, 2 * s - 1 + half)
                for k in range(NK):
                    rows = P if k < NK - 1 else TAIL
                    last = pe.matmul(scs[0:B, half, 0:HALF], cond_s[0:rows, k, :],
                                     raw[s % 2][0:rows, k, half * HALF:(half + 1) * HALF],
                                     start=(k == 0), stop=(k == NK - 1))
                last.then_inc(s_mod_full, 1)
        pro = Uses(0, PROLOGUE)
        pe.wait_ge(s_const, 7)
        pe.wait_ge(xhat_done, NT)
        for k in range(NK):
            transpose_y(k, pro)
        pe.wait_ge(s_w_lo, 4)
        for c in range(5):
            project(0, c, pro)
        pe.wait_ge(s_w_lo, 6)
        for t in range(NT):
            project_v(0, t, pro)
        pe.wait_ge(stack_in[0], 96)
        for i in range(HQ):
            for half in range(2):
                scores(2 * i + half, 0, i, half)
        pe.wait_ge(scs_free, 2 * HQ + 1)
        maxima(0, pro)
        pe.sem_inc(sct_full, 1)
        pe.sem_inc(pv_done, 2)
        pe.wait_ge(s_w_lo, 8)
        pe.wait_ge(s_const, 12)
        pe.wait_ge(vtmp_done, NT)
        pe.wait_ge(neg_done, 1)

        def product(b, unit):
            h, pair = divmod(unit, 2)
            pe.wait_ge(elo_done, b * UN + unit + 1)
            if pair == 0:
                pe.wait_ge(pv_out, b * H + h + 1)
            for kk in range(2):
                for part, e in enumerate((e_hi, e_lo)):
                    last = pe.matmul(pv[h % 2][0:VW, :], v_sb[:, 2 * pair + kk, h, :],
                                     e[:, unit % 2, kk * T:(kk + 1) * T],
                                     start=(pair == 0 and kk == 0 and part == 0),
                                     stop=(pair == 1 and kk == 1 and part == 1))
            last.then_inc(pv_done, 1)

        def merge_head(b, h, uses):
            job = ("O", h)
            bank = uses.bank(job)
            pe.wait_ge(pv_out, b * H + h + 3)
            bank_free(uses, job)
            for t in range(NT):
                last = pe.matmul(mm[bank][:, 64 * t:64 * t + HD + 1], pv_sb[:, h % 2, t * P:(t + 1) * P],
                                 merge[:, :], start=True, stop=True)
            last.then_inc(mm_full, 1)

        def body(b, has_next):
            uses = body_uses(b, has_next)
            for unit in range(UN):
                q, u = divmod(unit, 8)
                h = unit // 2
                par = q % 2
                if u == 0:
                    pe.wait_ge(stack_in[par], b * 192 + 96 * (q // 2) + 96)
                    pe.wait_ge(rows_in[par], b * 64 + 32 * (q // 2) + 32)
                if unit == 0:
                    pe.wait_ge(v_done, b * 2 * NT + NT)
                if unit == UN // 2:
                    pe.wait_ge(v_done, b * 2 * NT + 2 * NT)
                pe.wait_ge(sct_free, b * UN + unit + 1)
                for kk in range(2):
                    kt = 2 * (unit % 2) + kk
                    last = pe.matmul(sct[:, kk, :], ks[par][:, h % HQ, kt * P:(kt + 1) * P],
                                     qs[par][:, h % HQ, :], start=True, stop=True)
                last.then_inc(sct_full, 1)
                has_s = u in (1, 2, 4, 5) and (q < 3 or has_next)
                i = {1: 0, 2: 1, 4: 2, 5: 3}.get(u)
                sn = b * 2 * H + 2 * HQ + (q * HQ + (i or 0)) * 2
                nq = (q + 1) % NQ
                if has_s:
                    if i == 0:
                        nb = b if q < 3 else b + 1
                        pe.wait_ge(stack_in[nq % 2], nb * 192 + 96 * (nq // 2) + 96)
                    scores(sn, nq, i, 0)
                tail = []
                for job in JOBS[has_next][unit]:
                    if job[0] == "P":
                        project(b if job[1] >= 5 else b + 1, job[1], uses)
                    elif job[0] == "V":
                        project_v(job[1], job[2], uses)
                    elif job[0] == "T":
                        if job[1] == 0:
                            pe.wait_ge(xhat_done, b * NT + 2 * NT)
                        transpose_y(job[1], uses)
                    elif job[0] == "M":
                        pe.wait_ge(scs_free, b * 2 * H + 2 * HQ + (q + 1) * 2 * HQ + 1)
                        maxima(job[1], uses)
                    else:
                        tail.append(job)
                if unit >= 1:
                    product(b, unit - 1)
                for job in tail:
                    merge_head(b, job[1], uses)
                if has_s:
                    scores(sn + 1, nq, i, 1)
            product(b, UN - 1)
            merge_head(b, H - 1, uses)

            def transpose_attn(t):
                for job, ks_ in ((("XA", t), range(4)), (("XB", t), (4,))):
                    bank = uses.bank(job)
                    bank_free(uses, job)
                    for m, k in enumerate(ks_):
                        last = pe.transpose(mm[bank][:, m * P:(m + 1) * P], attn[:, t, k * P:(k + 1) * P], ident[:, :])
                    last.then_inc(mm_full, 1)

            def output(t):
                pe.wait_ge(at_done, b * 2 * NT + 2 * t + 2)
                for half in range(2):
                    job = ("Y", t, half)
                    bank = uses.bank(job)
                    bank_free(uses, job)
                    cols = slice(half * HALF, (half + 1) * HALF)
                    acc = mm[bank][:, 0:HALF]
                    n = 0
                    for k in range(NK - 1):
                        for lhs, rhs in ((at_hi, wo_hi), (at_hi, wo_lo), (at_lo, wo_hi)):
                            pe.matmul(acc, lhs[:, t % 2, k, :], rhs[:, k, cols], start=(n == 0), stop=False)
                            n += 1
                    pe.matmul(acc, at_hi[:, t % 2, 4, :], wo_hi[:, 4, cols], start=False, stop=False)
                    pe.matmul(acc, at_lo[:, t % 2, 4, :], wo_hi[:, 4, cols], start=False, stop=True
                              ).then_inc(mm_full, 1)

            pe.wait_ge(o_done, b * (H + 1) + H + 1)
            transpose_attn(0)
            for t in range(NT):
                if t + 1 < NT:
                    transpose_attn(t + 1)
                output(t)

        with pe.Fori(0, B - 1) as b:
            body(b, True)
        body(B - 1, False)
        pe.wait_ge(mm_full, len(PROLOGUE) + N_BODY * (B - 1) + len(in_order(JOBS[False])))
        pe.sem_inc(a_over, 1)

        s = sems_b
        pe.wait_ge(s["w_lo"], 10)

        def up(b, j):
            bank = (j + 1) % 2
            if j < 2:
                pe.wait_ge(s["ztmp_done"], b * NK + NK - 1 + j)
            else:
                pe.wait_ge(s["g_done"], b * NJ + j)
            cols = slice(j * P, (j + 1) * P)
            if j == 0:
                pe.wait_ge(s["z_done"], b * NK + NK)
            split_product(mm[bank][:, :], lambda k: w1_hi[:, k, cols], lambda k: w1_lo[:, k, cols],
                          lambda k: z_hi[:, k, :], lambda k: z_lo[:, k, :]).then_inc(s["mm_full"], 1)

        def down(b, j):
            pe.wait_ge(s["h_done"], b * NJ + j + 1)
            if j == 0:
                pe.wait_ge(s["yo_done"], b * 2 * NT + 1)
            for t in range(NT):
                toks = slice(t * P, (t + 1) * P)
                pair = y_pair[t // 2][:, YA * (t % 2):YA * (t % 2) + YA]
                for n, (lhs, rhs) in enumerate(((h_hi, w2_hi), (h_hi, w2_lo), (h_lo, w2_hi))):
                    pe.matmul(pair, lhs[:, j % 2, toks], rhs[:, j, 0:YA],
                              start=(j == 0 and n == 0 and t % 2 == 0), stop=(j == NJ - 1 and n == 2),
                              skip_group_check=True)
                    last = pe.matmul(y_own[t][:, 0:YB], lhs[:, j % 2, toks], rhs[:, j, YA:D],
                                     start=(j == 0 and n == 0), stop=(j == NJ - 1 and n == 2))
            return last.then_inc(s["m2_done"], 1)

        def body_b(b):
            for k in range(NK):
                bank = k % 2
                if k < 2:
                    pe.wait_ge(s["g_done"], b * NJ + 1)
                else:
                    pe.wait_ge(s["ztmp_done"], b * NK + k - 1)
                if k == 0:
                    pe.wait_ge(s["xhat_done"], b * NT + NT)
                for t in range(NT):
                    last = pe.transpose(mm[bank][:, t * P:(t + 1) * P], xn[:, t, k * P:(k + 1) * P], ident[:, :])
                last.then_inc(s["mm_full"], 1)
            up(b, 0)
            for j in range(1, NJ):
                up(b, j)
                down(b, j - 1)
            down(b, NJ - 1)

        with pe.Fori(0, B) as b:
            body_b(b)

    block.__exit__(None, None, None)
    slow.__exit__(None, None, None)


def kernel(**inputs):
    import numpy as _np
    import concourse.bacc as _bacc
    from concourse import mybir as _mybir
    from concourse.bass_utils import run_bass_kernel_spmd as _run

    a = {k.removeprefix("L0_cond_"): _np.asarray(v) for k, v in inputs.items()}
    qkv_w, qkv_b = a["qkv_w"], a["qkv_b"]
    wqk = qkv_w[:, :2 * D].reshape(D, 2, NQ, QW).transpose(0, 2, 1, 3).reshape(D, 2 * D)
    bqk = qkv_b[:2 * D].reshape(2, NQ, QW).transpose(1, 0, 2).reshape(NC, P).T
    laid = {
        "x": a["x"], "cond_t": a["cond_1152"].T, "wqk": wqk, "bqk": bqk,
        "wv": qkv_w[:, 2 * D:], "bv": qkv_b[2 * D:], "wo": a["out_w"], "bo": a["out_b"],
        "w1": a["w1"], "b1": a["b1"].reshape(NJ, P).T, "w2": a["w2"], "b2": a["b2"],
        "ada_w": a["ada_w"], "ada_b": a["ada_b"],
    }
    nc = _bacc.Bacc("TRN2", target_bir_lowering=False, num_devices=1, dynamic_dma_scratch_size=2048)
    arrays, args = {}, []
    for name, v in laid.items():
        v = _np.ascontiguousarray(v)
        arrays[f"in_{name}"] = v
        args.append(nc.dram_tensor(f"in_{name}", v.shape, _mybir.dt.from_np(v.dtype), kind="ExternalInput").ap())
    args.append(nc.dram_tensor("out_x", (B, T, D), F32, kind="ExternalOutput").ap())
    conditioned_block(nc, *args)
    r = _run(nc, [arrays], core_ids=[0])
    return r.results[0]["out_x"]
```

```python
import concourse.bass as bass
from concourse import mybir

F32 = mybir.dt.float32
F32R = mybir.dt.float32r
ACT = mybir.ActivationFunctionType
ALU = mybir.AluOpType
AX_X = mybir.AxisListType.X

B, T, D = 8, 512, 576
H, HD = 16, 36
E = 4 * D
P = 128
EPS = 1e-6
NT = T // P
NK = 5
TAIL = D - 4 * P
DP = NK * P
NQ = 4
HQ = H // NQ
NC = 2 * D // P
QW = HQ * HD
UN = 2 * H
VW = 2 * HD + 1
MW = HD + 2
HALF = D // 2
NJ = E // P
YA = 256
YB = D - YA
T_BANK = (1, 0, 1, 0, 0)
SCALE = float(HD) ** -0.5
RAW = E
CHUNKS = {0: (0, 1, 2), 1: (3, 4), 2: (5, 6), 3: (7, 8)}


def v_count(uses, half, t):
    place = half * NT + t
    if uses.jobs is PROLOGUE:
        return place
    return uses.b * 2 * NT + place + (0 if place >= NT + 2 else 2 * NT)


def p_batch(uses, c):
    if uses.jobs is PROLOGUE:
        return 0
    return uses.b if c == NC - 1 else uses.b + 1


def slot_writes(b, c):
    return b * 16 * (5 - c % 2) + 16 * (c // 2) + 16


class Layout:

    def __init__(self, nc, base):
        self.nc, self.at = nc, base

    def tile(self, name, shape, dtype=F32):
        n = 4
        for s in shape[1:]:
            n *= s
        t = self.nc.alloc_sbuf_tensor_at(name, shape, dtype, offset=self.at)
        self.at += (n + 31) // 32 * 32
        return t


def f32(ap):
    return ap.bitcast(F32)


def unit_jobs(has_next):
    jobs = {unit: [] for unit in range(UN)}
    jobs[1], jobs[3], jobs[5] = [("P", NC - 1)], [("V", 1, 2)], [("V", 1, 3)]
    if has_next:
        for k, unit in enumerate((10, 11, 11, 12, 13)):
            jobs[unit].append(("T", k))
    for q in range(NQ if has_next else NQ - 1):
        jobs[8 * q + 6].append(("M", (q + 1) % NQ))
    if has_next:
        for c, unit in enumerate((15, 17, 19, 22, 25, 28, 31)):
            jobs[unit].append(("P", c))
        for t, unit in enumerate((20, 23, 26, 29)):
            jobs[unit].append(("V", 0, t))
    jobs["flush"] = [("P", 7), ("V", 1, 0), ("V", 1, 1)] if has_next else []
    for t in range(NT):
        jobs["flush"] += [("Y", t, 0), ("Y", t, 1)]
    return jobs


def in_order(jobs):
    return [j for k in list(range(UN)) + ["flush"] for j in jobs[k]]


PROLOGUE = ([("T", k) for k in range(NK)] + [("P", c) for c in range(NC - 1)]
            + [("V", 0, t) for t in range(NT)] + [("V", 1, 0), ("V", 1, 1), ("M", 0)])
JOBS = {True: unit_jobs(True), False: unit_jobs(False)}
N_BODY = len(in_order(JOBS[True]))
assert N_BODY % 2 == 0
SCORE_TILES = {0: (0, 1), 1: (2, 3, 4), 2: (5, 6, 7), 3: (8, 9, 10), 4: (11, 12, 13), 5: (14, 15)}
N_SCORE = HQ * NT


class Uses:

    def __init__(self, first, jobs, b=0):
        self.first, self.jobs, self.b = first, jobs, b

    def full(self, job):
        return self.first + self.jobs.index(job) + 1

    def before(self, job):
        earlier = [j for j in self.jobs[:self.jobs.index(job)] if self.bank(j) == self.bank(job)]
        return earlier[-1] if earlier else None

    def bank(self, job):
        return (self.first + self.jobs.index(job)) % 2


def body_uses(b, has_next):
    return Uses(b * N_BODY + len(PROLOGUE), in_order(JOBS[has_next]), b)


def conditioned_block(nc, x, cond_t, wqk, bqk, wv, bv, wo, bo, w1, b1, w2, b2, ada_w, ada_b, out):
    base = (nc.sbuf_base + 63) // 64 * 64
    lay = Layout(nc, base)
    sem = nc.alloc_semaphore

    mods = nc.dram_tensor("mods", [6, B, D], F32, kind="Internal").ap()
    qk_scr = nc.dram_tensor("qk_scr", [B, 2, 2 * D, T], F32, kind="Internal").ap()
    x1 = nc.dram_tensor("x1", [B, T, D], F32, kind="Internal").ap()
    bias_o = nc.dram_tensor("bias_o", [D], F32, kind="Internal").ap()

    ident = lay.tile("ident", [P, P])
    stats = lay.tile("stats", [P, NT, 2, 6])
    moments = lay.tile("moments", [P, NT, 2])
    rstd = lay.tile("rstd", [P, NT])
    eps_half = lay.tile("eps_half", [P, 2, NT])
    modt = lay.tile("modt", [P, 2, NK])
    phase_base = lay.at
    nident = lay.tile("nident", [P, P])
    merge_f = lay.tile("merge_f", [VW, MW])
    merge = lay.tile("merge", [VW, MW], F32R)
    bqk_sb = lay.tile("bqk_sb", [P, NC])
    rowmax = lay.tile("rowmax", [P, NT, H])
    rden = lay.tile("rden", [P, 4, NT, 1])
    negmax = lay.tile("negmax", [HQ, 2, T], F32R)
    wqk_hi = lay.tile("wqk_hi", [P, NK, 2 * D], F32R)
    wqk_lo = lay.tile("wqk_lo", [P, NK - 1, 2 * D], F32R)
    wv_hi = lay.tile("wv_hi", [P, NK, D], F32R)
    wv_lo = lay.tile("wv_lo", [P, NK - 1, D], F32R)
    wo_hi = lay.tile("wo_hi", [P, NK, D], F32R)
    wo_lo = lay.tile("wo_lo", [P, NK - 1, D], F32R)
    y_hi = lay.tile("y_hi", [P, NK, T], F32R)
    y_lo = lay.tile("y_lo", [P, NK, T], F32R)
    y_tmp = lay.tile("y_tmp", [P, 2, T])
    dense = lay.tile("dense", [P, 2, 2, T], F32R)
    xt = lay.tile("xt", [P, NT, DP])
    attn = lay.tile("attn", [P, NT, DP])
    resid_tmp = lay.tile("resid_tmp", [P, D])
    c2_sb = lay.tile("c2_sb", [P, D])
    m2_sb = lay.tile("m2_sb", [P, D])
    pv_hi = lay.tile("pv_hi", [VW, 2, T], F32R)
    pv_at = lay.at
    pv_lo = lay.tile("pv_lo", [VW, 2, T], F32R)
    pv_end = lay.at
    lay.at = pv_at
    pv_f = lay.tile("pv_f", [VW, 2, T])
    assert lay.at == pv_end
    shared = lay.at
    qs = [lay.tile(f"qs{i}", [3 * HD + 2, HQ, T], F32R) for i in range(2)]
    ks = [lay.tile(f"ks{i}", [3 * HD + 2, HQ, T], F32R) for i in range(2)]
    v_sb = lay.tile("v_sb", [P, NT, H, VW], F32R)
    e_at = lay.at
    e_lo = lay.tile("e_lo", [P, 2, 2 * T], F32R)
    e_hi = lay.tile("e_hi", [P, 2, 2 * T], F32R)
    a_end = lay.at
    lay.at = e_at
    e_f = lay.tile("e_f", [P, 2, 2 * T])
    lay.at = e_at
    at_hi = lay.tile("at_hi", [P, 2, NK, P], F32R)
    at_lo = lay.tile("at_lo", [P, 2, NK, P], F32R)
    lay.at = shared
    raw = [lay.tile(f"raw{i}", [P, NK, D]) for i in range(4)]
    cond_sb = lay.tile("cond_sb", [P, NK, B])
    cond_e = lay.tile("cond_e", [P, NK, B])
    cond_s = lay.tile("cond_s", [P, NK, B])
    mod_row = lay.tile("mod_row", [B, 2, D])
    adab_sb = lay.tile("adab_sb", [B, 6, D])
    bv_sb = lay.tile("bv_sb", [P, NK])
    bo_row = lay.tile("bo_row", [1, D])
    assert lay.at <= a_end <= nc.sbuf_usable_end, (lay.at, a_end)
    lay.at = phase_base
    w1_hi = lay.tile("w1_hi", [P, NK, E], F32R)
    w1_lo = lay.tile("w1_lo", [P, NK - 1, E], F32R)
    w2_hi = lay.tile("w2_hi", [P, NJ, D], F32R)
    w2_lo = lay.tile("w2_lo", [P, NJ, D], F32R)
    b1_sb = lay.tile("b1_sb", [P, NJ])
    m5_sb = lay.tile("m5_sb", [P, D])
    c5_sb = lay.tile("c5_sb", [P, D])
    raw_at = lay.at
    z_hi = lay.tile("z_hi", [P, NK, T], F32R)
    z_lo = lay.tile("z_lo", [P, NK, T], F32R)
    g_f = lay.tile("g_f", [P, 2, T])
    h_hi = lay.tile("h_hi", [P, 2, T], F32R)
    h_lo = lay.tile("h_lo", [P, 2, T], F32R)
    xn = lay.tile("xn", [P, NT, DP])
    xr = lay.tile("xr", [P, NT, D])
    y_out = lay.tile("y_out", [P, D])
    b_end = lay.at
    lay.at = raw_at
    raw2 = [lay.tile(f"raw2_{i}", [P, RAW]) for i in range(3)]
    assert lay.at <= b_end <= nc.sbuf_usable_end, b_end

    mm = [nc.alloc_psum_tensor(f"mm{i}", [P, 512], F32) for i in range(2)]
    pv = [nc.alloc_psum_tensor(f"pv{i}", [P, 512], F32) for i in range(2)]
    sct = nc.alloc_psum_tensor("sct", [P, 2, 512], F32)
    scs = nc.alloc_psum_tensor("scs", [P, 2, 512], F32)
    y_pair = pv
    y_own = [sct[:, 0, :], sct[:, 1, :], scs[:, 0, :], scs[:, 1, :]]

    def at_psum(t, part):
        return scs[:, t % 2, :] if part == 0 else pv[t % 2][:, 0:P]

    s_const = sem("s_const")
    s_small = sem("s_small")
    s_ada = [sem(f"s_ada{i}") for i in range(2)]
    s_raw = sem("s_raw")
    s_rawk = [sem(f"s_rawk{i}") for i in range(4)]
    s_cond = sem("s_cond")
    s_mod_full = sem("s_mod_full")
    s_mod_row = sem("s_mod_row")
    s_mod_out = [sem(f"s_mod_out{i}") for i in range(2)]
    s_bo_full = sem("s_bo_full")
    s_bo_done = sem("s_bo_done")
    s_bo_out = sem("s_bo_out")
    s_w_hi = sem("s_w_hi")
    s_w_lo = sem("s_w_lo")
    mm_full = sem("mm_full")
    xn_in = sem("xn_in")
    xr_in = sem("xr_in")
    modt_in = sem("modt_in")
    m2_in = sem("m2_in")
    c2_done = sem("c2_done")
    chain = sem("chain")
    scaled = sem("scaled")
    var_done = sem("var_done")
    rstd_done = sem("rstd_done")
    xhat_done = sem("xhat_done")
    ytmp_done = sem("ytmp_done")
    yhi_done = sem("yhi_done")
    y_done = sem("y_done")
    p_hi = sem("p_hi")
    p_done = sem("p_done")
    dense_out = [sem(f"dense_out{i}") for i in range(2)]
    vhi_done = sem("vhi_done")
    v_done = sem("v_done")
    stack_in = [[sem(f"stack{i}_half{j}_in") for j in range(2)] for i in range(2)]
    scs_full = sem("scs_full")
    scs_free = sem("scs_free")
    neg_hi = sem("neg_hi")
    neg_done = sem("neg_done")
    rows_in = [sem(f"rows_in{i}") for i in range(2)]
    sct_full = sem("sct_full")
    sct_free = sem("sct_free")
    ehi_done = sem("ehi_done")
    elo_done = sem("elo_done")
    pv_done = sem("pv_done")
    pvhi_done = sem("pvhi_done")
    pvlo_done = sem("pvlo_done")
    o_full = sem("o_full")
    rden_done = sem("rden_done")
    o_done = sem("o_done")
    x_full = sem("x_full")
    at_hi_done = sem("at_hi_done")
    at_done = sem("at_done")
    yb_done = sem("yb_done")
    r_add = sem("r_add")
    x1_out = sem("x1_out")
    sp_steps = sem("sp_steps")
    a_over = sem("a_over")

    sems_b = {n: sem("b_" + n) for n in (
        "small w_hi w_lo mm_full xn_in xr_in modt_in m5_in chain var_done rstd_done c5_done"
        " scaled xhat_done ztmp_done zhi_done z_done g_done hhi_done h_done m2_done yo_done"
        " o_add out").split()}

    def gather_mod(eng, section, b, done):
        src = mods[section:section + 2, b, :]
        for n in range(2):
            eng.dma_start(modt[:, n, 0:4], src[n, 0:4 * P].rearrange("(k p) -> p k", p=P)).then_inc(done, 16)
        tail = src[:, 4 * P:D].rearrange("s (p o) -> p s o", o=1)
        eng.dma_start(modt[0:TAIL, :, 4:5], tail).then_inc(done, 16)
        eng.dma_start(modt[TAIL:P, :, 4:5], tail).then_inc(done, 16)

    def load_rows(eng, dst, src, done):
        eng.dma_start(dst[:, 0:4, :], src[0:4 * P, :].rearrange("(k p) n -> p k n", p=P)).then_inc(done, 16)
        eng.dma_start(dst[0:TAIL, 4, :], src[4 * P:D, :]).then_inc(done, 16)
        eng.dma_start(dst[TAIL:P, 4, :], src[4 * P:D, :]).then_inc(done, 16)

    slow = nc.allow_non_contiguous_dma(reason="a feature to a partition, 5 KB a batch")
    slow.__enter__()
    block = nc.Block()
    block.__enter__()

    @block.sync
    def _(sp):
        def write_chunk(b, c):
            sp.wait_ge(p_done, b * NC + c + 1)
            sp.dma_start(qk_scr[b, :, c * P:(c + 1) * P, :].rearrange("h p t -> p h t"),
                         f32(dense[:, c % 2, :, :])).then_inc(dense_out[c % 2], 16)

        def load_stack(b, q, half, units=None):
            if half == 0:
                for c in CHUNKS[q] if q == 0 else (CHUNKS[q][0] - 1,) + CHUNKS[q]:
                    sp.wait_ge(dense_out[c % 2], slot_writes(b, c) + 16)
                    sp.sem_inc(sp_steps, 1)
            if units is not None:
                sp.wait_ge(sct_full, units + 4 * half + 4 + 1)
            par = q % 2
            heads = slice(2 * half, 2 * half + 2)
            for dst, first, parts in ((qs[par], 0, (0, 1, 0)), (ks[par], QW, (0, 0, 1))):
                at = 2 * QW * q + first + 2 * half * HD
                for n, part in enumerate(parts):
                    sp.dma_start(f32(dst[n * HD:(n + 1) * HD, heads, :]),
                                 qk_scr[b, part, at:at + 2 * HD, :].rearrange("(i r) t -> r i t", r=HD)
                                 ).then_inc(stack_in[par][half], 16)

        def load_neg(count, q):
            sp.wait_ge(neg_done, count)
            for n in range(2):
                sp.dma_start(f32(qs[q % 2][3 * HD + n:3 * HD + n + 1, :, :]), f32(negmax[:, n, :])
                             ).then_inc(rows_in[q % 2], 16)

        def load_x(b, done):
            for t in range(NT):
                sp.dma_start(xt[:, t, 0:D], x[b, t * P:(t + 1) * P, :]).then_inc(done, 16)

        for s in dense_out:
            sp.sem_inc(s, 16)
        sp.sem_inc(x1_out, 16)
        load_rows(sp, cond_sb, cond_t, s_small)
        for s in range(6):
            sp.dma_start(adab_sb[:, s, :], ada_b[s * D:(s + 1) * D].partition_broadcast(B)).then_inc(s_small, 16)
        sp.dma_start(bqk_sb[:, :], bqk).then_inc(s_small, 16)
        sp.dma_start(bv_sb[:, 0:4], bv[0:4 * P].rearrange("(k p) -> p k", p=P)).then_inc(s_small, 16)
        sp.dma_start(bv_sb[0:TAIL, 4:5], bv[4 * P:D].rearrange("(p o) -> p o", o=1)).then_inc(s_small, 16)
        sp.dma_start(bo_row[:, :], bo.rearrange("(o n) -> o n", o=1)).then_inc(s_small, 16)
        load_rows(sp, raw[0], ada_w[:, 0:D], s_ada[0])
        load_rows(sp, raw[1], ada_w[:, D:2 * D], s_ada[1])
        load_x(0, xn_in)
        for i in range(2):
            load_rows(sp, raw[2 + i], wqk[:, i * D:(i + 1) * D], s_rawk[i])
        for s in range(6):
            sp.wait_ge(s_mod_row, 2 * s + 2)
            sp.dma_start(mods[s], mod_row[:, s % 2, :]).then_inc(s_mod_out[s % 2], 16)
            if s + 2 < 6:
                load_rows(sp, raw[s % 2], ada_w[:, (s + 2) * D:(s + 3) * D], s_ada[s % 2])
            if s == 1:
                for i in range(2):
                    sp.wait_ge(s_mod_out[i], 16)
                gather_mod(sp, 0, 0, modt_in)
        for i, w in enumerate((wv, wo)):
            sp.wait_ge(s_w_hi, i + 1)
            sp.wait_ge(s_w_lo, 2 * i + 2)
            load_rows(sp, raw[2 + i], w, s_rawk[2 + i])
        for i in range(2):
            sp.wait_ge(s_mod_out[i], 48)
        for c in range(3):
            write_chunk(0, c)
        sp.wait_ge(s_w_hi, 4)
        sp.wait_ge(s_w_lo, 8)
        sp.wait_ge(s_bo_done, 2)
        sp.dma_start(bias_o.rearrange("(o n) -> o n", o=1), bo_row[:, :]).then_inc(s_bo_out, 16)
        sp.wait_ge(s_bo_out, 16)
        sp.wait_ge(s_const, 12)
        load_stack(0, 0, 0)
        load_stack(0, 0, 1)
        for c in range(3, 5):
            write_chunk(0, c)
        load_stack(0, 1, 0)
        load_stack(0, 1, 1)
        for c in range(5, NC - 1):
            write_chunk(0, c)
        load_neg(1, 0)

        def body(b, has_next):
            if has_next:
                sp.wait_ge(x1_out, b * 64 + 16)
                load_x(b + 1, xn_in)
                sp.wait_ge(y_done, b * NK + NK)
                gather_mod(sp, 0, b + 1, modt_in)
            write_chunk(b, NC - 1)
            load_stack(b, 2, 0, b * UN)
            load_neg(b * NQ + 2, 1)
            load_stack(b, 2, 1, b * UN)
            load_stack(b, 3, 0, b * UN + 8)
            if has_next:
                sp.wait_ge(mm_full, body_uses(b, has_next).full(("T", NK - 1)))
            sp.wait_ge(x1_out, b * 64 + 16)
            load_x(b, xr_in)
            sp.dma_start(m2_sb[:, :], mods[2, b].partition_broadcast(P)).then_inc(m2_in, 16)
            sp.dma_start(c2_sb[:, :], bias_o.partition_broadcast(P)).then_inc(m2_in, 16)
            load_neg(b * NQ + 3, 2)
            if has_next:
                write_chunk(b + 1, 0)
            load_stack(b, 3, 1, b * UN + 8)
            if has_next:
                write_chunk(b + 1, 1)
                write_chunk(b + 1, 2)
                load_stack(b + 1, 0, 0, b * UN + 16)
            load_neg(b * NQ + 4, 3)
            if has_next:
                write_chunk(b + 1, 3)
                load_stack(b + 1, 0, 1, b * UN + 16)
                write_chunk(b + 1, 4)
                load_stack(b + 1, 1, 0, b * UN + 24)
                write_chunk(b + 1, 5)
                load_neg(b * NQ + 5, 0)
                load_stack(b + 1, 1, 1, b * UN + 24)
                write_chunk(b + 1, 6)
                write_chunk(b + 1, 7)
            for t in range(NT):
                sp.wait_ge(r_add, b * NT + t + 2)
                sp.dma_start(x1[b, t * P:(t + 1) * P, :], xt[:, t, 0:D]).then_inc(x1_out, 16)

        with sp.Fori(0, B - 1) as b:
            body(b, True)
        body(B - 1, False)
        sp.wait_ge(x1_out, 64 * B + 16)

        s = sems_b
        sp.wait_ge(a_over, 4)
        sp.dma_start(b1_sb[:, :], b1).then_inc(s["small"], 16)
        for n in range(10):
            if n >= 3:
                sp.wait_ge(s["w_hi"], n - 2)
                sp.wait_ge(s["w_lo"], n - 2)
            slot, done = raw2[n % 3], s_rawk[n % 3]
            if n < 4:
                sp.dma_start(slot[:, :], w1[n * P:(n + 1) * P, :]).then_inc(done, 16)
            elif n == 4:
                sp.dma_start(slot[0:TAIL, :], w1[4 * P:D, :]).then_inc(done, 16)
                sp.dma_start(slot[TAIL:P, :], w1[4 * P:D, :]).then_inc(done, 16)
            else:
                j = 4 * (n - 5)
                m = min(4, NJ - j)
                sp.dma_start(slot[:, 0:m * D].rearrange("p (j n) -> p j n", n=D),
                             w2[j * P:(j + m) * P, :].rearrange("(j p) n -> p j n", p=P)).then_inc(done, 16)
        sp.wait_ge(s["w_hi"], 10)
        sp.wait_ge(s["w_lo"], 10)

        def load_x1(b):
            for t in range(NT):
                sp.dma_start(xn[:, t, 0:D], x1[b, t * P:(t + 1) * P, :]).then_inc(s["xn_in"], 16)
            gather_mod(sp, 3, b, s["modt_in"])

        load_x1(0)

        def body_b(b, has_next):
            sp.wait_ge(s["out"], b * 64 + 16)
            sp.dma_start(m5_sb[:, :], mods[5, b].partition_broadcast(P)).then_inc(s["m5_in"], 16)
            sp.dma_start(c5_sb[:, :], b2.partition_broadcast(P)).then_inc(s["m5_in"], 16)
            for t in range(NT):
                sp.dma_start(xr[:, t, :], x1[b, t * P:(t + 1) * P, :]).then_inc(s["xr_in"], 16)
            if has_next:
                sp.wait_ge(s["z_done"], b * NK + NK)
                load_x1(b + 1)
            for t in range(NT):
                sp.wait_ge(s["o_add"], b * NT + t + 2)
                sp.dma_start(out[b, t * P:(t + 1) * P, :], xr[:, t, :]).then_inc(s["out"], 16)

        sp.sem_inc(s["out"], 16)
        with sp.Fori(0, B - 1) as b:
            body_b(b, True)
        body_b(B - 1, False)
        sp.wait_ge(s["out"], 64 * B + 16)

    @block.gpsimd
    def _(pool):
        def inverse_deviation(count, var_sem, done):
            pool.wait_ge(var_sem, NT * count)
            pool.tensor_tensor(rstd[:, :], moments[:, :, 1], eps_half[:, 0, :], ALU.add).then_inc(done, 1)
            pool.wait_ge(done, 2 * count - 1)
            pool.tensor_tensor(rstd[:, :], rstd[:, :], eps_half[:, 1, :], ALU.pow).then_inc(done, 1)

        for n, (m, v) in enumerate(((ident[:, :], 0.0), (nident[:, :], 0.0), (merge_f[:, :], 0.0),
                                    (eps_half[:, 0, :], EPS), (eps_half[:, 1, :], -0.5))):
            if n:
                pool.wait_ge(s_const, n)
            pool.memset(m, v).then_inc(s_const, 1)
        for n, (m, fill) in enumerate(((ident, 1.0), (nident, -1.0))):
            pool.wait_ge(s_const, 5 + n)
            pool.affine_select(out=m[:, :], in_=m[:, :], compare_op=ALU.not_equal, fill=fill,
                               base=0, pattern=[[-1, P]], channel_multiplier=1).then_inc(s_const, 1)
        pool.wait_ge(s_const, 7)
        pool.affine_select(out=merge_f[:, 0:HD], in_=merge_f[:, 0:HD], compare_op=ALU.not_equal, fill=1.0,
                           base=0, pattern=[[-1, HD]], channel_multiplier=1).then_inc(s_const, 1)
        pool.wait_ge(s_const, 8)
        pool.affine_select(out=merge_f[:, :], in_=merge_f[:, :], compare_op=ALU.not_equal, fill=1.0,
                           base=-HD, pattern=[[-1, MW]], channel_multiplier=1).then_inc(s_const, 1)
        inverse_deviation(1, var_done, rstd_done)
        pool.wait_ge(s_w_hi, 4)
        pool.wait_ge(s_w_lo, 8)
        pool.wait_ge(s_mod_row, 12)
        for i in range(2):
            pool.wait_ge(s_mod_out[i], 48)
        pool.wait_ge(s_bo_out, 16)
        for i in range(2):
            pool.wait_ge(s_const, 10 + i)
            pool.memset(f32(ks[i][96:3 * HD + 2, :, :]), 1.0).then_inc(s_const, 1)
        pool.wait_ge(s_const, 12)
        pool.memset(f32(v_sb[:, :, :, VW - 1:VW]), 1.0).then_inc(s_const, 1)

        pool.sem_inc(r_add, 1)

        def body(b, has_next):
            for h in range(H):
                pool.wait_ge(pvhi_done, b * H + h + 1)
                pool.tensor_tensor(pv_lo[:, h % 2, :], pv_f[:, h % 2, :], f32(pv_hi[:, h % 2, :]), ALU.subtract
                                   ).then_inc(pvlo_done, 1)
                if h == 2 and has_next:
                    inverse_deviation(b + 2, var_done, rstd_done)
                if h == H // 2 + 2:
                    pool.wait_ge(m2_in, b * 32 + 32)
                    pool.tensor_tensor(c2_sb[:, :], c2_sb[:, :], m2_sb[:, :], ALU.mult).then_inc(c2_done, 1)
                    pool.wait_ge(c2_done, b * (NT + 1) + 1)
                    pool.wait_ge(xr_in, b * 64 + 64)
                if H // 2 + 2 <= h < H // 2 + 2 + NT:
                    t = h - H // 2 - 2
                    pool.tensor_tensor(xt[:, t, 0:D], xt[:, t, 0:D], c2_sb[:, :], ALU.add).then_inc(c2_done, 1)
            for t in range(NT):
                if t == 0:
                    pool.wait_ge(c2_done, b * (NT + 1) + NT + 1)
                pool.wait_ge(yb_done, b * 2 * NT + 2 * t + 3)
                pool.tensor_tensor(xt[:, t, 0:D], xt[:, t, 0:D], resid_tmp[:, :], ALU.add).then_inc(r_add, 1)

        with pool.Fori(0, B - 1) as b:
            body(b, True)
        body(B - 1, False)
        pool.wait_ge(r_add, NT * B + 1)
        pool.sem_inc(a_over, 1)

        s = sems_b
        inverse_deviation(1, s["var_done"], s["rstd_done"])

        def body_b(b, has_next):
            pool.wait_ge(s["m5_in"], b * 32 + 32)
            pool.tensor_tensor(c5_sb[:, :], c5_sb[:, :], m5_sb[:, :], ALU.mult).then_inc(s["c5_done"], 1)
            pool.wait_ge(s["c5_done"], b * (NT + 1) + 1)
            pool.wait_ge(s["xr_in"], b * 64 + 64)
            for t in range(NT):
                pool.tensor_tensor(xr[:, t, :], xr[:, t, :], c5_sb[:, :], ALU.add).then_inc(s["c5_done"], 1)
            if has_next:
                inverse_deviation(b + 2, s["var_done"], s["rstd_done"])

        with pool.Fori(0, B - 1) as b:
            body_b(b, True)
        body_b(B - 1, False)

    @block.scalar
    def _(act):
        def chunk_hi(b, c, uses):
            act.wait_ge(mm_full, uses.full(("P", c)))
            act.wait_ge(dense_out[c % 2], slot_writes(b, c))
            act.activation(dense[:, c % 2, 0, :], mm[uses.bank(("P", c))][:, :], ACT.Identity,
                           bias=bqk_sb[:, c:c + 1]).then_inc(p_hi, 1)

        def v_high(half, t, uses):
            act.wait_ge(mm_full, uses.full(("V", half, t)))
            hd = H // 2
            act.activation(v_sb[:, t, half * hd:(half + 1) * hd, 0:HD],
                           mm[uses.bank(("V", half, t))][:, 0:HALF].rearrange("p (h d) -> p h d", d=HD),
                           ACT.Copy).then_inc(vhi_done, 1)

        def modulate(b, k, uses):
            act.wait_ge(mm_full, uses.full(("T", k)))
            if k == 0:
                act.wait_ge(modt_in, b * 64 + 64)
            if k >= 2:
                act.wait_ge(y_done, b * NK + k - 1)
            act.activation(y_tmp[:, k % 2, :], mm[uses.bank(("T", k))][:, :], ACT.Identity,
                           bias=modt[:, 0, k:k + 1], scale=modt[:, 1, k:k + 1]).then_inc(ytmp_done, 1)
            act.wait_ge(ytmp_done, b * NK + k + 1)
            act.activation(y_hi[:, k, :], y_tmp[:, k % 2, :], ACT.Copy).then_inc(yhi_done, 1)

        act.wait_ge(s_small, 48 + 96 + 64)
        act.activation(cond_e[:, :, :], cond_sb[:, :, :], ACT.Exp, scale=-1.0).then_inc(s_cond, 1)
        for n, (dst, col) in enumerate(((wqk_hi, 0), (wqk_hi, D), (wv_hi, 0), (wo_hi, 0))):
            act.wait_ge(s_rawk[n], 48)
            act.activation(dst[:, :, col:col + D], raw[2 + n % 2][:, :, :], ACT.Copy).then_inc(s_w_hi, 1)
        act.wait_ge(s_const, 9)
        act.activation(merge[:, :], merge_f[:, :], ACT.Copy).then_inc(s_const, 1)
        pro = Uses(0, PROLOGUE)
        for k in range(NK):
            modulate(0, k, pro)
        for c in range(NC - 1):
            chunk_hi(0, c, pro)
        for half, t in [(0, t) for t in range(NT)] + [(1, 0), (1, 1)]:
            v_high(half, t, pro)
        act.wait_ge(mm_full, pro.full(("M", 0)))
        act.activation(negmax[:, 0, :], mm[pro.bank(("M", 0))][0:HQ, :], ACT.Copy).then_inc(neg_hi, 1)
        act.sem_inc(sct_free, 1)

        def head_out(b, h):
            act.wait_ge(pv_done, b * UN + 2 * h + 4)
            if h >= 2:
                act.wait_ge(o_full, b * H + h - 1)
            act.activation(pv_f[:, h % 2, :], pv[h % 2][0:VW, :], ACT.Copy)
            act.activation(pv_hi[:, h % 2, :], pv[h % 2][0:VW, :], ACT.Copy).then_inc(pvhi_done, 1)

        def body(b, has_next):
            uses = body_uses(b, has_next)
            for unit in range(UN):
                n = b * UN + unit
                act.wait_ge(sct_full, n + 2)
                act.wait_ge(pv_done, n + 1)
                act.activation(e_f[:, unit % 2, :].rearrange("p (k t) -> p k t", k=2), sct[:, :, :],
                               ACT.Exp, scale=SCALE).then_inc(sct_free, 1)
                act.wait_ge(sct_free, n + 2)
                act.activation(e_hi[:, unit % 2, :], e_f[:, unit % 2, :], ACT.Copy).then_inc(ehi_done, 1)
                for job in JOBS[has_next][unit]:
                    if job[0] == "P":
                        chunk_hi(p_batch(uses, job[1]), job[1], uses)
                    elif job[0] == "V":
                        v_high(job[1], job[2], uses)
                    elif job[0] == "T":
                        modulate(b + 1, job[1], uses)
                    elif job[0] == "M":
                        q = job[1]
                        act.wait_ge(mm_full, uses.full(job))
                        before = (q - 1) % NQ
                        act.wait_ge(rows_in[before % 2], b * 64 + 32 * (before // 2) + 32)
                        act.activation(negmax[:, 0, :], mm[uses.bank(job)][0:HQ, :], ACT.Copy).then_inc(neg_hi, 1)
                if unit % 2 == 0 and unit >= 2:
                    head_out(b, unit // 2 - 1)
            head_out(b, H - 1)
            if has_next:
                chunk_hi(b + 1, 7, uses)
                v_high(1, 0, uses)
            for t in range(NT):
                if t == 2 and has_next:
                    v_high(1, 1, uses)
                for n, (lo, hi) in enumerate(((0, 4), (4, 5))):
                    act.wait_ge(x_full, b * 2 * NT + 2 * t + n + 1)
                    if t >= 2 and n == 0:
                        act.wait_ge(mm_full, uses.full(("Y", t - 2, 1)))
                    act.activation(at_hi[:, t % 2, lo:hi, :], at_psum(t, n).rearrange("p (k t) -> p k t", t=P),
                                   ACT.Copy).then_inc(at_hi_done, 1)

        with act.Fori(0, B - 1) as b:
            body(b, True)
        body(B - 1, False)
        act.wait_ge(at_hi_done, 2 * NT * B)
        act.sem_inc(a_over, 1)

        s = sems_b
        for n in range(10):
            act.wait_ge(s_rawk[n % 3], 48 + 16 * (n // 3 + 1) + (16 if n % 3 == 1 and n >= 4 else 0))
            if n < 5:
                dst, src = w1_hi[:, n, :], raw2[n % 3][:, :]
            else:
                j = 4 * (n - 5)
                m = min(4, NJ - j)
                dst, src = w2_hi[:, j:j + m, :], raw2[n % 3][:, 0:m * D].rearrange("p (j n) -> p j n", n=D)
            act.activation(dst, src, ACT.Copy).then_inc(s["w_hi"], 1)

        def modulate_b(b, k, full):
            act.wait_ge(s["mm_full"], full)
            if k == 0:
                act.wait_ge(s["modt_in"], b * 64 + 64)
            if k >= 2:
                act.wait_ge(s["z_done"], b * NK + k - 1)
            elif not (isinstance(b, int) and b == 0):
                act.wait_ge(s["h_done"], b * NJ + k - 1)
            act.activation(g_f[:, k % 2, :], mm[T_BANK[k]][:, :], ACT.Identity, bias=modt[:, 0, k:k + 1],
                           scale=modt[:, 1, k:k + 1]).then_inc(s["ztmp_done"], 1)
            act.wait_ge(s["ztmp_done"], b * NK + k + 1)
            act.activation(z_hi[:, k, :], g_f[:, k % 2, :], ACT.Copy).then_inc(s["zhi_done"], 1)

        def body_b(b, has_next):
            for j in range(NJ):
                act.wait_ge(s["mm_full"], b * (NK + NJ) + NK + j + 1)
                if j >= 2:
                    act.wait_ge(s["m2_done"], b * NJ + j - 1)
                act.activation(g_f[:, j % 2, :], mm[(j + 1) % 2][:, :], ACT.Gelu_apprx_tanh,
                               bias=b1_sb[:, j:j + 1]).then_inc(s["g_done"], 1)
                act.wait_ge(s["g_done"], b * NJ + j + 2)
                act.activation(h_hi[:, j % 2, :], g_f[:, j % 2, :], ACT.Copy).then_inc(s["hhi_done"], 1)
            if has_next:
                for k in range(NK):
                    modulate_b(b + 1, k, (b + 1) * (NK + NJ) + k + 1)

        act.sem_inc(s["g_done"], 1)
        act.wait_ge(s["small"], 16)
        for k in range(NK):
            modulate_b(0, k, k + 1)
        with act.Fori(0, B - 1) as b:
            body_b(b, True)
        body_b(B - 1, False)

    @block.vector
    def _(dve):
        def moments_of(b, tile_in, in_sem, ch, done, t):
            if t == 0:
                dve.wait_ge(in_sem, b * 64 + 64)
            dve.bn_stats(stats[:, t, 0, :], tile_in[:, t, 0:HALF]).then_inc(ch, 1)
            dve.bn_stats(stats[:, t, 1, :], tile_in[:, t, HALF:D]).then_inc(ch, 1)
            dve.wait_ge(ch, b * 3 * NT + 3 * t + 2)
            dve.sem_inc(ch, 1)
            dve.bn_aggr(moments[:, t, :], stats[:, t, :, :]).then_inc(done, 1)

        def normalise(b, tile, rs, sc, done, t):
            if t == 0:
                dve.wait_ge(rs, b * 2 + 2)
            dve.tensor_scalar(tile[:, t, 0:D], tile[:, t, 0:D], moments[:, t, 0:1], rstd[:, t:t + 1],
                              ALU.subtract, ALU.mult).then_inc(sc, 1)
            dve.wait_ge(sc, b * NT + t + 1)
            dve.tensor_copy(tile[:, t, D:DP], tile[:, t, 4 * P:D]).then_inc(done, 1)

        def y_low(b, k):
            dve.wait_ge(yhi_done, b * NK + k + 1)
            dve.tensor_tensor(y_lo[:, k, :], y_tmp[:, k % 2, :], f32(y_hi[:, k, :]), ALU.subtract
                              ).then_inc(y_done, 1)

        def chunk_low(b, c, uses):
            dve.wait_ge(p_hi, b * NC + c + 1)
            bank = uses.bank(("P", c))
            dve.scalar_tensor_tensor(dense[:, c % 2, 1, :], mm[bank][:, :], bqk_sb[:, c:c + 1],
                                     f32(dense[:, c % 2, 0, :]), ALU.add, ALU.subtract).then_inc(p_done, 1)

        def v_low(half, t, uses):
            dve.wait_ge(vhi_done, v_count(uses, half, t) + 1)
            heads = slice(half * H // 2, (half + 1) * H // 2)
            dve.tensor_tensor(v_sb[:, t, heads, HD:2 * HD],
                              mm[uses.bank(("V", half, t))][:, 0:HALF].rearrange("p (h d) -> p h d", d=HD),
                              f32(v_sb[:, t, heads, 0:HD]), ALU.subtract).then_inc(v_done, 1)

        def max_of(n, q, tile):
            dve.wait_ge(scs_full, n + 1)
            i, t = divmod(tile, NT)
            dve.tensor_reduce(rowmax[:, t, q * HQ + i:q * HQ + i + 1], scs[:, tile % 2, :], AX_X, ALU.max
                              ).then_inc(scs_free, 1)

        def neg_low(count, q, uses):
            bank = uses.bank(("M", q))
            dve.wait_ge(neg_hi, count)
            dve.tensor_tensor(negmax[:, 1, :], mm[bank][0:HQ, :], f32(negmax[:, 0, :]), ALU.subtract
                              ).then_inc(neg_done, 1)

        dve.sem_inc(yb_done, 1)
        for t in range(NT):
            moments_of(0, xt, xn_in, chain, var_done, t)
        dve.wait_ge(s_cond, 1)
        dve.tensor_scalar(cond_e[:, :, :], cond_e[:, :, :], 1.0, None, ALU.add).then_inc(s_cond, 1)
        dve.wait_ge(s_cond, 2)
        dve.reciprocal(cond_e[:, :, :], cond_e[:, :, :]).then_inc(s_cond, 1)
        dve.wait_ge(s_cond, 3)
        dve.tensor_tensor(cond_s[:, :, :], cond_sb[:, :, :], cond_e[:, :, :], ALU.mult).then_inc(s_cond, 1)
        for t in range(NT):
            normalise(0, xt, rstd_done, scaled, xhat_done, t)

        def mod_half(s, half):
            n = 2 * s + half
            dve.wait_ge(s_mod_full, n + 1)
            if s >= 2 and half == 0:
                dve.wait_ge(s_mod_out[s % 2], 16 * (s // 2))
            cols = slice(half * HALF, (half + 1) * HALF)
            one = 1.0 if s in (1, 4) else 0.0
            dve.scalar_tensor_tensor(mod_row[:, s % 2, cols], scs[0:B, half, 0:HALF], one,
                                     adab_sb[:, s, cols], ALU.add, ALU.add).then_inc(s_mod_row, 1)

        def weights_low(n):
            dst, hi, col = ((wqk_lo, wqk_hi, 0), (wqk_lo, wqk_hi, D), (wv_lo, wv_hi, 0), (wo_lo, wo_hi, 0))[n]
            r = raw[2 + n % 2]
            dve.wait_ge(s_w_hi, n + 1)
            dve.tensor_tensor(dst[:, :, col:col + D], r[:, 0:4, :], f32(hi[:, 0:4, col:col + D]), ALU.subtract
                              ).then_inc(s_w_lo, 1)
            dve.tensor_tensor(hi[TAIL:P, 4, col:col + D], r[TAIL:P, 4, :], f32(hi[TAIL:P, 4, col:col + D]),
                              ALU.subtract).then_inc(s_w_lo, 1)

        for s in range(2):
            mod_half(s, 0)
            mod_half(s, 1)
        weights_low(0)
        weights_low(1)
        pro = Uses(0, PROLOGUE)
        for s in range(2, 6):
            mod_half(s, 0)
            mod_half(s, 1)
        weights_low(2)
        weights_low(3)
        for k in range(NK):
            y_low(0, k)
        for c in range(3):
            chunk_low(0, c, pro)
        for half in range(2):
            cols = slice(half * HALF, (half + 1) * HALF)
            dve.wait_ge(s_bo_full, half + 1)
            dve.tensor_tensor(bo_row[:, cols], pv[half][0:1, 0:HALF], bo_row[:, cols], ALU.add).then_inc(s_bo_done, 1)
        for c in range(3, NC - 1):
            chunk_low(0, c, pro)
        for half, t in [(0, t) for t in range(NT)] + [(1, 0), (1, 1)]:
            if t == 0:
                dve.wait_ge(s_const, 13)
            v_low(half, t, pro)
        for n in range(N_SCORE):
            max_of(n, 0, n)
        neg_low(1, 0, pro)

        def norm(b, h):
            dve.wait_ge(o_full, b * H + h + 1)
            src = pv[h % 2][:, 0:NT * 64].rearrange("p (t c) -> p t c", c=64)
            dve.reciprocal(rden[:, h % 4, :, :], src[:, :, HD:HD + 1]).then_inc(rden_done, 1)
            dve.wait_ge(rden_done, b * H + h + 1)
            dve.tensor_tensor(attn[:, :, h * HD:(h + 1) * HD], src[:, :, 0:HD],
                              rden[:, h % 4, :, :].to_broadcast([P, NT, HD]), ALU.mult).then_inc(o_done, 1)

        def body(b, has_next):
            uses = body_uses(b, has_next)
            for unit in range(UN):
                q, u = divmod(unit, 8)
                n = b * UN + unit
                tiles = SCORE_TILES.get(u, ()) if q < 3 or has_next else ()
                sn = (b * NQ + q + 1) * N_SCORE
                for tile in tiles[:1]:
                    max_of(sn + tile, (q + 1) % NQ, tile)
                if unit % 2 == 0 and unit >= 4:
                    norm(b, unit // 2 - 2)
                for tile in tiles[1:2]:
                    max_of(sn + tile, (q + 1) % NQ, tile)
                dve.wait_ge(ehi_done, n + 1)
                dve.tensor_tensor(e_lo[:, unit % 2, :], e_f[:, unit % 2, :], f32(e_hi[:, unit % 2, :]),
                                  ALU.subtract).then_inc(elo_done, 1)
                for job in JOBS[has_next][unit]:
                    if job[0] == "P":
                        chunk_low(p_batch(uses, job[1]), job[1], uses)
                    elif job[0] == "V":
                        v_low(job[1], job[2], uses)
                    elif job[0] == "T":
                        y_low(b + 1, job[1])
                for tile in tiles[2:]:
                    max_of(sn + tile, (q + 1) % NQ, tile)
                for job in JOBS[has_next][unit]:
                    if job[0] == "M":
                        neg_low(b * NQ + q + 2, job[1], uses)
                if has_next:
                    for t in {6: (0, 1), 7: (2, 3)}.get(unit, ()):
                        moments_of(b + 1, xt, xn_in, chain, var_done, t)
                    for t in {8: (0, 1), 9: (2, 3)}.get(unit, ()):
                        normalise(b + 1, xt, rstd_done, scaled, xhat_done, t)
            norm(b, H - 2)
            if has_next:
                chunk_low(b + 1, 7, uses)
            norm(b, H - 1)
            dve.wait_ge(o_done, b * (H + 1) + H)
            dve.tensor_copy(attn[:, :, D:DP], attn[:, :, 4 * P:D]).then_inc(o_done, 1)
            if has_next:
                v_low(1, 0, uses)

            def transposed_low(t):
                for n, (lo, hi) in enumerate(((0, 4), (4, 5))):
                    dve.wait_ge(at_hi_done, b * 2 * NT + 2 * t + n + 1)
                    dve.tensor_tensor(at_lo[:, t % 2, lo:hi, :], at_psum(t, n).rearrange("p (k t) -> p k t", t=P),
                                      f32(at_hi[:, t % 2, lo:hi, :]), ALU.subtract).then_inc(at_done, 1)

            def times_m2(t):
                for half in range(2):
                    bank = uses.bank(("Y", t, half))
                    cols = slice(half * HALF, (half + 1) * HALF)
                    dve.wait_ge(mm_full, uses.full(("Y", t, half)))
                    if half == 0:
                        dve.wait_ge(r_add, b * NT + t + 1)
                    if t == 0 and half == 0:
                        dve.wait_ge(m2_in, b * 32 + 32)
                    dve.tensor_tensor(resid_tmp[:, cols], mm[bank][:, 0:HALF], m2_sb[:, cols], ALU.mult
                                      ).then_inc(yb_done, 1)

            transposed_low(0)
            transposed_low(1)
            if has_next:
                v_low(1, 1, uses)
            for t in range(NT):
                times_m2(t)
                if t + 2 < NT:
                    transposed_low(t + 2)

        with dve.Fori(0, B - 1) as b:
            body(b, True)
        body(B - 1, False)
        dve.wait_ge(yb_done, 2 * NT * B + 1)
        dve.sem_inc(a_over, 1)

        s = sems_b
        dve.sem_inc(s["yo_done"], 1)
        dve.sem_inc(s["o_add"], 1)
        for n in range(10):
            dve.wait_ge(s["w_hi"], n + 1)
            r = raw2[n % 3]
            if n < 4:
                dve.tensor_tensor(w1_lo[:, n, :], r[:, :], f32(w1_hi[:, n, :]), ALU.subtract).then_inc(s["w_lo"], 1)
            elif n == 4:
                dve.tensor_tensor(w1_hi[TAIL:P, 4, :], r[TAIL:P, :], f32(w1_hi[TAIL:P, 4, :]),
                                  ALU.subtract).then_inc(s["w_lo"], 1)
            else:
                j = 4 * (n - 5)
                m = min(4, NJ - j)
                dve.tensor_tensor(w2_lo[:, j:j + m, :], r[:, 0:m * D].rearrange("p (j n) -> p j n", n=D),
                                  f32(w2_hi[:, j:j + m, :]), ALU.subtract).then_inc(s["w_lo"], 1)

        def norm_b(b, first):
            if first:
                for t in range(NT):
                    moments_of(b, xn, s["xn_in"], s["chain"], s["var_done"], t)
            else:
                for t in range(NT):
                    normalise(b, xn, s["rstd_done"], s["scaled"], s["xhat_done"], t)

        norm_b(0, True)
        norm_b(0, False)

        def hidden_low(b, j):
            dve.wait_ge(s["hhi_done"], b * NJ + j + 1)
            dve.tensor_tensor(h_lo[:, j % 2, :], g_f[:, j % 2, :], f32(h_hi[:, j % 2, :]), ALU.subtract
                              ).then_inc(s["h_done"], 1)

        def z_low(b, k):
            dve.wait_ge(s["zhi_done"], b * NK + k + 1)
            dve.tensor_tensor(z_lo[:, k, :], g_f[:, k % 2, :], f32(z_hi[:, k, :]), ALU.subtract
                              ).then_inc(s["z_done"], 1)

        def add_sums(b, t):
            if t == 0:
                dve.wait_ge(s["m2_done"], b * NJ + NJ)
                dve.wait_ge(s["c5_done"], b * (NT + 1) + NT + 1)
            dve.wait_ge(s["o_add"], b * NT + t + 1)
            pair = y_pair[t // 2][:, YA * (t % 2):YA * (t % 2) + YA]
            dve.tensor_tensor(y_out[:, 0:YA], pair, m5_sb[:, 0:YA], ALU.mult).then_inc(s["yo_done"], 1)
            dve.tensor_tensor(y_out[:, YA:D], y_own[t][:, 0:YB], m5_sb[:, YA:D], ALU.mult
                              ).then_inc(s["yo_done"], 1)
            dve.wait_ge(s["yo_done"], b * 2 * NT + 2 * t + 3)
            dve.tensor_tensor(xr[:, t, :], xr[:, t, :], y_out[:, :], ALU.add).then_inc(s["o_add"], 1)

        def body_b(b, has_next):
            for j in range(NJ):
                hidden_low(b, j)
                if has_next and j == 6:
                    norm_b(b + 1, True)
                if has_next and j == 8:
                    norm_b(b + 1, False)
            if has_next:
                for k in range(4):
                    z_low(b + 1, k)
            add_sums(b, 0)
            add_sums(b, 1)
            if has_next:
                z_low(b + 1, 4)
            add_sums(b, 2)
            add_sums(b, 3)

        for k in range(NK):
            z_low(0, k)
        with dve.Fori(0, B - 1) as b:
            body_b(b, True)
        body_b(B - 1, False)

    @block.tensor
    def _(pe):
        def bank_free(uses, job):
            b, last = uses.b, uses.before(job)
            if last is None:
                if uses.jobs is not PROLOGUE:
                    pe.wait_ge(yb_done, b * 2 * NT + 1)
                return
            kind, n = last[0], last[1]
            prologue = uses.jobs is PROLOGUE
            if kind == "T":
                pe.wait_ge(ytmp_done, (0 if prologue else b + 1) * NK + n + 1)
            elif kind == "P":
                pe.wait_ge(p_done, p_batch(uses, n) * NC + n + 1)
            elif kind == "V":
                pe.wait_ge(v_done, v_count(uses, n, last[2]) + 1)
            elif kind == "M":
                pe.wait_ge(neg_done, 1 if prologue else b * NQ + (n - 1) % NQ + 2)
            else:
                pe.wait_ge(yb_done, b * 2 * NT + 2 * n + last[2] + 2)

        def split_product(acc, w_hi, w_lo, y_h, y_l, chunks=range(NK), before=None):
            for k in chunks:
                if before is not None:
                    before(k)
                terms = [(w_hi, y_h), (w_hi, y_l)] + ([(w_lo, y_h)] if k < NK - 1 else [])
                for n, (w, y) in enumerate(terms):
                    last = pe.matmul(acc, w(k), y(k), start=(k == 0 and n == 0), stop=(k == NK - 1 and n == 1))
            return last

        def project(b, c, uses, part=None):
            job = ("P", c)
            if part != 1:
                bank_free(uses, job)
                if c == 0:
                    pe.wait_ge(y_done, b * NK + NK)
            cols = slice(c * P, (c + 1) * P)
            last = split_product(mm[uses.bank(job)][:, :], lambda k: wqk_hi[:, k, cols],
                                 lambda k: wqk_lo[:, k, cols], lambda k: y_hi[:, k, :],
                                 lambda k: y_lo[:, k, :], (range(NK), range(2), range(2, NK))[
                                     0 if part is None else part + 1])
            if part != 0:
                last.then_inc(mm_full, 1)

        def project_v(half, t, uses):
            job = ("V", half, t)
            bank = uses.bank(job)
            bank_free(uses, job)
            cols = slice(half * HALF, (half + 1) * HALF)
            toks = slice(t * P, (t + 1) * P)
            acc = mm[bank][:, 0:HALF]
            n = 0
            for k in range(NK - 1):
                for lhs, rhs in ((y_hi, wv_hi), (y_hi, wv_lo), (y_lo, wv_hi)):
                    pe.matmul(acc, lhs[:, k, toks], rhs[:, k, cols], start=(n == 0), stop=False)
                    n += 1
            pe.matmul(acc, y_hi[:, 4, toks], wv_hi[:, 4, cols], start=False, stop=False)
            pe.matmul(acc, y_lo[:, 4, toks], wv_hi[:, 4, cols], start=False, stop=True).then_inc(mm_full, 1)

        def transpose_y(k, uses):
            job = ("T", k)
            bank = uses.bank(job)
            bank_free(uses, job)
            for t in range(NT):
                last = pe.transpose(mm[bank][:, t * P:(t + 1) * P], xt[:, t, k * P:(k + 1) * P], ident[:, :])
            last.then_inc(mm_full, 1)

        def scores(n, q, tile):
            if not (isinstance(n, int) and n < 2):
                pe.wait_ge(scs_free, n - 1)
            i, t = divmod(tile, NT)
            pe.matmul(scs[:, tile % 2, :], qs[q % 2][0:3 * HD, i, t * P:(t + 1) * P],
                      ks[q % 2][0:3 * HD, i, :], start=True, stop=True).then_inc(scs_full, 1)

        def maxima(q, uses):
            job = ("M", q)
            bank = uses.bank(job)
            bank_free(uses, job)
            for t in range(NT):
                last = pe.matmul(mm[bank][0:HQ, t * P:(t + 1) * P], rowmax[:, t, q * HQ:(q + 1) * HQ],
                                 nident[:, :], start=True, stop=True)
            last.then_inc(mm_full, 1)

        pe.wait_ge(s_cond, 4)
        for s in range(6):
            pe.wait_ge(s_ada[s % 2], 48 * (s // 2 + 1))
            for half in range(2):
                if s >= 1:
                    pe.wait_ge(s_mod_row, 2 * s - 1 + half)
                for k in range(NK):
                    rows = P if k < NK - 1 else TAIL
                    last = pe.matmul(scs[0:B, half, 0:HALF], cond_s[0:rows, k, :],
                                     raw[s % 2][0:rows, k, half * HALF:(half + 1) * HALF],
                                     start=(k == 0), stop=(k == NK - 1))
                last.then_inc(s_mod_full, 1)
        pro = Uses(0, PROLOGUE)
        pe.wait_ge(s_const, 7)
        pe.wait_ge(xhat_done, NT)
        for k in range(NK):
            transpose_y(k, pro)
        pe.wait_ge(s_w_lo, 4)
        for c in range(3):
            project(0, c, pro)
        pe.wait_ge(s_rawk[3], 48)
        for half in range(2):
            for k in range(NK):
                rows = P if k < NK - 1 else TAIL
                last = pe.matmul(pv[half][0:1, 0:HALF], bv_sb[0:rows, k:k + 1],
                                 raw[3][0:rows, k, half * HALF:(half + 1) * HALF],
                                 start=(k == 0), stop=(k == NK - 1))
            last.then_inc(s_bo_full, 1)
        for c in range(3, NC - 1):
            project(0, c, pro)
        pe.wait_ge(s_w_lo, 6)
        for half, t in [(0, t) for t in range(NT)] + [(1, 0), (1, 1)]:
            project_v(half, t, pro)
        pe.wait_ge(stack_in[0][0], 96)
        pe.wait_ge(stack_in[0][1], 96)
        pe.wait_ge(s_mod_row, 12)
        for n in range(N_SCORE):
            scores(n, 0, n)
        pe.wait_ge(scs_free, N_SCORE)
        maxima(0, pro)
        pe.sem_inc(sct_full, 1)
        pe.sem_inc(pv_done, 2)
        pe.wait_ge(s_w_lo, 8)
        pe.wait_ge(s_const, 13)
        pe.wait_ge(v_done, NT + 2)
        pe.wait_ge(s_bo_done, 2)
        pe.wait_ge(neg_done, 1)

        def product(b, unit):
            h, pair = divmod(unit, 2)
            pe.wait_ge(elo_done, b * UN + unit + 1)
            if pair == 0 and h >= 2:
                pe.wait_ge(o_done, b * (H + 1) + h - 1)
            for kk in range(2):
                for part, e in enumerate((e_hi, e_lo)):
                    last = pe.matmul(pv[h % 2][0:VW, :], v_sb[:, 2 * pair + kk, h, :],
                                     e[:, unit % 2, kk * T:(kk + 1) * T],
                                     start=(pair == 0 and kk == 0 and part == 0),
                                     stop=(pair == 1 and kk == 1 and part == 1))
            last.then_inc(pv_done, 1)

        def merge_head(b, h):
            pe.wait_ge(pvlo_done, b * H + h + 1)
            for t in range(NT):
                for n, part in enumerate((pv_hi, pv_lo)):
                    last = pe.matmul(pv[h % 2][:, 64 * t:64 * t + MW], part[:, h % 2, t * P:(t + 1) * P],
                                     merge[:, :], start=(n == 0), stop=(n == 1))
            last.then_inc(o_full, 1)

        def body(b, has_next):
            uses = body_uses(b, has_next)
            for unit in range(UN):
                q, u = divmod(unit, 8)
                h = unit // 2
                par = q % 2
                if u == 0:
                    for half in range(2):
                        pe.wait_ge(stack_in[par][half], b * 192 + 96 * (q // 2) + 96)
                    pe.wait_ge(rows_in[par], b * 64 + 32 * (q // 2) + 32)
                if unit == 0:
                    pe.wait_ge(v_done, b * 2 * NT + NT)
                if unit == UN // 2:
                    pe.wait_ge(v_done, b * 2 * NT + 2 * NT)
                pe.wait_ge(sct_free, b * UN + unit + 1)
                for kk in range(2):
                    kt = 2 * (unit % 2) + kk
                    last = pe.matmul(sct[:, kk, :], ks[par][:, h % HQ, kt * P:(kt + 1) * P],
                                     qs[par][:, h % HQ, :], start=True, stop=True)
                last.then_inc(sct_full, 1)
                if unit % 2 == 0 and unit >= 4:
                    merge_head(b, unit // 2 - 2)
                nq = (q + 1) % NQ
                tiles = SCORE_TILES.get(u, ()) if q < 3 or has_next else ()
                sn = (b * NQ + q + 1) * N_SCORE
                nb = b if q < 3 else b + 1
                if u in (0, 3) and tiles:
                    pe.wait_ge(stack_in[nq % 2][u // 3], nb * 192 + 96 * (nq // 2) + 96)
                for tile in tiles[:1]:
                    scores(sn + tile, nq, tile)
                for job in JOBS[has_next][unit]:
                    if job[0] == "M":
                        pe.wait_ge(scs_free, sn + N_SCORE)
                        maxima(job[1], uses)
                    elif job[0] == "P":
                        project(p_batch(uses, job[1]), job[1], uses, 1)
                    elif job[0] == "V":
                        project_v(job[1], job[2], uses)
                    elif job[0] == "T":
                        if job[1] == 0:
                            pe.wait_ge(xhat_done, b * NT + 2 * NT)
                        transpose_y(job[1], uses)
                for job in JOBS[has_next].get(unit + 1, ()):
                    if job[0] == "P":
                        project(p_batch(uses, job[1]), job[1], uses, 0)
                for tile in tiles[1:2]:
                    scores(sn + tile, nq, tile)
                if unit >= 1:
                    product(b, unit - 1)
                for tile in tiles[2:]:
                    scores(sn + tile, nq, tile)
            product(b, UN - 1)
            merge_head(b, H - 2)
            if has_next:
                project(b + 1, 7, uses)
            merge_head(b, H - 1)
            if has_next:
                project_v(1, 0, uses)

            def transpose_attn(t):
                for n, chunks in enumerate((range(4), (4,))):
                    if t >= 2:
                        pe.wait_ge(at_done, b * 2 * NT + 2 * (t - 2) + n + 1)
                    for m, k in enumerate(chunks):
                        last = pe.transpose(at_psum(t, n)[:, m * P:(m + 1) * P], attn[:, t, k * P:(k + 1) * P],
                                            ident[:, :])
                    last.then_inc(x_full, 1)

            def output(t):
                pe.wait_ge(at_done, b * 2 * NT + 2 * t + 2)
                for half in range(2):
                    job = ("Y", t, half)
                    bank = uses.bank(job)
                    bank_free(uses, job)
                    cols = slice(half * HALF, (half + 1) * HALF)
                    acc = mm[bank][:, 0:HALF]
                    n = 0
                    for k in range(NK - 1):
                        for lhs, rhs in ((at_hi, wo_hi), (at_hi, wo_lo), (at_lo, wo_hi)):
                            pe.matmul(acc, lhs[:, t % 2, k, :], rhs[:, k, cols], start=(n == 0), stop=False)
                            n += 1
                    pe.matmul(acc, at_hi[:, t % 2, 4, :], wo_hi[:, 4, cols], start=False, stop=False)
                    pe.matmul(acc, at_lo[:, t % 2, 4, :], wo_hi[:, 4, cols], start=False, stop=True
                              ).then_inc(mm_full, 1)

            pe.wait_ge(o_done, b * (H + 1) + H + 1)
            transpose_attn(0)
            transpose_attn(1)
            if has_next:
                project_v(1, 1, uses)
            for t in range(NT):
                output(t)
                if t + 2 < NT:
                    transpose_attn(t + 2)

        with pe.Fori(0, B - 1) as b:
            body(b, True)
        body(B - 1, False)
        pe.wait_ge(mm_full, len(PROLOGUE) + N_BODY * (B - 1) + len(in_order(JOBS[False])))
        pe.sem_inc(a_over, 1)

        s = sems_b
        pe.wait_ge(s["w_lo"], 10)

        def transpose_b(b, k):
            bank = T_BANK[k]
            if k == 0:
                pe.wait_ge(s["xhat_done"], b * NT + NT)
            if k >= 2:
                pe.wait_ge(s["ztmp_done"], b * NK + (1, 2, 4)[k - 2])
            elif not (isinstance(b, int) and b == 0):
                pe.wait_ge(s["g_done"], b * NJ + k)
            for t in range(NT):
                last = pe.transpose(mm[bank][:, t * P:(t + 1) * P], xn[:, t, k * P:(k + 1) * P], ident[:, :])
            last.then_inc(s["mm_full"], 1)

        def up(b, j):
            bank = (j + 1) % 2
            if j < 2:
                pe.wait_ge(s["ztmp_done"], b * NK + (3, 5)[j])
            else:
                pe.wait_ge(s["g_done"], b * NJ + j)
            cols = slice(j * P, (j + 1) * P)
            split_product(mm[bank][:, :], lambda k: w1_hi[:, k, cols], lambda k: w1_lo[:, k, cols],
                          lambda k: z_hi[:, k, :], lambda k: z_lo[:, k, :],
                          before=(lambda k: pe.wait_ge(s["z_done"], b * NK + k + 1)) if j == 0 else None
                          ).then_inc(s["mm_full"], 1)

        def down(b, j):
            pe.wait_ge(s["h_done"], b * NJ + j + 1)
            if j == 0:
                pe.wait_ge(s["yo_done"], b * 2 * NT + 1)
            for t in range(NT):
                toks = slice(t * P, (t + 1) * P)
                pair = y_pair[t // 2][:, YA * (t % 2):YA * (t % 2) + YA]
                for n, (lhs, rhs) in enumerate(((h_hi, w2_hi), (h_hi, w2_lo), (h_lo, w2_hi))):
                    pe.matmul(pair, lhs[:, j % 2, toks], rhs[:, j, 0:YA],
                              start=(j == 0 and n == 0 and t % 2 == 0), stop=(j == NJ - 1 and n == 2),
                              skip_group_check=True)
                    last = pe.matmul(y_own[t][:, 0:YB], lhs[:, j % 2, toks], rhs[:, j, YA:D],
                                     start=(j == 0 and n == 0), stop=(j == NJ - 1 and n == 2))
            return last.then_inc(s["m2_done"], 1)

        def body_b(b, has_next):
            up(b, 0)
            for j in range(1, NJ):
                up(b, j)
                if j < NJ - 1:
                    down(b, j - 1)
            if has_next:
                transpose_b(b + 1, 0)
                transpose_b(b + 1, 1)
            down(b, NJ - 2)
            if has_next:
                transpose_b(b + 1, 2)
                transpose_b(b + 1, 3)
            down(b, NJ - 1)
            if has_next:
                transpose_b(b + 1, 4)

        for k in range(NK):
            transpose_b(0, k)
        with pe.Fori(0, B - 1) as b:
            body_b(b, True)
        body_b(B - 1, False)

    block.__exit__(None, None, None)
    slow.__exit__(None, None, None)


def kernel(**inputs):
    import numpy as _np
    import concourse.bacc as _bacc
    from concourse import mybir as _mybir
    from concourse.bass_utils import run_bass_kernel_spmd as _run

    a = {k.removeprefix("L0_cond_"): _np.asarray(v) for k, v in inputs.items()}
    qkv_w, qkv_b = a["qkv_w"], a["qkv_b"]
    wqk = qkv_w[:, :2 * D].reshape(D, 2, NQ, QW).transpose(0, 2, 1, 3).reshape(D, 2 * D)
    bqk = qkv_b[:2 * D].reshape(2, NQ, QW).transpose(1, 0, 2).reshape(NC, P).T
    laid = {
        "x": a["x"], "cond_t": a["cond_1152"].T, "wqk": wqk, "bqk": bqk,
        "wv": qkv_w[:, 2 * D:], "bv": qkv_b[2 * D:], "wo": a["out_w"], "bo": a["out_b"],
        "w1": a["w1"], "b1": a["b1"].reshape(NJ, P).T, "w2": a["w2"], "b2": a["b2"],
        "ada_w": a["ada_w"], "ada_b": a["ada_b"],
    }
    nc = _bacc.Bacc("TRN2", target_bir_lowering=False, num_devices=1, dynamic_dma_scratch_size=2048)
    arrays, args = {}, []
    for name, v in laid.items():
        v = _np.ascontiguousarray(v)
        arrays[f"in_{name}"] = v
        args.append(nc.dram_tensor(f"in_{name}", v.shape, _mybir.dt.from_np(v.dtype), kind="ExternalInput").ap())
    args.append(nc.dram_tensor("out_x", (B, T, D), F32, kind="ExternalOutput").ap())
    conditioned_block(nc, *args)
    r = _run(nc, [arrays], core_ids=[0])
    return r.results[0]["out_x"]
```

```python
import concourse.bass as bass
from concourse import mybir

F32 = mybir.dt.float32
F32R = mybir.dt.float32r
ACT = mybir.ActivationFunctionType
ALU = mybir.AluOpType
AX_X = mybir.AxisListType.X

B, T, D = 8, 512, 576
H, HD = 16, 36
E = 4 * D
P = 128
EPS = 1e-6
NT = T // P
NK = 5
TAIL = D - 4 * P
DP = NK * P
NQ = 4
HQ = H // NQ
NC = 2 * D // P
QW = HQ * HD
UN = 2 * H
VW = 2 * HD + 1
MW = HD + 2
HALF = D // 2
NJ = E // P
YA = 256
YB = D - YA
T_BANK = (1, 0, 1, 0, 0)
SCALE = float(HD) ** -0.5
RAW = E
CHUNKS = {0: (0, 1, 2), 1: (3, 4), 2: (5, 6), 3: (7, 8)}


def v_count(uses, half, t):
    place = half * NT + t
    if uses.jobs is PROLOGUE:
        return place
    return uses.b * 2 * NT + place + (0 if place >= NT + 2 else 2 * NT)


def p_batch(uses, c):
    if uses.jobs is PROLOGUE:
        return 0
    return uses.b if c == NC - 1 else uses.b + 1


def slot_writes(b, c):
    return b * 16 * (5 - c % 2) + 16 * (c // 2) + 16


class Layout:

    def __init__(self, nc, base):
        self.nc, self.at = nc, base

    def tile(self, name, shape, dtype=F32):
        n = 4
        for s in shape[1:]:
            n *= s
        t = self.nc.alloc_sbuf_tensor_at(name, shape, dtype, offset=self.at)
        self.at += (n + 31) // 32 * 32
        return t


def f32(ap):
    return ap.bitcast(F32)


def unit_jobs(has_next):
    jobs = {unit: [] for unit in range(UN)}
    jobs[1], jobs[2], jobs[4] = [("P", NC - 1)], [("V", 1, 2)], [("V", 1, 3)]
    if has_next:
        for k, unit in enumerate((8, 8, 9, 10, 11)):
            jobs[unit].append(("T", k))
    for q in range(NQ if has_next else NQ - 1):
        jobs[8 * q + 6].append(("M", (q + 1) % NQ))
    if has_next:
        for c, unit in enumerate((13, 15, 19, 21, 25, 27, 31)):
            jobs[unit].append(("P", c))
        for t, unit in enumerate((17, 22, 23, 29)):
            jobs[unit].append(("V", 0, t))
    jobs["flush"] = [("P", 7), ("V", 1, 0), ("V", 1, 1)] if has_next else []
    for t in range(NT):
        jobs["flush"] += [("Y", t, 0), ("Y", t, 1)]
    return jobs


def in_order(jobs):
    return [j for k in list(range(UN)) + ["flush"] for j in jobs[k]]


V_FIRST = [(0, t) for t in range(NT)] + [(1, 0), (1, 1)]
PROLOGUE = ([("T", k) for k in range(NK)] + [("P", c) for c in range(NC - 2)]
            + [("V",) + v for v in V_FIRST] + [("M", 0), ("P", NC - 2)])
JOBS = {True: unit_jobs(True), False: unit_jobs(False)}
N_BODY = len(in_order(JOBS[True]))
assert N_BODY % 2 == 0 and len(PROLOGUE) % 2 == 0
SCORE_TILES = {0: (0, 1), 1: (2, 3, 4), 2: (5, 6, 7), 3: (8, 9, 10), 4: (11, 12, 13), 5: (14, 15)}
N_SCORE = HQ * NT
SCORES_WITH_V = 3
PIECE_UNITS = (7, 15, 22, 25, 28)
PIECE_CHUNKS = (1, 5, 9, 13)


class Uses:

    def __init__(self, first, jobs, b=0):
        self.first, self.jobs, self.b = first, jobs, b

    def full(self, job):
        return self.first + self.jobs.index(job) + 1

    def before(self, job):
        earlier = [j for j in self.jobs[:self.jobs.index(job)] if self.bank(j) == self.bank(job)]
        return earlier[-1] if earlier else None

    def bank(self, job):
        return self.jobs.index(job) % 2


def body_uses(b, has_next):
    return Uses(b * N_BODY + len(PROLOGUE), in_order(JOBS[has_next]), b)


def conditioned_block(nc, x, cond_t, wqk, bqk, wv, bv, wo, bo, w1, b1, w2, b2, ada_w, ada_b, out):
    base = (nc.sbuf_base + 63) // 64 * 64
    lay = Layout(nc, base)
    sem = nc.alloc_semaphore

    mods = nc.dram_tensor("mods", [6, B, D], F32, kind="Internal").ap()
    qk_scr = nc.dram_tensor("qk_scr", [B, 2, 2 * D, T], F32, kind="Internal").ap()
    x1 = nc.dram_tensor("x1", [B, T, D], F32, kind="Internal").ap()
    bias_o = nc.dram_tensor("bias_o", [D], F32, kind="Internal").ap()

    ident = lay.tile("ident", [P, P])
    stats = lay.tile("stats", [P, NT, 2, 6])
    moments = lay.tile("moments", [P, NT, 2])
    rstd = lay.tile("rstd", [P, NT])
    eps_half = lay.tile("eps_half", [P, 2, NT])
    modt = lay.tile("modt", [P, 2, NK])
    b1_sb = lay.tile("b1_sb", [P, NJ])
    small_at = lay.at
    nident = lay.tile("nident", [P, P])
    merge_f = lay.tile("merge_f", [VW, MW])
    merge = lay.tile("merge", [VW, MW], F32R)
    bqk_sb = lay.tile("bqk_sb", [P, NC])
    rowmax = lay.tile("rowmax", [P, NT, H])
    rden = lay.tile("rden", [P, 4, NT, 1])
    negmax = lay.tile("negmax", [HQ, 2, T], F32R)
    small_end = weights_at = lay.at
    wqk_hi = lay.tile("wqk_hi", [P, NK, 2 * D], F32R)
    wqk_lo = lay.tile("wqk_lo", [P, NK - 1, 2 * D], F32R)
    wv_hi = lay.tile("wv_hi", [P, NK, D], F32R)
    wv_lo = lay.tile("wv_lo", [P, NK - 1, D], F32R)
    y_hi = lay.tile("y_hi", [P, NK, T], F32R)
    y_lo = lay.tile("y_lo", [P, NK, T], F32R)
    y_tmp = lay.tile("y_tmp", [P, 2, T])
    dense = lay.tile("dense", [P, 2, 2, T], F32R)
    v_at = lay.at
    v_sb = lay.tile("v_sb", [P, NT, H, VW], F32R)
    v_end = lay.at
    wo_hi = lay.tile("wo_hi", [P, NK, D], F32R)
    wo_lo = lay.tile("wo_lo", [P, NK - 1, D], F32R)
    attn = lay.tile("attn", [P, NT, DP])
    xt = lay.tile("xt", [P, NT, DP])
    resid_tmp = lay.tile("resid_tmp", [P, D])
    c2_sb = lay.tile("c2_sb", [P, D])
    m2_sb = lay.tile("m2_sb", [P, D])
    pv_hi = lay.tile("pv_hi", [VW, 2, T], F32R)
    pv_at = lay.at
    pv_lo = lay.tile("pv_lo", [VW, 2, T], F32R)
    stacks_at = lay.at
    lay.at = pv_at
    pv_f = lay.tile("pv_f", [VW, 2, T])
    qs, ks = [], []
    for i in range(2):
        qs.append(lay.tile(f"qs{i}", [3 * HD + 2, HQ, T], F32R))
        ks.append(lay.tile(f"ks{i}", [3 * HD + 2, HQ, T], F32R))
    e_at = lay.at
    e_lo = lay.tile("e_lo", [P, 2, 2 * T], F32R)
    e_hi = lay.tile("e_hi", [P, 2, 2 * T], F32R)
    a_end = lay.at
    lay.at = e_at
    e_f = lay.tile("e_f", [P, 2, 2 * T])
    lay.at = e_at
    at_hi = lay.tile("at_hi", [P, 2, NK, P], F32R)
    at_lo = lay.tile("at_lo", [P, 2, NK, P], F32R)
    at_end = lay.at
    lay.at = stacks_at
    raw = [lay.tile(f"raw{i}", [P, NK, D]) for i in range(4)]
    cond_sb = lay.tile("cond_sb", [P, NK, B])
    cond_e = lay.tile("cond_e", [P, NK, B])
    cond_s = lay.tile("cond_s", [P, NK, B])
    bv_sb = lay.tile("bv_sb", [P, NK])
    bo_row = lay.tile("bo_row", [1, D])
    assert lay.at <= a_end <= nc.sbuf_usable_end, (lay.at, a_end)
    lay.at = v_at
    mod_row = lay.tile("mod_row", [B, 2, D])
    adab_sb = lay.tile("adab_sb", [B, 6, D])
    assert lay.at <= v_end
    lay.at = weights_at
    w1_hi = lay.tile("w1_hi", [P, NK, E], F32R)
    w1_lo = lay.tile("w1_lo", [P, NK - 1, E], F32R)
    raw_at = lay.at
    raw_b = lay.tile("raw_b", [P, RAW])
    c5_sb = lay.tile("c5_sb", [P, D])
    assert lay.at <= v_at
    lay.at = raw_at
    xr = lay.tile("xr", [P, NT, D])
    lay.at = v_at
    w2_pieces = [lay.tile(f"w2_piece{m}", [P, 4, 2, D], F32R) for m in range(NJ // 4)]
    assert w2_pieces and lay.at <= stacks_at
    lay.at = stacks_at
    xn = lay.tile("xn", [P, NT, DP])
    assert lay.at <= stacks_at + (e_at - stacks_at) // 2
    z_hi = lay.tile("z_hi", [P, NK, T], F32R)
    z_lo = lay.tile("z_lo", [P, NK, T], F32R)
    assert lay.at <= e_at
    h_hi = lay.tile("h_hi", [P, 2, T], F32R)
    h_lo = lay.tile("h_lo", [P, 2, T], F32R)
    w2_last = [lay.tile(f"w2_last{i}", [P, D], F32R) for i in range(2)]
    assert lay.at >= at_end
    g_f = lay.tile("g_f", [P, 2, T])
    w2_last.append(lay.tile("w2_last2", [P, D], F32R))
    assert lay.at <= nc.sbuf_usable_end
    lay.at = small_at
    m5_sb = lay.tile("m5_sb", [P, D])
    w2_last.append(lay.tile("w2_last3", [P, D], F32R))
    assert lay.at <= small_end
    y_out = c5_sb

    def w2_part(j, part):
        m, i = divmod(j, 4)
        return w2_pieces[m][:, i, part, :] if m < len(w2_pieces) else w2_last[2 * i + part][:, :]

    mm = [nc.alloc_psum_tensor(f"mm{i}", [P, 512], F32) for i in range(2)]
    pv = [nc.alloc_psum_tensor(f"pv{i}", [P, 512], F32) for i in range(2)]
    sct = nc.alloc_psum_tensor("sct", [P, 2, 512], F32)
    scs = nc.alloc_psum_tensor("scs", [P, 2, 512], F32)
    y_pair = pv
    y_own = [sct[:, 0, :], sct[:, 1, :], scs[:, 0, :], scs[:, 1, :]]

    def at_psum(t, part):
        return scs[:, t % 2, :] if part == 0 else pv[t % 2][:, 0:P]

    s_const = sem("s_const")
    s_cond_in = sem("s_cond_in")
    s_adab = sem("s_adab")
    s_small = sem("s_small")
    s_ada = [sem(f"s_ada{i}") for i in range(2)]
    s_rawk = [sem(f"s_rawk{i}") for i in range(4)]
    s_cond = sem("s_cond")
    s_mod_full = sem("s_mod_full")
    s_mod_row = sem("s_mod_row")
    s_mod_out = [sem(f"s_mod_out{i}") for i in range(2)]
    s_bo_full = sem("s_bo_full")
    s_bo_done = sem("s_bo_done")
    s_bo_out = sem("s_bo_out")
    s_w_hi = sem("s_w_hi")
    s_w_lo = sem("s_w_lo")
    mm_full = sem("mm_full")
    xn_in = sem("xn_in")
    xr_in = sem("xr_in")
    modt_in = sem("modt_in")
    m2_in = sem("m2_in")
    c2_done = sem("c2_done")
    chain = sem("chain")
    scaled = sem("scaled")
    var_done = sem("var_done")
    rstd_done = sem("rstd_done")
    xhat_done = sem("xhat_done")
    ytmp_done = sem("ytmp_done")
    yhi_done = sem("yhi_done")
    y_done = sem("y_done")
    p_hi = sem("p_hi")
    p_done = sem("p_done")
    dense_out = [sem(f"dense_out{i}") for i in range(2)]
    vhi_done = sem("vhi_done")
    v_done = sem("v_done")
    stack_in = [[sem(f"stack{i}_half{j}_in") for j in range(2)] for i in range(2)]
    scs_full = sem("scs_full")
    scs_free = sem("scs_free")
    neg_hi = sem("neg_hi")
    neg_done = sem("neg_done")
    rows_in = [sem(f"rows_in{i}") for i in range(2)]
    sct_full = sem("sct_full")
    sct_free = sem("sct_free")
    ehi_done = sem("ehi_done")
    elo_done = sem("elo_done")
    elo_pool = sem("elo_pool")
    pv_done = sem("pv_done")
    pvhi_done = sem("pvhi_done")
    pvlo_done = sem("pvlo_done")
    o_full = sem("o_full")
    rden_done = sem("rden_done")
    o_done = sem("o_done")
    x_full = sem("x_full")
    at_hi_done = sem("at_hi_done")
    at_done = sem("at_done")
    yb_done = sem("yb_done")
    r_add = sem("r_add")
    x1_out = sem("x1_out")
    sp_steps = sem("sp_steps")
    a_over = sem("a_over")

    sems_b = {n: sem("b_" + n) for n in (
        "raw w_hi w_lo mm_full xn_in xr_in modt_in m5_in chain var_done rstd_done c5_done"
        " scaled xhat_done ztmp_done zhi_done z_done g_done hhi_done h_done m2_done yo_done"
        " o_add out").split()}

    def gather_mod(eng, section, b, done):
        src = mods[section:section + 2, b, :]
        for n in range(2):
            eng.dma_start(modt[:, n, 0:4], src[n, 0:4 * P].rearrange("(k p) -> p k", p=P)).then_inc(done, 16)
        tail = src[:, 4 * P:D].rearrange("s (p o) -> p s o", o=1)
        eng.dma_start(modt[0:TAIL, :, 4:5], tail).then_inc(done, 16)
        eng.dma_start(modt[TAIL:P, :, 4:5], tail).then_inc(done, 16)

    def load_rows(eng, dst, src, done):
        eng.dma_start(dst[:, 0:4, :], src[0:4 * P, :].rearrange("(k p) n -> p k n", p=P)).then_inc(done, 16)
        eng.dma_start(dst[0:TAIL, 4, :], src[4 * P:D, :]).then_inc(done, 16)
        eng.dma_start(dst[TAIL:P, 4, :], src[4 * P:D, :]).then_inc(done, 16)

    slow = nc.allow_non_contiguous_dma(reason="a feature to a partition, 5 KB a batch")
    slow.__enter__()
    block = nc.Block()
    block.__enter__()

    @block.sync
    def _(sp):
        def write_chunk(b, c):
            sp.wait_ge(p_done, b * NC + c + 1)
            sp.dma_start(qk_scr[b, :, c * P:(c + 1) * P, :].rearrange("h p t -> p h t"),
                         f32(dense[:, c % 2, :, :])).then_inc(dense_out[c % 2], 16)

        def load_stack(b, q, half, units=None):
            if half == 0:
                for c in CHUNKS[q] if q == 0 else (CHUNKS[q][0] - 1,) + CHUNKS[q]:
                    sp.wait_ge(dense_out[c % 2], slot_writes(b, c) + 16)
                    sp.sem_inc(sp_steps, 1)
            if units is not None:
                sp.wait_ge(sct_full, units + 4 * half + 4 + 1)
            par = q % 2
            heads = slice(2 * half, 2 * half + 2)
            for dst, first, parts in ((qs[par], 0, (0, 1, 0)), (ks[par], QW, (0, 0, 1))):
                at = 2 * QW * q + first + 2 * half * HD
                for n, part in enumerate(parts):
                    sp.dma_start(f32(dst[n * HD:(n + 1) * HD, heads, :]),
                                 qk_scr[b, part, at:at + 2 * HD, :].rearrange("(i r) t -> r i t", r=HD)
                                 ).then_inc(stack_in[par][half], 16)

        def load_neg(count, q):
            sp.wait_ge(neg_done, count)
            for n in range(2):
                sp.dma_start(f32(qs[q % 2][3 * HD + n:3 * HD + n + 1, :, :]), f32(negmax[:, n, :])
                             ).then_inc(rows_in[q % 2], 16)

        def load_x(b, done):
            for t in range(NT):
                sp.dma_start(xt[:, t, 0:D], x[b, t * P:(t + 1) * P, :]).then_inc(done, 16)

        def load_piece(n):
            if n > 0:
                sp.wait_ge(sems_b["w_hi"], n)
                sp.wait_ge(sems_b["w_lo"], n)
            raw_in = sems_b["raw"]
            if n < 4:
                sp.dma_start(raw_b[:, :], w1[n * P:(n + 1) * P, :]).then_inc(raw_in, 16)
            elif n == 4:
                sp.dma_start(raw_b[0:TAIL, :], w1[4 * P:D, :]).then_inc(raw_in, 16)
                sp.dma_start(raw_b[TAIL:P, :], w1[4 * P:D, :]).then_inc(raw_in, 16)
            else:
                j = 4 * (n - 5)
                m = min(4, NJ - j)
                sp.dma_start(raw_b[:, 0:m * D].rearrange("p (j n) -> p j n", n=D),
                             w2[j * P:(j + m) * P, :].rearrange("(j p) n -> p j n", p=P)).then_inc(raw_in, 16)

        def load_x1(b):
            for t in range(NT):
                sp.dma_start(xn[:, t, 0:D], x1[b, t * P:(t + 1) * P, :]).then_inc(sems_b["xn_in"], 16)
            gather_mod(sp, 3, b, sems_b["modt_in"])

        for s in dense_out:
            sp.sem_inc(s, 16)
        sp.sem_inc(x1_out, 16)
        load_rows(sp, cond_sb, cond_t, s_cond_in)
        load_rows(sp, raw[0], ada_w[:, 0:D], s_ada[0])
        sp.dma_start(adab_sb[:, :, :].rearrange("p s d -> p (s d)"), ada_b.partition_broadcast(B)).then_inc(s_adab, 16)
        load_rows(sp, raw[1], ada_w[:, D:2 * D], s_ada[1])
        load_x(0, xn_in)
        for i in range(2):
            load_rows(sp, raw[2 + i], wqk[:, i * D:(i + 1) * D], s_rawk[i])
        sp.dma_start(bqk_sb[:, :], bqk).then_inc(s_small, 16)
        sp.dma_start(b1_sb[:, :], b1).then_inc(s_small, 16)
        sp.dma_start(bv_sb[:, 0:4], bv[0:4 * P].rearrange("(k p) -> p k", p=P)).then_inc(s_small, 16)
        sp.dma_start(bv_sb[0:TAIL, 4:5], bv[4 * P:D].rearrange("(p o) -> p o", o=1)).then_inc(s_small, 16)
        sp.dma_start(bo_row[:, :], bo.rearrange("(o n) -> o n", o=1)).then_inc(s_small, 16)

        def next_section(s):
            sp.wait_ge(s_mod_row, 2 * s + 2)
            sp.dma_start(mods[s], mod_row[:, s % 2, :]).then_inc(s_mod_out[s % 2], 16)
            if s == 1:
                for i in range(2):
                    sp.wait_ge(s_mod_out[i], 16)
                gather_mod(sp, 0, 0, modt_in)
            if s + 2 < 6:
                load_rows(sp, raw[s % 2], ada_w[:, (s + 2) * D:(s + 3) * D], s_ada[s % 2])

        next_section(0)
        next_section(1)
        for i, w in enumerate((wv, wo)):
            sp.wait_ge(s_w_hi, i + 1)
            sp.wait_ge(s_w_lo, 2 * i + 2)
            load_rows(sp, raw[2 + i], w, s_rawk[2 + i])
        next_section(2)
        for c in range(3):
            write_chunk(0, c)
        for s in range(3, 6):
            next_section(s)
        sp.wait_ge(s_bo_done, 2)
        sp.dma_start(bias_o.rearrange("(o n) -> o n", o=1), bo_row[:, :]).then_inc(s_bo_out, 16)
        sp.wait_ge(s_bo_out, 16)
        sp.wait_ge(s_const, 11)
        load_stack(0, 0, 0)
        load_stack(0, 0, 1)
        for c in range(3, 5):
            write_chunk(0, c)
        sp.wait_ge(s_const, 12)
        load_stack(0, 1, 0)
        load_stack(0, 1, 1)
        for c in range(5, NC - 2):
            write_chunk(0, c)
        load_neg(1, 0)
        write_chunk(0, NC - 2)

        def body(b, has_next):
            if has_next:
                sp.wait_ge(x1_out, b * 64 + 16)
                load_x(b + 1, xn_in)
                sp.wait_ge(y_done, b * NK + NK)
                gather_mod(sp, 0, b + 1, modt_in)
            write_chunk(b, NC - 1)
            if not has_next:
                for i in range(2):
                    sp.wait_ge(dense_out[i], slot_writes(b, NC - 1 - i) + 16)
                load_piece(0)
            load_stack(b, 2, 0, b * UN)
            load_neg(b * NQ + 2, 1)
            load_stack(b, 2, 1, b * UN)
            if has_next:
                sp.wait_ge(mm_full, body_uses(b, has_next).full(("T", NK - 1)))
            sp.wait_ge(x1_out, b * 64 + 16)
            load_x(b, xr_in)
            sp.dma_start(m2_sb[:, :], mods[2, b].partition_broadcast(P)).then_inc(m2_in, 16)
            sp.dma_start(c2_sb[:, :], bias_o.partition_broadcast(P)).then_inc(m2_in, 16)
            if not has_next:
                load_piece(1)
            load_stack(b, 3, 0, b * UN + 8)
            if has_next:
                write_chunk(b + 1, 0)
            load_neg(b * NQ + 3, 2)
            if has_next:
                write_chunk(b + 1, 1)
            load_stack(b, 3, 1, b * UN + 8)
            if has_next:
                write_chunk(b + 1, 2)
                load_stack(b + 1, 0, 0, b * UN + 16)
                write_chunk(b + 1, 3)
            else:
                load_piece(2)
            load_neg(b * NQ + 4, 3)
            if has_next:
                load_stack(b + 1, 0, 1, b * UN + 16)
                write_chunk(b + 1, 4)
                write_chunk(b + 1, 5)
                load_stack(b + 1, 1, 0, b * UN + 24)
                load_neg(b * NQ + 5, 0)
                write_chunk(b + 1, 6)
                load_stack(b + 1, 1, 1, b * UN + 24)
                write_chunk(b + 1, 7)
            else:
                load_piece(3)
                sp.wait_ge(sct_full, b * UN + 24 + 1)
                load_x1(0)
                for n in range(4, 7):
                    load_piece(n)
            for t in range(NT):
                sp.wait_ge(r_add, b * NT + t + 2)
                sp.dma_start(x1[b, t * P:(t + 1) * P, :], xt[:, t, 0:D]).then_inc(x1_out, 16)

        with sp.Fori(0, B - 1) as b:
            body(b, True)
        body(B - 1, False)
        sp.wait_ge(x1_out, 64 * B + 16)

        s = sems_b
        sp.wait_ge(a_over, 4)
        sp.wait_ge(s["z_done"], NK)
        load_x1(1)
        for n in range(7, 10):
            load_piece(n)
        sp.wait_ge(s["w_hi"], 10)
        sp.wait_ge(s["w_lo"], 10)

        def body_b(b, has_next):
            sp.wait_ge(s["out"], b * 64 + 16)
            sp.dma_start(m5_sb[:, :], mods[5, b].partition_broadcast(P)).then_inc(s["m5_in"], 16)
            sp.dma_start(c5_sb[:, :], b2.partition_broadcast(P)).then_inc(s["m5_in"], 16)
            for t in range(NT):
                sp.dma_start(xr[:, t, :], x1[b, t * P:(t + 1) * P, :]).then_inc(s["xr_in"], 16)
            if has_next and not (isinstance(b, int) and b == 0):
                sp.wait_ge(s["z_done"], b * NK + NK)
                load_x1(b + 1)
            for t in range(NT):
                sp.wait_ge(s["o_add"], b * NT + t + 2)
                sp.dma_start(out[b, t * P:(t + 1) * P, :], xr[:, t, :]).then_inc(s["out"], 16)

        sp.sem_inc(s["out"], 16)
        body_b(0, True)
        with sp.Fori(1, B - 1) as b:
            body_b(b, True)
        body_b(B - 1, False)
        sp.wait_ge(s["out"], 64 * B + 16)

    @block.gpsimd
    def _(pool):
        def inverse_deviation(count, var_sem, done):
            pool.wait_ge(var_sem, NT * count)
            pool.tensor_tensor(rstd[:, :], moments[:, :, 1], eps_half[:, 0, :], ALU.add).then_inc(done, 1)
            pool.wait_ge(done, 2 * count - 1)
            pool.tensor_tensor(rstd[:, :], rstd[:, :], eps_half[:, 1, :], ALU.pow).then_inc(done, 1)

        for n, (m, v) in enumerate(((ident[:, :], 0.0), (nident[:, :], 0.0), (merge_f[:, :], 0.0),
                                    (eps_half[:, 0, :], EPS), (eps_half[:, 1, :], -0.5))):
            if n:
                pool.wait_ge(s_const, n)
            pool.memset(m, v).then_inc(s_const, 1)
        for n, (m, fill) in enumerate(((ident, 1.0), (nident, -1.0))):
            pool.wait_ge(s_const, 5 + n)
            pool.affine_select(out=m[:, :], in_=m[:, :], compare_op=ALU.not_equal, fill=fill,
                               base=0, pattern=[[-1, P]], channel_multiplier=1).then_inc(s_const, 1)
        pool.wait_ge(s_const, 7)
        pool.affine_select(out=merge_f[:, 0:HD], in_=merge_f[:, 0:HD], compare_op=ALU.not_equal, fill=1.0,
                           base=0, pattern=[[-1, HD]], channel_multiplier=1).then_inc(s_const, 1)
        pool.wait_ge(s_const, 8)
        pool.affine_select(out=merge_f[:, :], in_=merge_f[:, :], compare_op=ALU.not_equal, fill=1.0,
                           base=-HD, pattern=[[-1, MW]], channel_multiplier=1).then_inc(s_const, 1)
        inverse_deviation(1, var_done, rstd_done)
        pool.wait_ge(s_w_hi, 4)
        pool.wait_ge(s_w_lo, 8)
        pool.wait_ge(s_mod_full, 12)
        pool.wait_ge(s_bo_full, 2)
        for i in range(2):
            pool.wait_ge(s_const, 10 + i)
            pool.memset(f32(ks[i][96:3 * HD + 2, :, :]), 1.0).then_inc(s_const, 1)
        pool.wait_ge(s_const, 12)
        for i in range(2):
            pool.wait_ge(s_mod_out[i], 48)
        pool.memset(f32(v_sb[:, :, :, VW - 1:VW]), 1.0).then_inc(s_const, 1)

        pool.sem_inc(r_add, 1)

        def body(b, has_next):
            for h in range(H):
                pool.wait_ge(ehi_done, b * UN + 2 * h + 2)
                pool.tensor_tensor(e_lo[:, 1, T:], e_f[:, 1, T:], f32(e_hi[:, 1, T:]), ALU.subtract
                                   ).then_inc(elo_pool, 1)
                if h == 2 and has_next:
                    inverse_deviation(b + 2, var_done, rstd_done)
                if h == 13 and not has_next:
                    inverse_deviation(1, sems_b["var_done"], sems_b["rstd_done"])
                pool.wait_ge(pvhi_done, b * H + h + 1)
                pool.tensor_tensor(pv_lo[:, h % 2, :], pv_f[:, h % 2, :], f32(pv_hi[:, h % 2, :]), ALU.subtract
                                   ).then_inc(pvlo_done, 1)
                if h == H // 2 + 2:
                    pool.wait_ge(m2_in, b * 32 + 32)
                    pool.tensor_tensor(c2_sb[:, :], c2_sb[:, :], m2_sb[:, :], ALU.mult).then_inc(c2_done, 1)
                    pool.wait_ge(c2_done, b * (NT + 1) + 1)
                    pool.wait_ge(xr_in, b * 64 + 64)
                if H // 2 + 2 <= h < H // 2 + 2 + NT:
                    t = h - H // 2 - 2
                    pool.tensor_tensor(xt[:, t, 0:D], xt[:, t, 0:D], c2_sb[:, :], ALU.add).then_inc(c2_done, 1)
            for t in range(NT):
                if t == 0:
                    pool.wait_ge(c2_done, b * (NT + 1) + NT + 1)
                pool.wait_ge(yb_done, b * 2 * NT + 2 * t + 3)
                pool.tensor_tensor(xt[:, t, 0:D], xt[:, t, 0:D], resid_tmp[:, :], ALU.add).then_inc(r_add, 1)

        with pool.Fori(0, B - 1) as b:
            body(b, True)
        body(B - 1, False)
        pool.wait_ge(r_add, NT * B + 1)
        pool.sem_inc(a_over, 1)

        s = sems_b
        def body_b(b, has_next):
            if has_next:
                inverse_deviation(b + 2, s["var_done"], s["rstd_done"])
            pool.wait_ge(s["m5_in"], b * 32 + 32)
            pool.tensor_tensor(c5_sb[:, :], c5_sb[:, :], m5_sb[:, :], ALU.mult).then_inc(s["c5_done"], 1)
            pool.wait_ge(s["c5_done"], b * (NT + 1) + 1)
            pool.wait_ge(s["xr_in"], b * 64 + 64)
            for t in range(NT):
                pool.tensor_tensor(xr[:, t, :], xr[:, t, :], c5_sb[:, :], ALU.add).then_inc(s["c5_done"], 1)

        body_b(0, True)
        with pool.Fori(1, B - 1) as b:
            body_b(b, True)
        body_b(B - 1, False)

    @block.scalar
    def _(act):
        def chunk_hi(b, c, uses):
            act.wait_ge(mm_full, uses.full(("P", c)))
            act.wait_ge(dense_out[c % 2], slot_writes(b, c))
            act.activation(dense[:, c % 2, 0, :], mm[uses.bank(("P", c))][:, :], ACT.Identity,
                           bias=bqk_sb[:, c:c + 1]).then_inc(p_hi, 1)

        def v_high(half, t, uses):
            act.wait_ge(mm_full, uses.full(("V", half, t)))
            hd = H // 2
            act.activation(v_sb[:, t, half * hd:(half + 1) * hd, 0:HD],
                           mm[uses.bank(("V", half, t))][:, 0:HALF].rearrange("p (h d) -> p h d", d=HD),
                           ACT.Copy).then_inc(vhi_done, 1)

        def modulate(b, k, uses):
            act.wait_ge(mm_full, uses.full(("T", k)))
            if k == 0:
                act.wait_ge(modt_in, b * 64 + 64)
            if k >= 2:
                act.wait_ge(y_done, b * NK + k - 1)
            act.activation(y_tmp[:, k % 2, :], mm[uses.bank(("T", k))][:, :], ACT.Identity,
                           bias=modt[:, 0, k:k + 1], scale=modt[:, 1, k:k + 1]).then_inc(ytmp_done, 1)
            act.wait_ge(ytmp_done, b * NK + k + 1)
            act.activation(y_hi[:, k, :], y_tmp[:, k % 2, :], ACT.Copy).then_inc(yhi_done, 1)

        act.wait_ge(s_cond_in, 48)
        act.activation(cond_e[:, :, :], cond_sb[:, :, :], ACT.Exp, scale=-1.0).then_inc(s_cond, 1)
        def weights_high(n):
            dst, col = ((wqk_hi, 0), (wqk_hi, D), (wv_hi, 0), (wo_hi, 0))[n]
            act.wait_ge(s_rawk[n], 48)
            act.activation(dst[:, :, col:col + D], raw[2 + n % 2][:, :, :], ACT.Copy).then_inc(s_w_hi, 1)

        weights_high(0)
        weights_high(1)
        pro = Uses(0, PROLOGUE)
        for k in range(NK):
            modulate(0, k, pro)
        act.wait_ge(s_small, 80)
        for c in range(3):
            chunk_hi(0, c, pro)
        weights_high(2)
        weights_high(3)
        act.wait_ge(s_const, 9)
        act.activation(merge[:, :], merge_f[:, :], ACT.Copy).then_inc(s_const, 1)
        for c in range(3, NC - 2):
            chunk_hi(0, c, pro)
        act.wait_ge(s_const, 13)
        for half, t in V_FIRST:
            v_high(half, t, pro)
        act.wait_ge(mm_full, pro.full(("M", 0)))
        act.activation(negmax[:, 0, :], mm[pro.bank(("M", 0))][0:HQ, :], ACT.Copy).then_inc(neg_hi, 1)
        chunk_hi(0, NC - 2, pro)
        act.sem_inc(sct_free, 1)

        def head_out(b, h):
            act.wait_ge(pv_done, b * UN + 2 * h + 4)
            if h >= 2:
                act.wait_ge(o_full, b * H + h - 1)
            act.activation(pv_f[:, h % 2, :], pv[h % 2][0:VW, :], ACT.Copy)
            act.activation(pv_hi[:, h % 2, :], pv[h % 2][0:VW, :], ACT.Copy).then_inc(pvhi_done, 1)

        def modulate_b(b, k, full):
            act.wait_ge(sems_b["mm_full"], full)
            if k == 0:
                act.wait_ge(sems_b["modt_in"], b * 64 + 64)
            if k >= 2:
                act.wait_ge(sems_b["z_done"], b * NK + k - 1)
            elif not (isinstance(b, int) and b == 0):
                act.wait_ge(sems_b["h_done"], b * NJ + k - 1)
            act.activation(g_f[:, k % 2, :], mm[T_BANK[k]][:, :], ACT.Identity, bias=modt[:, 0, k:k + 1],
                           scale=modt[:, 1, k:k + 1]).then_inc(sems_b["ztmp_done"], 1)
            act.wait_ge(sems_b["ztmp_done"], b * NK + k + 1)
            act.activation(z_hi[:, k, :], g_f[:, k % 2, :], ACT.Copy).then_inc(sems_b["zhi_done"], 1)

        def piece_high(n):
            act.wait_ge(sems_b["raw"], 16 * (n + 1 + (n >= 4)))
            if n < 5:
                act.activation(w1_hi[:, n, :], raw_b[:, :], ACT.Copy).then_inc(sems_b["w_hi"], 1)
            elif n < 9:
                act.activation(w2_pieces[n - 5][:, :, 0, :], raw_b[:, :].rearrange("p (j n) -> p j n", n=D),
                               ACT.Copy).then_inc(sems_b["w_hi"], 1)
            else:
                act.activation(w2_part(NJ - 2, 0), raw_b[:, 0:D], ACT.Copy)
                act.activation(w2_part(NJ - 1, 0), raw_b[:, D:2 * D], ACT.Copy).then_inc(sems_b["w_hi"], 1)

        def body(b, has_next):
            uses = body_uses(b, has_next)
            for unit in range(UN):
                n = b * UN + unit
                act.wait_ge(sct_full, n + 2)
                act.wait_ge(pv_done, n + 1)
                act.activation(e_f[:, unit % 2, :].rearrange("p (k t) -> p k t", k=2), sct[:, :, :],
                               ACT.Exp, scale=SCALE).then_inc(sct_free, 1)
                for job in JOBS[has_next][unit]:
                    if job[0] == "M":
                        q = job[1]
                        act.wait_ge(mm_full, uses.full(job))
                        before = (q - 1) % NQ
                        act.wait_ge(rows_in[before % 2], b * 64 + 32 * (before // 2) + 32)
                        act.activation(negmax[:, 0, :], mm[uses.bank(job)][0:HQ, :], ACT.Copy).then_inc(neg_hi, 1)
                act.wait_ge(sct_free, n + 2)
                act.activation(e_hi[:, unit % 2, :], e_f[:, unit % 2, :], ACT.Copy).then_inc(ehi_done, 1)
                for job in JOBS[has_next][unit]:
                    if job[0] == "P":
                        chunk_hi(p_batch(uses, job[1]), job[1], uses)
                    elif job[0] == "V":
                        v_high(job[1], job[2], uses)
                    elif job[0] == "T":
                        modulate(b + 1, job[1], uses)
                if unit % 2 == 0 and unit >= 2:
                    head_out(b, unit // 2 - 1)
                if not has_next and unit in PIECE_UNITS:
                    piece_high(PIECE_UNITS.index(unit))
            if has_next:
                chunk_hi(b + 1, 7, uses)
            head_out(b, H - 1)
            if has_next:
                v_high(1, 0, uses)
            else:
                for k in range(NK):
                    modulate_b(0, k, k + 1)
                piece_high(5)
            for t in range(NT):
                if t == 2 and has_next:
                    v_high(1, 1, uses)
                for n, (lo, hi) in enumerate(((0, 4), (4, 5))):
                    act.wait_ge(x_full, b * 2 * NT + 2 * t + n + 1)
                    if t >= 2 and n == 0:
                        act.wait_ge(mm_full, uses.full(("Y", t - 2, 1)))
                    act.activation(at_hi[:, t % 2, lo:hi, :], at_psum(t, n).rearrange("p (k t) -> p k t", t=P),
                                   ACT.Copy).then_inc(at_hi_done, 1)

        with act.Fori(0, B - 1) as b:
            body(b, True)
        body(B - 1, False)
        act.wait_ge(at_hi_done, 2 * NT * B)
        act.sem_inc(a_over, 1)

        s = sems_b
        def body_b(b, has_next):
            for j in range(NJ):
                act.wait_ge(s["mm_full"], b * (NK + NJ) + NK + j + 1)
                if j >= 2:
                    act.wait_ge(s["m2_done"], b * NJ + j - 1)
                act.activation(g_f[:, j % 2, :], mm[(j + 1) % 2][:, :], ACT.Gelu_apprx_tanh,
                               bias=b1_sb[:, j:j + 1]).then_inc(s["g_done"], 1)
                act.wait_ge(s["g_done"], b * NJ + j + 2)
                act.activation(h_hi[:, j % 2, :], g_f[:, j % 2, :], ACT.Copy).then_inc(s["hhi_done"], 1)
                if isinstance(b, int) and b == 0 and j in PIECE_CHUNKS:
                    piece_high(6 + PIECE_CHUNKS.index(j))
            if has_next:
                for k in range(NK):
                    modulate_b(b + 1, k, (b + 1) * (NK + NJ) + k + 1)

        act.sem_inc(s["g_done"], 1)
        act.wait_ge(a_over, 4)
        act.wait_ge(x1_out, 64 * B + 16)
        body_b(0, True)
        with act.Fori(1, B - 1) as b:
            body_b(b, True)
        body_b(B - 1, False)

    @block.vector
    def _(dve):
        def moments_of(b, tile_in, in_sem, ch, done, t):
            if t == 0:
                dve.wait_ge(in_sem, b * 64 + 64)
            dve.bn_stats(stats[:, t, 0, :], tile_in[:, t, 0:HALF]).then_inc(ch, 1)
            dve.bn_stats(stats[:, t, 1, :], tile_in[:, t, HALF:D]).then_inc(ch, 1)
            dve.wait_ge(ch, b * 3 * NT + 3 * t + 2)
            dve.sem_inc(ch, 1)
            dve.bn_aggr(moments[:, t, :], stats[:, t, :, :]).then_inc(done, 1)

        def normalise(b, tile, rs, sc, done, t):
            if t == 0:
                dve.wait_ge(rs, b * 2 + 2)
            dve.tensor_scalar(tile[:, t, 0:D], tile[:, t, 0:D], moments[:, t, 0:1], rstd[:, t:t + 1],
                              ALU.subtract, ALU.mult).then_inc(sc, 1)
            dve.wait_ge(sc, b * NT + t + 1)
            dve.tensor_copy(tile[:, t, D:DP], tile[:, t, 4 * P:D]).then_inc(done, 1)

        def y_low(b, k):
            dve.wait_ge(yhi_done, b * NK + k + 1)
            dve.tensor_tensor(y_lo[:, k, :], y_tmp[:, k % 2, :], f32(y_hi[:, k, :]), ALU.subtract
                              ).then_inc(y_done, 1)

        def chunk_low(b, c, uses):
            dve.wait_ge(p_hi, b * NC + c + 1)
            bank = uses.bank(("P", c))
            dve.scalar_tensor_tensor(dense[:, c % 2, 1, :], mm[bank][:, :], bqk_sb[:, c:c + 1],
                                     f32(dense[:, c % 2, 0, :]), ALU.add, ALU.subtract).then_inc(p_done, 1)

        def v_low(half, t, uses):
            dve.wait_ge(vhi_done, v_count(uses, half, t) + 1)
            heads = slice(half * H // 2, (half + 1) * H // 2)
            dve.tensor_tensor(v_sb[:, t, heads, HD:2 * HD],
                              mm[uses.bank(("V", half, t))][:, 0:HALF].rearrange("p (h d) -> p h d", d=HD),
                              f32(v_sb[:, t, heads, 0:HD]), ALU.subtract).then_inc(v_done, 1)

        def max_of(n, q, tile):
            dve.wait_ge(scs_full, n + 1)
            i, t = divmod(tile, NT)
            dve.tensor_reduce(rowmax[:, t, q * HQ + i:q * HQ + i + 1], scs[:, tile % 2, :], AX_X, ALU.max
                              ).then_inc(scs_free, 1)

        def neg_low(count, q, uses):
            bank = uses.bank(("M", q))
            dve.wait_ge(neg_hi, count)
            dve.tensor_tensor(negmax[:, 1, :], mm[bank][0:HQ, :], f32(negmax[:, 0, :]), ALU.subtract
                              ).then_inc(neg_done, 1)

        dve.sem_inc(yb_done, 1)
        dve.wait_ge(s_cond, 1)
        dve.tensor_scalar(cond_e[:, :, :], cond_e[:, :, :], 1.0, None, ALU.add).then_inc(s_cond, 1)
        dve.wait_ge(s_cond, 2)
        dve.reciprocal(cond_e[:, :, :], cond_e[:, :, :]).then_inc(s_cond, 1)
        dve.wait_ge(s_cond, 3)
        dve.tensor_tensor(cond_s[:, :, :], cond_sb[:, :, :], cond_e[:, :, :], ALU.mult).then_inc(s_cond, 1)

        def mod_half(s, half):
            n = 2 * s + half
            dve.wait_ge(s_mod_full, n + 1)
            if s >= 2 and half == 0:
                dve.wait_ge(s_mod_out[s % 2], 16 * (s // 2))
            cols = slice(half * HALF, (half + 1) * HALF)
            one = 1.0 if s in (1, 4) else 0.0
            dve.scalar_tensor_tensor(mod_row[:, s % 2, cols], scs[0:B, half, 0:HALF], one,
                                     adab_sb[:, s, cols], ALU.add, ALU.add).then_inc(s_mod_row, 1)

        def weights_low(n):
            dst, hi, col = ((wqk_lo, wqk_hi, 0), (wqk_lo, wqk_hi, D), (wv_lo, wv_hi, 0), (wo_lo, wo_hi, 0))[n]
            r = raw[2 + n % 2]
            dve.wait_ge(s_w_hi, n + 1)
            dve.tensor_tensor(dst[:, :, col:col + D], r[:, 0:4, :], f32(hi[:, 0:4, col:col + D]), ALU.subtract
                              ).then_inc(s_w_lo, 1)
            dve.tensor_tensor(hi[TAIL:P, 4, col:col + D], r[TAIL:P, 4, :], f32(hi[TAIL:P, 4, col:col + D]),
                              ALU.subtract).then_inc(s_w_lo, 1)

        pro = Uses(0, PROLOGUE)
        dve.wait_ge(s_adab, 16)
        mod_half(0, 0)
        mod_half(0, 1)
        for t in range(NT):
            moments_of(0, xt, xn_in, chain, var_done, t)
        mod_half(1, 0)
        mod_half(1, 1)
        for t in range(NT):
            normalise(0, xt, rstd_done, scaled, xhat_done, t)
        weights_low(0)
        weights_low(1)
        for k in range(NK):
            y_low(0, k)
        mod_half(2, 0)
        mod_half(2, 1)
        for c in range(3):
            chunk_low(0, c, pro)
        weights_low(2)
        weights_low(3)
        mod_half(3, 0)
        mod_half(3, 1)
        dve.wait_ge(s_small, 80)
        for half in range(2):
            cols = slice(half * HALF, (half + 1) * HALF)
            dve.wait_ge(s_bo_full, half + 1)
            dve.tensor_tensor(bo_row[:, cols], pv[half][0:1, 0:HALF], bo_row[:, cols], ALU.add).then_inc(s_bo_done, 1)
        for s in (4, 5):
            mod_half(s, 0)
            mod_half(s, 1)
        for c in range(3, NC - 2):
            chunk_low(0, c, pro)
        dve.wait_ge(s_const, 13)
        for i, (half, t) in enumerate(V_FIRST):
            v_low(half, t, pro)
            for n in range(SCORES_WITH_V * i, min(SCORES_WITH_V * (i + 1), N_SCORE)):
                max_of(n, 0, n)
        neg_low(1, 0, pro)
        chunk_low(0, NC - 2, pro)

        def norm(b, h):
            dve.wait_ge(o_full, b * H + h + 1)
            src = pv[h % 2][:, 0:NT * 64].rearrange("p (t c) -> p t c", c=64)
            dve.reciprocal(rden[:, h % 4, :, :], src[:, :, HD:HD + 1]).then_inc(rden_done, 1)
            dve.wait_ge(rden_done, b * H + h + 1)
            dve.tensor_tensor(attn[:, :, h * HD:(h + 1) * HD], src[:, :, 0:HD],
                              rden[:, h % 4, :, :].to_broadcast([P, NT, HD]), ALU.mult).then_inc(o_done, 1)

        def piece_low(n):
            dve.wait_ge(sems_b["w_hi"], n + 1)
            if n < 4:
                dve.tensor_tensor(w1_lo[:, n, :], raw_b[:, :], f32(w1_hi[:, n, :]), ALU.subtract
                                  ).then_inc(sems_b["w_lo"], 1)
            elif n == 4:
                dve.tensor_tensor(w1_hi[TAIL:P, 4, :], raw_b[TAIL:P, :], f32(w1_hi[TAIL:P, 4, :]),
                                  ALU.subtract).then_inc(sems_b["w_lo"], 1)
            elif n < 9:
                w = w2_pieces[n - 5]
                dve.tensor_tensor(w[:, :, 1, :], raw_b[:, :].rearrange("p (j n) -> p j n", n=D),
                                  f32(w[:, :, 0, :]), ALU.subtract).then_inc(sems_b["w_lo"], 1)
            else:
                for i in range(2):
                    last = dve.tensor_tensor(w2_part(NJ - 2 + i, 1), raw_b[:, i * D:(i + 1) * D],
                                             f32(w2_part(NJ - 2 + i, 0)), ALU.subtract)
                last.then_inc(sems_b["w_lo"], 1)

        def moments_b(b, t):
            moments_of(b, xn, sems_b["xn_in"], sems_b["chain"], sems_b["var_done"], t)

        def normalise_b(b, t):
            normalise(b, xn, sems_b["rstd_done"], sems_b["scaled"], sems_b["xhat_done"], t)

        def z_low(b, k):
            dve.wait_ge(sems_b["zhi_done"], b * NK + k + 1)
            dve.tensor_tensor(z_lo[:, k, :], g_f[:, k % 2, :], f32(z_hi[:, k, :]), ALU.subtract
                              ).then_inc(sems_b["z_done"], 1)

        def body(b, has_next):
            uses = body_uses(b, has_next)
            for unit in range(UN):
                q, u = divmod(unit, 8)
                n = b * UN + unit
                tiles = SCORE_TILES.get(u, ()) if q < 3 or has_next else ()
                sn = (b * NQ + q + 1) * N_SCORE
                for tile in tiles[:1]:
                    max_of(sn + tile, (q + 1) % NQ, tile)
                if unit % 2 == 0 and unit >= 4:
                    norm(b, unit // 2 - 2)
                for tile in tiles[1:2]:
                    max_of(sn + tile, (q + 1) % NQ, tile)
                if ("M", (q + 1) % NQ) in JOBS[has_next][unit]:
                    neg_low(b * NQ + q + 2, (q + 1) % NQ, uses)
                dve.wait_ge(ehi_done, n + 1)
                cols = slice(0, T if unit % 2 else 2 * T)
                dve.tensor_tensor(e_lo[:, unit % 2, cols], e_f[:, unit % 2, cols], f32(e_hi[:, unit % 2, cols]),
                                  ALU.subtract).then_inc(elo_done, 1)
                for job in JOBS[has_next][unit]:
                    if job[0] == "P":
                        chunk_low(p_batch(uses, job[1]), job[1], uses)
                    elif job[0] == "V":
                        v_low(job[1], job[2], uses)
                    elif job[0] == "T":
                        y_low(b + 1, job[1])
                for tile in tiles[2:]:
                    max_of(sn + tile, (q + 1) % NQ, tile)
                if has_next:
                    for t in {3: (0, 1), 5: (2, 3)}.get(unit, ()):
                        moments_of(b + 1, xt, xn_in, chain, var_done, t)
                    for t in {6: (0, 1), 7: (2, 3)}.get(unit, ()):
                        normalise(b + 1, xt, rstd_done, scaled, xhat_done, t)
                else:
                    if unit in PIECE_UNITS:
                        piece_low(PIECE_UNITS.index(unit))
                    for t in {26: (0, 1), 27: (2, 3)}.get(unit, ()):
                        moments_b(0, t)
                    for t in {29: (0, 1), 30: (2, 3)}.get(unit, ()):
                        normalise_b(0, t)
            if has_next:
                chunk_low(b + 1, 7, uses)
            norm(b, H - 2)
            if has_next:
                v_low(1, 0, uses)
            else:
                for k in range(NK):
                    z_low(0, k)
            norm(b, H - 1)
            dve.wait_ge(o_done, b * (H + 1) + H)
            dve.tensor_copy(attn[:, :, D:DP], attn[:, :, 4 * P:D]).then_inc(o_done, 1)
            if not has_next:
                piece_low(5)

            def transposed_low(t):
                for n, (lo, hi) in enumerate(((0, 4), (4, 5))):
                    dve.wait_ge(at_hi_done, b * 2 * NT + 2 * t + n + 1)
                    dve.tensor_tensor(at_lo[:, t % 2, lo:hi, :], at_psum(t, n).rearrange("p (k t) -> p k t", t=P),
                                      f32(at_hi[:, t % 2, lo:hi, :]), ALU.subtract).then_inc(at_done, 1)

            def times_m2(t):
                for half in range(2):
                    bank = uses.bank(("Y", t, half))
                    cols = slice(half * HALF, (half + 1) * HALF)
                    dve.wait_ge(mm_full, uses.full(("Y", t, half)))
                    if half == 0:
                        dve.wait_ge(r_add, b * NT + t + 1)
                    if t == 0 and half == 0:
                        dve.wait_ge(m2_in, b * 32 + 32)
                    dve.tensor_tensor(resid_tmp[:, cols], mm[bank][:, 0:HALF], m2_sb[:, cols], ALU.mult
                                      ).then_inc(yb_done, 1)

            transposed_low(0)
            transposed_low(1)
            if has_next:
                v_low(1, 1, uses)
            for t in range(NT):
                times_m2(t)
                if t + 2 < NT:
                    transposed_low(t + 2)

        with dve.Fori(0, B - 1) as b:
            body(b, True)
        body(B - 1, False)
        dve.wait_ge(yb_done, 2 * NT * B + 1)
        dve.sem_inc(a_over, 1)

        s = sems_b
        dve.sem_inc(s["yo_done"], 1)
        dve.sem_inc(s["o_add"], 1)
        def hidden_low(b, j):
            dve.wait_ge(s["hhi_done"], b * NJ + j + 1)
            dve.tensor_tensor(h_lo[:, j % 2, :], g_f[:, j % 2, :], f32(h_hi[:, j % 2, :]), ALU.subtract
                              ).then_inc(s["h_done"], 1)

        def add_sums(b, t):
            if t == 0:
                dve.wait_ge(s["m2_done"], b * NJ + NJ)
                dve.wait_ge(s["c5_done"], b * (NT + 1) + NT + 1)
            dve.wait_ge(s["o_add"], b * NT + t + 1)
            pair = y_pair[t // 2][:, YA * (t % 2):YA * (t % 2) + YA]
            dve.tensor_tensor(y_out[:, 0:YA], pair, m5_sb[:, 0:YA], ALU.mult).then_inc(s["yo_done"], 1)
            dve.tensor_tensor(y_out[:, YA:D], y_own[t][:, 0:YB], m5_sb[:, YA:D], ALU.mult
                              ).then_inc(s["yo_done"], 1)
            dve.wait_ge(s["yo_done"], b * 2 * NT + 2 * t + 3)
            dve.tensor_tensor(xr[:, t, :], xr[:, t, :], y_out[:, :], ALU.add).then_inc(s["o_add"], 1)

        def body_b(b, has_next):
            for j in range(NJ):
                hidden_low(b, j)
                if isinstance(b, int) and b == 0 and j in PIECE_CHUNKS:
                    piece_low(6 + PIECE_CHUNKS.index(j))
                if has_next and j in (6, 7):
                    for t in (2 * j - 12, 2 * j - 11):
                        moments_b(b + 1, t)
                if has_next and j in (10, 11):
                    for t in (2 * j - 20, 2 * j - 19):
                        normalise_b(b + 1, t)
            if has_next:
                for k in range(4):
                    z_low(b + 1, k)
            add_sums(b, 0)
            add_sums(b, 1)
            if has_next:
                z_low(b + 1, 4)
            add_sums(b, 2)
            add_sums(b, 3)

        body_b(0, True)
        with dve.Fori(1, B - 1) as b:
            body_b(b, True)
        body_b(B - 1, False)

    @block.tensor
    def _(pe):
        def bank_free(uses, job):
            b, last = uses.b, uses.before(job)
            if last is None:
                if uses.jobs is not PROLOGUE:
                    pe.wait_ge(yb_done, b * 2 * NT + 1)
                return
            kind, n = last[0], last[1]
            prologue = uses.jobs is PROLOGUE
            if kind == "T":
                pe.wait_ge(ytmp_done, (0 if prologue else b + 1) * NK + n + 1)
            elif kind == "P":
                pe.wait_ge(p_done, p_batch(uses, n) * NC + n + 1)
            elif kind == "V":
                pe.wait_ge(v_done, v_count(uses, n, last[2]) + 1)
            elif kind == "M":
                pe.wait_ge(neg_done, 1 if prologue else b * NQ + (n - 1) % NQ + 2)
            else:
                pe.wait_ge(yb_done, b * 2 * NT + 2 * n + last[2] + 2)

        def split_product(acc, w_hi, w_lo, y_h, y_l, chunks=range(NK), before=None):
            for k in chunks:
                if before is not None:
                    before(k)
                terms = [(w_hi, y_h), (w_hi, y_l)] + ([(w_lo, y_h)] if k < NK - 1 else [])
                for n, (w, y) in enumerate(terms):
                    last = pe.matmul(acc, w(k), y(k), start=(k == 0 and n == 0), stop=(k == NK - 1 and n == 1))
            return last

        def project(b, c, uses, part=None):
            job = ("P", c)
            if part != 1:
                bank_free(uses, job)
                if c == 0:
                    pe.wait_ge(y_done, b * NK + NK)
            cols = slice(c * P, (c + 1) * P)
            last = split_product(mm[uses.bank(job)][:, :], lambda k: wqk_hi[:, k, cols],
                                 lambda k: wqk_lo[:, k, cols], lambda k: y_hi[:, k, :],
                                 lambda k: y_lo[:, k, :], (range(NK), range(2), range(2, NK))[
                                     0 if part is None else part + 1])
            if part != 0:
                last.then_inc(mm_full, 1)

        def project_v(half, t, uses):
            job = ("V", half, t)
            bank = uses.bank(job)
            bank_free(uses, job)
            cols = slice(half * HALF, (half + 1) * HALF)
            toks = slice(t * P, (t + 1) * P)
            acc = mm[bank][:, 0:HALF]
            n = 0
            for k in range(NK - 1):
                for lhs, rhs in ((y_hi, wv_hi), (y_hi, wv_lo), (y_lo, wv_hi)):
                    pe.matmul(acc, lhs[:, k, toks], rhs[:, k, cols], start=(n == 0), stop=False)
                    n += 1
            pe.matmul(acc, y_hi[:, 4, toks], wv_hi[:, 4, cols], start=False, stop=False)
            pe.matmul(acc, y_lo[:, 4, toks], wv_hi[:, 4, cols], start=False, stop=True).then_inc(mm_full, 1)

        def transpose_y(k, uses):
            job = ("T", k)
            bank = uses.bank(job)
            bank_free(uses, job)
            for t in range(NT):
                last = pe.transpose(mm[bank][:, t * P:(t + 1) * P], xt[:, t, k * P:(k + 1) * P], ident[:, :])
            last.then_inc(mm_full, 1)

        def scores(n, q, tile):
            if not (isinstance(n, int) and n < 2):
                pe.wait_ge(scs_free, n - 1)
            i, t = divmod(tile, NT)
            pe.matmul(scs[:, tile % 2, :], qs[q % 2][0:3 * HD, i, t * P:(t + 1) * P],
                      ks[q % 2][0:3 * HD, i, :], start=True, stop=True).then_inc(scs_full, 1)

        def maxima(q, uses):
            job = ("M", q)
            bank = uses.bank(job)
            bank_free(uses, job)
            for t in range(NT):
                last = pe.matmul(mm[bank][0:HQ, t * P:(t + 1) * P], rowmax[:, t, q * HQ:(q + 1) * HQ],
                                 nident[:, :], start=True, stop=True)
            last.then_inc(mm_full, 1)

        def section(s):
            pe.wait_ge(s_ada[s % 2], 48 * (s // 2 + 1))
            for half in range(2):
                if s >= 1:
                    pe.wait_ge(s_mod_row, 2 * s - 1 + half)
                for k in range(NK):
                    rows = P if k < NK - 1 else TAIL
                    last = pe.matmul(scs[0:B, half, 0:HALF], cond_s[0:rows, k, :],
                                     raw[s % 2][0:rows, k, half * HALF:(half + 1) * HALF],
                                     start=(k == 0), stop=(k == NK - 1))
                last.then_inc(s_mod_full, 1)

        pe.wait_ge(s_cond, 4)
        section(0)
        section(1)
        pro = Uses(0, PROLOGUE)
        pe.wait_ge(s_const, 7)
        pe.wait_ge(xhat_done, NT)
        for k in range(NK):
            transpose_y(k, pro)
        section(2)
        pe.wait_ge(s_w_lo, 4)
        for c in range(3):
            project(0, c, pro)
        section(3)
        pe.wait_ge(s_rawk[3], 48)
        pe.wait_ge(s_small, 80)
        for half in range(2):
            for k in range(NK):
                rows = P if k < NK - 1 else TAIL
                last = pe.matmul(pv[half][0:1, 0:HALF], bv_sb[0:rows, k:k + 1],
                                 raw[3][0:rows, k, half * HALF:(half + 1) * HALF],
                                 start=(k == 0), stop=(k == NK - 1))
            last.then_inc(s_bo_full, 1)
        section(4)
        section(5)
        for c in range(3, NC - 2):
            project(0, c, pro)
        pe.wait_ge(s_w_lo, 6)
        pe.wait_ge(s_mod_row, 12)
        for i, (half, t) in enumerate(V_FIRST):
            project_v(half, t, pro)
            if i == 0:
                pe.wait_ge(stack_in[0][0], 96)
                pe.wait_ge(stack_in[0][1], 96)
            for n in range(SCORES_WITH_V * i, min(SCORES_WITH_V * (i + 1), N_SCORE)):
                scores(n, 0, n)
        pe.wait_ge(scs_free, N_SCORE)
        maxima(0, pro)
        project(0, NC - 2, pro)
        pe.sem_inc(sct_full, 1)
        pe.sem_inc(pv_done, 2)
        pe.wait_ge(s_w_lo, 8)
        pe.wait_ge(s_const, 13)
        pe.wait_ge(v_done, NT + 2)
        pe.wait_ge(p_done, NC - 1)
        pe.wait_ge(s_bo_done, 2)
        pe.wait_ge(neg_done, 1)

        def product(b, unit):
            h, pair = divmod(unit, 2)
            pe.wait_ge(ehi_done, b * UN + unit + 1)
            if pair == 0 and h >= 2:
                pe.wait_ge(o_done, b * (H + 1) + h - 1)
            for part, e in enumerate((e_hi, e_lo)):
                for kk in range(2):
                    if part == 1 and kk == 0:
                        pe.wait_ge(elo_done, b * UN + unit + 1)
                    if part == 1 and kk == 1 and pair == 1:
                        pe.wait_ge(elo_pool, b * H + h + 1)
                    last = pe.matmul(pv[h % 2][0:VW, :], v_sb[:, 2 * pair + kk, h, :],
                                     e[:, unit % 2, kk * T:(kk + 1) * T],
                                     start=(pair == 0 and kk == 0 and part == 0),
                                     stop=(pair == 1 and kk == 1 and part == 1))
            last.then_inc(pv_done, 1)

        def merge_head(b, h):
            pe.wait_ge(pvlo_done, b * H + h + 1)
            for t in range(NT):
                for n, part in enumerate((pv_hi, pv_lo)):
                    last = pe.matmul(pv[h % 2][:, 64 * t:64 * t + MW], part[:, h % 2, t * P:(t + 1) * P],
                                     merge[:, :], start=(n == 0), stop=(n == 1))
            last.then_inc(o_full, 1)

        def transpose_b(b, k):
            bank = T_BANK[k]
            if k == 0:
                pe.wait_ge(sems_b["xhat_done"], b * NT + NT)
            if k >= 2:
                pe.wait_ge(sems_b["ztmp_done"], b * NK + (1, 2, 4)[k - 2])
            elif not (isinstance(b, int) and b == 0):
                pe.wait_ge(sems_b["g_done"], b * NJ + k)
            for t in range(NT):
                last = pe.transpose(mm[bank][:, t * P:(t + 1) * P], xn[:, t, k * P:(k + 1) * P], ident[:, :])
            last.then_inc(sems_b["mm_full"], 1)

        def body(b, has_next):
            uses = body_uses(b, has_next)
            tiles, nq, sn = (), 0, 0
            for unit in range(UN):
                q, u = divmod(unit, 8)
                h = unit // 2
                par = q % 2
                if u == 0:
                    for half in range(2):
                        pe.wait_ge(stack_in[par][half], b * 192 + 96 * (q // 2) + 96)
                    pe.wait_ge(rows_in[par], b * 64 + 32 * (q // 2) + 32)
                if unit == 0:
                    pe.wait_ge(v_done, b * 2 * NT + NT)
                if unit == UN // 2:
                    pe.wait_ge(v_done, b * 2 * NT + 2 * NT)
                pe.wait_ge(sct_free, b * UN + unit + 1)
                for kk in range(2):
                    kt = 2 * (unit % 2) + kk
                    last = pe.matmul(sct[:, kk, :], ks[par][:, h % HQ, kt * P:(kt + 1) * P],
                                     qs[par][:, h % HQ, :], start=True, stop=True)
                last.then_inc(sct_full, 1)
                for tile in tiles[2:]:
                    scores(sn + tile, nq, tile)
                nq = (q + 1) % NQ
                tiles = SCORE_TILES.get(u, ()) if q < 3 or has_next else ()
                sn = (b * NQ + q + 1) * N_SCORE
                if ("M", nq) in JOBS[has_next][unit]:
                    pe.wait_ge(scs_free, sn + N_SCORE)
                    maxima(nq, uses)
                if unit % 2 == 0 and unit >= 4:
                    merge_head(b, unit // 2 - 2)
                nb = b if q < 3 else b + 1
                if u in (0, 3) and tiles:
                    pe.wait_ge(stack_in[nq % 2][u // 3], nb * 192 + 96 * (nq // 2) + 96)
                for tile in tiles[:1]:
                    scores(sn + tile, nq, tile)
                for job in JOBS[has_next][unit]:
                    if job[0] == "P":
                        project(p_batch(uses, job[1]), job[1], uses, 1)
                    elif job[0] == "V":
                        project_v(job[1], job[2], uses)
                    elif job[0] == "T":
                        if job[1] == 0:
                            pe.wait_ge(xhat_done, b * NT + 2 * NT)
                        transpose_y(job[1], uses)
                for job in JOBS[has_next].get(unit + 1, ()):
                    if job[0] == "P":
                        project(p_batch(uses, job[1]), job[1], uses, 0)
                for tile in tiles[1:2]:
                    scores(sn + tile, nq, tile)
                if unit >= 1:
                    product(b, unit - 1)
            if has_next:
                project(b + 1, 7, uses)
            product(b, UN - 1)
            merge_head(b, H - 2)
            if has_next:
                project_v(1, 0, uses)
            else:
                for k in range(NK):
                    transpose_b(0, k)
            merge_head(b, H - 1)

            def transpose_attn(t):
                for n, chunks in enumerate((range(4), (4,))):
                    if t >= 2:
                        pe.wait_ge(at_done, b * 2 * NT + 2 * (t - 2) + n + 1)
                    for m, k in enumerate(chunks):
                        last = pe.transpose(at_psum(t, n)[:, m * P:(m + 1) * P], attn[:, t, k * P:(k + 1) * P],
                                            ident[:, :])
                    last.then_inc(x_full, 1)

            def output(t):
                pe.wait_ge(at_done, b * 2 * NT + 2 * t + 2)
                for half in range(2):
                    job = ("Y", t, half)
                    bank = uses.bank(job)
                    bank_free(uses, job)
                    cols = slice(half * HALF, (half + 1) * HALF)
                    acc = mm[bank][:, 0:HALF]
                    n = 0
                    for k in range(NK - 1):
                        for lhs, rhs in ((at_hi, wo_hi), (at_hi, wo_lo), (at_lo, wo_hi)):
                            pe.matmul(acc, lhs[:, t % 2, k, :], rhs[:, k, cols], start=(n == 0), stop=False)
                            n += 1
                    pe.matmul(acc, at_hi[:, t % 2, 4, :], wo_hi[:, 4, cols], start=False, stop=False)
                    pe.matmul(acc, at_lo[:, t % 2, 4, :], wo_hi[:, 4, cols], start=False, stop=True
                              ).then_inc(mm_full, 1)

            pe.wait_ge(o_done, b * (H + 1) + H + 1)
            transpose_attn(0)
            transpose_attn(1)
            if has_next:
                project_v(1, 1, uses)
            if not has_next:
                pe.wait_ge(sems_b["ztmp_done"], NK)
            for t in range(NT):
                output(t)
                if t + 2 < NT:
                    transpose_attn(t + 2)

        with pe.Fori(0, B - 1) as b:
            body(b, True)
        body(B - 1, False)
        pe.wait_ge(mm_full, len(PROLOGUE) + N_BODY * (B - 1) + len(in_order(JOBS[False])))
        pe.sem_inc(a_over, 1)

        s = sems_b
        def up(b, j):
            bank = (j + 1) % 2
            if j < 2:
                pe.wait_ge(s["ztmp_done"], b * NK + (3, 5)[j])
            else:
                pe.wait_ge(s["g_done"], b * NJ + j)
            cols = slice(j * P, (j + 1) * P)
            split_product(mm[bank][:, :], lambda k: w1_hi[:, k, cols], lambda k: w1_lo[:, k, cols],
                          lambda k: z_hi[:, k, :], lambda k: z_lo[:, k, :],
                          before=(lambda k: pe.wait_ge(s["z_done"], b * NK + k + 1)) if j == 0 else None
                          ).then_inc(s["mm_full"], 1)

        def down(b, j):
            pe.wait_ge(s["h_done"], b * NJ + j + 1)
            if isinstance(b, int) and b == 0 and j % 4 == 0:
                pe.wait_ge(s["w_lo"], 6 + j // 4)
            if j == 0:
                pe.wait_ge(s["yo_done"], b * 2 * NT + 1)
            for t in range(NT):
                toks = slice(t * P, (t + 1) * P)
                pair = y_pair[t // 2][:, YA * (t % 2):YA * (t % 2) + YA]
                for n, (lhs, rhs) in enumerate(((h_hi, 0), (h_hi, 1), (h_lo, 0))):
                    pe.matmul(pair, lhs[:, j % 2, toks], w2_part(j, rhs)[:, 0:YA],
                              start=(j == 0 and n == 0 and t % 2 == 0), stop=(j == NJ - 1 and n == 2),
                              skip_group_check=True)
                    last = pe.matmul(y_own[t][:, 0:YB], lhs[:, j % 2, toks], w2_part(j, rhs)[:, YA:D],
                                     start=(j == 0 and n == 0), stop=(j == NJ - 1 and n == 2))
            return last.then_inc(s["m2_done"], 1)

        def body_b(b, has_next):
            up(b, 0)
            for j in range(1, NJ):
                up(b, j)
                if j < NJ - 1:
                    down(b, j - 1)
            if has_next:
                transpose_b(b + 1, 0)
                transpose_b(b + 1, 1)
            down(b, NJ - 2)
            if has_next:
                transpose_b(b + 1, 2)
                transpose_b(b + 1, 3)
            down(b, NJ - 1)
            if has_next:
                transpose_b(b + 1, 4)

        pe.wait_ge(yb_done, 2 * NT * B + 1)
        pe.wait_ge(s["w_lo"], 5)
        body_b(0, True)
        with pe.Fori(1, B - 1) as b:
            body_b(b, True)
        body_b(B - 1, False)

    block.__exit__(None, None, None)
    slow.__exit__(None, None, None)


def kernel(**inputs):
    import numpy as _np
    import concourse.bacc as _bacc
    from concourse import mybir as _mybir
    from concourse.bass_utils import run_bass_kernel_spmd as _run

    a = {k.removeprefix("L0_cond_"): _np.asarray(v) for k, v in inputs.items()}
    qkv_w, qkv_b = a["qkv_w"], a["qkv_b"]
    wqk = qkv_w[:, :2 * D].reshape(D, 2, NQ, QW).transpose(0, 2, 1, 3).reshape(D, 2 * D)
    bqk = qkv_b[:2 * D].reshape(2, NQ, QW).transpose(1, 0, 2).reshape(NC, P).T
    laid = {
        "x": a["x"], "cond_t": a["cond_1152"].T, "wqk": wqk, "bqk": bqk,
        "wv": qkv_w[:, 2 * D:], "bv": qkv_b[2 * D:], "wo": a["out_w"], "bo": a["out_b"],
        "w1": a["w1"], "b1": a["b1"].reshape(NJ, P).T, "w2": a["w2"], "b2": a["b2"],
        "ada_w": a["ada_w"], "ada_b": a["ada_b"],
    }
    nc = _bacc.Bacc("TRN2", target_bir_lowering=False, num_devices=1, dynamic_dma_scratch_size=2048)
    arrays, args = {}, []
    for name, v in laid.items():
        v = _np.ascontiguousarray(v)
        arrays[f"in_{name}"] = v
        args.append(nc.dram_tensor(f"in_{name}", v.shape, _mybir.dt.from_np(v.dtype), kind="ExternalInput").ap())
    args.append(nc.dram_tensor("out_x", (B, T, D), F32, kind="ExternalOutput").ap())
    conditioned_block(nc, *args)
    r = _run(nc, [arrays], core_ids=[0])
    return r.results[0]["out_x"]
```
